# Optimizing a Trainium2 kernel written in Bass

```python
import numpy as np
import jax
import jax.numpy as jnp

def _softmax(x, axis=-1):
    return jax.nn.softmax(x, axis=axis)

def _gelu(x):
    return jax.nn.gelu(x, approximate=True)

def _silu(x):
    return jax.nn.silu(x)

def _sigmoid(x):
    return jax.nn.sigmoid(x)

def _layernorm(x, axis=-1, eps=1e-05):
    m = jnp.mean(x, axis=axis, keepdims=True)
    v = jnp.var(x, axis=axis, keepdims=True)
    return (x - m) / jnp.sqrt(v + eps)

def _scatter_add(tgt, idx, src, axis=0):
    return tgt.at[idx].add(src)

def _segment_sum(src, seg, n):
    return jax.ops.segment_sum(src, seg, n)
kernel_name = 'mk_gnn_preln_d4_gnn_r8_c444a3'

def setup_inputs(seed: int=0):
    np.random.seed(seed)
    _w = jnp.asarray

    def _rec_inputs():
        import jax
        import jax.numpy as jnp
        _gk = jax.random.key(seed)
        x = -0.000202 + 1 * jax.random.normal(jax.random.fold_in(_gk, 1), (6250, 128), jnp.float32)
        _s = jax.random.randint(jax.random.fold_in(_gk, 2), (100000,), 0, 6250, jnp.int32)
        _d = jax.random.randint(jax.random.fold_in(_gk, 3), (100000,), 0, 6250, jnp.int32)
        _loop = jnp.arange(6250, dtype=jnp.int32)
        src = jnp.concatenate([_s, _d, _loop])
        dst = jnp.concatenate([_d, _s, _loop])
        _o = jnp.argsort(dst, stable=True)
        src = src[_o]
        dst = dst[_o]
        edge_attr_10 = 0.000254407 + 0.99978 * jax.random.normal(jax.random.fold_in(_gk, 12), (206250, 10), jnp.float32)
        edge_attr_32 = 0.000196303 + 1.00016 * jax.random.normal(jax.random.fold_in(_gk, 13), (206250, 32), jnp.float32)
        edge_weight = jax.random.uniform(jax.random.fold_in(_gk, 15), (206250,), jnp.float32, 0.0, 0.999999)
        return (x, src, dst, edge_attr_10, edge_attr_32, edge_weight)
    x, src, dst, edge_attr_10, edge_attr_32, edge_weight = _rec_inputs()

    def _L0_gnn_setup():
        import jax, jax.numpy as jnp
        import numpy as np
        N_NODES = 6250
        N_EDGES = 100000
        IN_DIM = 128
        HID = 128
        EDGE_DIM = 10
        BN_EPS = 1e-05
        key = jax.random.key(seed)
        ks = jax.random.split(key, 12)
        s = 0.05
        return {'x': jax.random.normal(ks[0], (N_NODES, IN_DIM), dtype=jnp.float32), 'edge_index': jax.random.randint(ks[1], (2, N_EDGES), 0, N_NODES, dtype=jnp.int32), 'edge_attr': jax.random.normal(ks[2], (N_EDGES, EDGE_DIM), dtype=jnp.float32), 'Wq': jax.random.normal(ks[3], (HID, IN_DIM), dtype=jnp.float32) * s, 'bq': jnp.zeros((HID,), dtype=jnp.float32), 'Wk': jax.random.normal(ks[4], (HID, IN_DIM), dtype=jnp.float32) * s, 'bk': jnp.zeros((HID,), dtype=jnp.float32), 'Wv': jax.random.normal(ks[5], (HID, IN_DIM), dtype=jnp.float32) * s, 'bv': jnp.zeros((HID,), dtype=jnp.float32), 'We': jax.random.normal(ks[6], (HID, EDGE_DIM), dtype=jnp.float32) * s, 'Wskip': jax.random.normal(ks[7], (HID, IN_DIM), dtype=jnp.float32) * s, 'bskip': jnp.zeros((HID,), dtype=jnp.float32), 'gamma': jnp.ones((HID,), dtype=jnp.float32), 'beta': jnp.zeros((HID,), dtype=jnp.float32)}
    _L0_gnn_all = _L0_gnn_setup()
    _L0_gnn_in = {k: v for k, v in _L0_gnn_all.items() if k in ('Wq', 'bq', 'Wk', 'bk', 'Wv', 'bv', 'We', 'Wskip', 'bskip', 'gamma', 'beta')}
    del _L0_gnn_all

    def _L1_gnn_setup():
        import jax, jax.numpy as jnp
        import numpy as np
        N_NODES = 12500
        N_EDGES = 200000
        D_IN = 128
        D_OUT = 128
        key = jax.random.key(seed)
        k1, k2, k3, k4, k5 = jax.random.split(key, 5)
        feat = jax.random.normal(k1, (N_NODES, D_IN), dtype=jnp.float32)
        W_neigh = jax.random.normal(k2, (D_IN, D_OUT), dtype=jnp.float32) * (1.0 / np.sqrt(D_IN))
        W_self = jax.random.normal(k3, (D_IN, D_OUT), dtype=jnp.float32) * (1.0 / np.sqrt(D_IN))
        b_self = jnp.zeros((D_OUT,), dtype=jnp.float32)
        src = jax.random.randint(k4, (N_EDGES,), 0, N_NODES, dtype=jnp.int32)
        dst = jnp.sort(jax.random.randint(k5, (N_EDGES,), 0, N_NODES, dtype=jnp.int32))
        return {'feat': feat, 'W_neigh': W_neigh, 'W_self': W_self, 'b_self': b_self, 'src': src, 'dst': dst}
    _L1_gnn_all = _L1_gnn_setup()
    _L1_gnn_in = {k: v for k, v in _L1_gnn_all.items() if k in ('W_neigh', 'W_self', 'b_self')}
    del _L1_gnn_all

    def _L2_gnn_setup():
        import jax, jax.numpy as jnp
        import numpy as np
        ORDER = 2
        ALPHA = 0.05

        def spmm_scatter(x, edge_indices, edge_attr):
            src = edge_indices[0]
            dst = edge_indices[1]
            msgs = x[src] * edge_attr[:, None]
            return jax.ops.segment_sum(msgs, dst, num_segments=x.shape[0])
        key = jax.random.key(seed)
        k1, k2, k3, k4 = jax.random.split(key, 4)
        N, E, D, OUT = (12500, 200000, 128, 128)
        x = jax.random.normal(k1, (N, D), dtype=jnp.float32)
        edge_indices = jax.random.randint(k2, (2, E), 0, N, dtype=jnp.int64)
        edge_attr = jax.random.uniform(k3, (E,), dtype=jnp.float32)
        W = jax.random.normal(k4, (D, OUT), dtype=jnp.float32) / np.sqrt(D)
        b = jnp.zeros((OUT,), dtype=jnp.float32)
        return {'x': x, 'edge_indices': edge_indices, 'edge_attr': edge_attr, 'W': W, 'b': b}
    _L2_gnn_all = _L2_gnn_setup()
    _L2_gnn_in = {k: v for k, v in _L2_gnn_all.items() if k in ('W', 'b')}
    del _L2_gnn_all

    def _L3_gnn_setup():
        import jax, jax.numpy as jnp
        import numpy as np
        N, E = (6250, 100000)
        NODE_DIM, EDGE_DIM, HIDDEN_DIM = (128, 32, 128)
        LN_EPS = 1e-05
        key = jax.random.key(seed)
        ks = jax.random.split(key, 10)

        def lin(k, fan_in, fan_out):
            bound = 1.0 / np.sqrt(fan_in)
            kw, kb = jax.random.split(k)
            W = jax.random.uniform(kw, (fan_out, fan_in), jnp.float32, -bound, bound)
            b = jax.random.uniform(kb, (fan_out,), jnp.float32, -bound, bound)
            return (W, b)
        x = jax.random.normal(ks[0], (N, NODE_DIM), jnp.float32)
        edge_index = jax.random.randint(ks[1], (2, E), 0, N, jnp.int64)
        edge_attr = jax.random.normal(ks[2], (E, EDGE_DIM), jnp.float32)
        W1, b1 = lin(ks[3], 2 * NODE_DIM + EDGE_DIM, HIDDEN_DIM)
        W2, b2 = lin(ks[4], HIDDEN_DIM, HIDDEN_DIM)
        Wu, bu = lin(ks[5], HIDDEN_DIM, NODE_DIM)
        gamma = jnp.ones((NODE_DIM,), jnp.float32)
        beta = jnp.zeros((NODE_DIM,), jnp.float32)
        return {'x': x, 'edge_attr': edge_attr, 'W1': W1, 'b1': b1, 'W2': W2, 'b2': b2, 'Wu': Wu, 'bu': bu, 'gamma': gamma, 'beta': beta, 'edge_index': edge_index}
    _L3_gnn_all = _L3_gnn_setup()
    _L3_gnn_in = {k: v for k, v in _L3_gnn_all.items() if k in ('W1', 'b1', 'W2', 'b2', 'Wu', 'bu', 'gamma', 'beta')}
    del _L3_gnn_all
    return {'x': x, 'src': src, 'dst': dst, 'edge_attr_10': edge_attr_10, 'edge_attr_32': edge_attr_32, 'edge_weight': edge_weight, 'L0_gnn_Wq': _L0_gnn_in['Wq'], 'L0_gnn_bq': _L0_gnn_in['bq'], 'L0_gnn_Wk': _L0_gnn_in['Wk'], 'L0_gnn_bk': _L0_gnn_in['bk'], 'L0_gnn_Wv': _L0_gnn_in['Wv'], 'L0_gnn_bv': _L0_gnn_in['bv'], 'L0_gnn_We': _L0_gnn_in['We'], 'L0_gnn_Wskip': _L0_gnn_in['Wskip'], 'L0_gnn_bskip': _L0_gnn_in['bskip'], 'L0_gnn_gamma': _L0_gnn_in['gamma'], 'L0_gnn_beta': _L0_gnn_in['beta'], 'L1_gnn_W_neigh': _L1_gnn_in['W_neigh'], 'L1_gnn_W_self': _L1_gnn_in['W_self'], 'L1_gnn_b_self': _L1_gnn_in['b_self'], 'L2_gnn_W': _L2_gnn_in['W'], 'L2_gnn_b': _L2_gnn_in['b'], 'L3_gnn_W1': _L3_gnn_in['W1'], 'L3_gnn_b1': _L3_gnn_in['b1'], 'L3_gnn_W2': _L3_gnn_in['W2'], 'L3_gnn_b2': _L3_gnn_in['b2'], 'L3_gnn_Wu': _L3_gnn_in['Wu'], 'L3_gnn_bu': _L3_gnn_in['bu'], 'L3_gnn_gamma': _L3_gnn_in['gamma'], 'L3_gnn_beta': _L3_gnn_in['beta']}

def reference(x, src, dst, edge_attr_10, edge_attr_32, edge_weight, L0_gnn_Wq, L0_gnn_bq, L0_gnn_Wk, L0_gnn_bk, L0_gnn_Wv, L0_gnn_bv, L0_gnn_We, L0_gnn_Wskip, L0_gnn_bskip, L0_gnn_gamma, L0_gnn_beta, L1_gnn_W_neigh, L1_gnn_W_self, L1_gnn_b_self, L2_gnn_W, L2_gnn_b, L3_gnn_W1, L3_gnn_b1, L3_gnn_W2, L3_gnn_b2, L3_gnn_Wu, L3_gnn_bu, L3_gnn_gamma, L3_gnn_beta):
    import jax
    import jax.numpy as jnp

    def _L0_gnn_ref(x, edge_index, edge_attr, Wq, bq, Wk, bk, Wv, bv, We, Wskip, bskip, gamma, beta):
        import jax, jax.numpy as jnp
        import numpy as np
        N_NODES = 6250
        N_EDGES = 100000
        IN_DIM = 128
        HID = 128
        EDGE_DIM = 10
        BN_EPS = 1e-05
        N = x.shape[0]
        d = Wq.shape[0]
        src, dst = (edge_index[0], edge_index[1])
        q_all = x @ Wq.T + bq
        k_all = x @ Wk.T + bk
        v_all = x @ Wv.T + bv
        e = edge_attr @ We.T
        q = q_all[dst]
        k = k_all[src] + e
        v = v_all[src] + e
        scale = 1.0 / jnp.sqrt(jnp.asarray(d, dtype=x.dtype))
        alpha = (q * k).sum(-1) * scale
        amax = jax.ops.segment_max(alpha, dst, num_segments=N)
        ex = jnp.exp(alpha - amax[dst])
        denom = jax.ops.segment_sum(ex, dst, num_segments=N)
        w = ex / denom[dst]
        agg = jax.ops.segment_sum(v * w[:, None], dst, num_segments=N)
        out = agg + x @ Wskip.T + bskip
        h = jax.nn.relu(out)
        mean = h.mean(0)
        var = ((h - mean) ** 2).mean(0)
        return gamma * (h - mean) * jax.lax.rsqrt(var + BN_EPS) + beta

    def _L1_gnn_ref(feat, W_neigh, W_self, b_self, src, dst):
        import jax, jax.numpy as jnp
        import numpy as np
        N_NODES = 12500
        N_EDGES = 200000
        D_IN = 128
        D_OUT = 128
        "SAGE 'mean' aggregation: h = fc_self(feat) + fc_neigh(mean_{u in N(v)} feat_u).\n            in_feats == out_feats -> lin_before_mp is False: aggregate raw features first.\n            In-degrees are clamped to min 1.0 as in set_graph_data."
        n = feat.shape[0]
        deg = jax.ops.segment_sum(jnp.ones_like(dst, dtype=feat.dtype), dst, num_segments=n)
        deg = jnp.maximum(deg, 1.0)
        agg = jax.ops.segment_sum(feat[src], dst, num_segments=n)
        h_neigh = agg / deg[:, None] @ W_neigh
        h_self = feat @ W_self + b_self
        return h_self + h_neigh

    def _L2_gnn_ref(x, edge_indices, edge_attr, W, b):
        import jax, jax.numpy as jnp
        import numpy as np
        ORDER = 2
        ALPHA = 0.05

        def spmm_scatter(x, edge_indices, edge_attr):
            src = edge_indices[0]
            dst = edge_indices[1]
            msgs = x[src] * edge_attr[:, None]
            return jax.ops.segment_sum(msgs, dst, num_segments=x.shape[0])
        orig_feature = x
        features = (1.0 - ALPHA) * spmm_scatter(x, edge_indices, edge_attr)
        sum_feature = x
        for _ in range(ORDER):
            sum_feature = sum_feature + features
        feature = sum_feature / ORDER + ALPHA * orig_feature
        out = feature @ W + b
        return out

    def _L3_gnn_ref(x, edge_attr, W1, b1, W2, b2, Wu, bu, gamma, beta, edge_index):
        import jax, jax.numpy as jnp
        import numpy as np
        N, E = (6250, 100000)
        NODE_DIM, EDGE_DIM, HIDDEN_DIM = (128, 32, 128)
        LN_EPS = 1e-05
        src, dst = (edge_index[0], edge_index[1])
        msg_input = jnp.concatenate([x[src], x[dst], edge_attr], axis=-1)
        h = jax.nn.relu(msg_input @ W1.T + b1)
        messages = h @ W2.T + b2
        agg = jax.ops.segment_sum(messages, dst, num_segments=x.shape[0])
        upd = jax.nn.relu(agg @ Wu.T + bu)
        y = x + upd
        mean = jnp.mean(y, axis=-1, keepdims=True)
        var = jnp.mean(jnp.square(y - mean), axis=-1, keepdims=True)
        return (y - mean) * jax.lax.rsqrt(var + LN_EPS) * gamma + beta
    edge_index = jnp.stack([src, dst])
    h = jnp.maximum(_layernorm(x, axis=-1), 0.0)
    x = x + _L0_gnn_ref(h, edge_index, edge_attr_10, L0_gnn_Wq, L0_gnn_bq, L0_gnn_Wk, L0_gnn_bk, L0_gnn_Wv, L0_gnn_bv, L0_gnn_We, L0_gnn_Wskip, L0_gnn_bskip, L0_gnn_gamma, L0_gnn_beta)
    h = jnp.maximum(_layernorm(x, axis=-1), 0.0)
    x = x + _L1_gnn_ref(h, L1_gnn_W_neigh, L1_gnn_W_self, L1_gnn_b_self, src, dst)
    h = jnp.maximum(_layernorm(x, axis=-1), 0.0)
    x = x + _L2_gnn_ref(h, edge_index, edge_weight, L2_gnn_W, L2_gnn_b)
    h = jnp.maximum(_layernorm(x, axis=-1), 0.0)
    x = x + _L3_gnn_ref(h, edge_attr_32, L3_gnn_W1, L3_gnn_b1, L3_gnn_W2, L3_gnn_b2, L3_gnn_Wu, L3_gnn_bu, L3_gnn_gamma, L3_gnn_beta, edge_index)
    return x

_drawn_inputs = setup_inputs


def setup_inputs(seed=0):
    import zlib

    import numpy as np

    out = dict(_drawn_inputs(seed))
    spreads = {'L0_gnn_bq': (0.0, 0.8),
     'L0_gnn_bk': (0.0, 2.0),
     'L0_gnn_bv': (0.0, 0.1),
     'L0_gnn_bskip': (0.0, 0.1),
     'L0_gnn_gamma': (1.0, 0.2),
     'L0_gnn_beta': (0.0, 0.1),
     'L1_gnn_b_self': (0.0, 0.1),
     'L2_gnn_b': (0.0, 0.581),
     'L3_gnn_gamma': (1.0, 0.58),
     'L3_gnn_beta': (0.0, 0.68)}
    factors = {'edge_attr_32': 4.509,
     'L0_gnn_Wq': 4.381,
     'L0_gnn_Wk': 4.76,
     'L3_gnn_b1': 3.769,
     'L3_gnn_bu': 21.806}
    for name, (base, spread) in spreads.items():
        noise = np.random.default_rng([zlib.crc32(name.encode()), seed]).standard_normal(out[name].shape)
        drawn = base * np.exp(spread * noise) if base else spread * noise
        out[name] = jnp.asarray(drawn.astype(out[name].dtype))
    for name, factor in factors.items():
        out[name] = (out[name] * factor).astype(out[name].dtype)
    return out
```

```python
import concourse.bass as bass
from concourse import mybir
from contextlib import ExitStack, contextmanager

fp32 = mybir.dt.float32
i32 = mybir.dt.int32
ALU = mybir.AluOpType
ACT = mybir.ActivationFunctionType
AX = mybir.AxisListType

N, F, E = 6250, 128, 206250
E0, E3 = 10, 32
P = 128
TB = 4
PIECE = 7
BODY = 2 * PIECE
IT = 29
NB = IT * BODY
NT = NB * TB
ST = PIECE * TB
assert NT * P >= E
NPT, NTL = 125, 50
assert NPT * NTL == N
PAIRS = NTL // 2
NCOL = 6400
EPS = 1e-5
BIG = 1e30
ALPHA = 0.05
LAYERS = 4
FEW = (4, 32)
ANY = (1, 128)
STORED = (1, 2, 3, 6)
LOADS = 25
PAD_DST = 2 * N



class Tally:

    def __init__(self):
        self.n, self.i, self.per = 0, 0, 0

    def up(self):
        self.n += 1
        return self.i * self.per + self.n

    @contextmanager
    def loop(self, i, runs, per):
        start = self.n
        self.i, self.per = i, per
        yield
        assert self.n - start == per, (self.n - start, per)
        self.i, self.per, self.n = 0, 0, start + runs * per


def program(nc, d, out):
    SCALE = float(F) ** -0.5
    ctx = ExitStack()
    with ctx:
        def sb(name, shape, dt=fp32):
            return ctx.enter_context(nc.sbuf_tensor(name, shape, dt))

        def sem(name):
            return ctx.enter_context(nc.semaphore(name))

        h_table = nc.dram_tensor("h_table", (N, F), fp32).ap()
        b_table = nc.dram_tensor("b_table", (N + P, F), fp32).ap()

        R = sb("R", [P, NCOL])
        U = sb("U", [P, NCOL])
        A = sb("A", [P, NCOL])
        C = sb("C", [P, NCOL])
        D = sb("D", [E0 + 1, NCOL])

        def rows(buf):
            return buf[0:NPT, :].rearrange("p (t f) -> p t f", f=F)

        ring = sb("ring", [P, BODY, TB, F])
        idx = sb("idx", [P, 2, ST], i32)
        dloc = sb("dloc", [P, NT + TB])
        base_i = sb("base_i", [1, NT], i32)
        flag = sb("flag", [1, 1], i32)
        S_ = sb("S", [P, 2 * TB * P])
        S2_ = sb("S2", [P, 2 * TB * P])
        eaT = sb("eaT", [E3, 2, TB * P])
        hT = sb("hT", [P, 2, TB * P])
        ea_rows = sb("ea_rows", [P, 2, ST, E0 + 1])
        dst_r = sb("dst_r", [ST, 2, P], i32)
        sd = sb("sd", [ST, P])
        step = sb("step", [ST, P + 1])
        run_f = sb("run_f", [ST, P])
        run_b = sb("run_b", [ST, P])
        at_first = sb("at_first", [ST, P])
        at_last = sb("at_last", [ST, P])
        al_t = sb("al_t", [ST, P])
        alpha = sb("alpha", [P, ST])
        ex = sb("ex", [P, 2, ST])
        edge_r = sb("edge_r", [1, 2, 2 * ST + 1], i32)
        row = sb("row", [1, 8, ST + 1])
        tail = sb("tail", [1, 1])
        cin = sb("cin", [ST, 2])
        fac = sb("fac", [P, 1])
        facr = sb("facr", [1, 1])
        iota = sb("iota", [P, P])
        ident = sb("ident", [P, P])
        ones = sb("ones", [P, P])
        WK, WN, WS, W2L = (sb(n, [P, P]) for n in ("wk", "w_neigh", "w_self", "w_two"))
        WqT, WvT, WskT, W2T, WuT = (sb(n, [P, P]) for n in ("wqT", "wvT", "wskT", "w2T", "wuT"))
        W1abT = sb("w1abT", [P, 2 * P])
        W1cT = sb("w1cT", [E3, P])
        bk_we = sb("bk_we", [P, E0 + 1])
        bv_we = sb("bv_we", [P, E0 + 1])
        bv_weT = sb("bv_weT", [E0 + 1, P + 1])
        bq_c = sb("bq_c", [P, 1])
        g0, be0 = (sb(n, [P, P]) for n in ("g0", "be0"))
        g3, be3 = (ring[:, k, 0, :] for k in range(2))
        bskip, bself, btwo, b1, b2, bu = (sb(n, [1, P]) for n in ("bskip", "bself", "btwo", "b1", "b2", "bu"))
        stat = sb("stat", [P, 4, NTL])
        st1 = sb("st1", [P, 2, P])
        st2 = sb("st2", [P, 2, P])
        st3 = sb("st3", [E0 + 1, 2 * NPT])
        st4 = sb("st4", [P, 2 * NPT])
        rc = sb("rc", [P, 2])
        mean_bc, scale_bc, tmp_bc = (ring[:, k, 0, :] for k in range(3))

        bank = [ctx.enter_context(nc.psum_tensor(f"bank{k}", [P, 512], fp32)) for k in range(8)]

        raw = {n: ring[:, k, 0, :] for k, n in enumerate(("q", "v", "skip", "w2", "wu"))}
        raw_w1 = ring[:, 6, 0:3, :].rearrange("p a f -> p (a f)")[:, 0:2 * F + E3]
        dst_i = C[:, 0:NT].bitcast(i32)
        base_f = U[0:1, 0:NT]
        last_i = A[0:1, 0:NT].bitcast(i32)
        reach = A[0:1, NT:NT + NB]

        s_junk = {e: sem("passed_" + e) for e in ("pool", "act", "pe", "dve", "loads")}
        loaded, consts, x_loaded, wT_ps, wT_sb, bases_done, base_ps = (
            sem(n) for n in ("loaded", "consts", "x_loaded", "wT_ps", "wT_sb", "bases_done", "base_ps"))
        ch = sem("dve_chain")
        flag_ready = sem("flag_ready")
        h_ready, h_stored, var_ready, sd_ready, prepared = (
            sem(n) for n in ("h_ready", "h_stored", "var_ready", "sd_ready", "prepared"))
        node = {(l, w): {n: sem(f"{('prep', 'finish')[w]}{l}_{n}") for n in names} for (l, w), names in {
            (0, 0): ("st", "T", "hT", "q", "qs", "y", "yout"), (0, 1): ("st", "y", "qs", "yout"),
            (1, 0): ("st", "T", "hT"), (1, 1): ("st", "y", "q", "qs", "yout"),
            (2, 0): ("st", "T", "hT"), (2, 1): ("q", "st", "y", "yout"),
            (3, 0): ("st", "T", "hT", "q", "qs"), (3, 1): ("st", "q", "qs", "y", "yout")}.items()}
        bn_sum, bn_x, y_done, stored, wt_in, w1c_in = (sem(n) for n in ("bn_sum", "bn_x", "y_done", "stored", "wt_in", "w1c_in"))
        idx_ready = [sem(f"idx_ready{p}") for p in range(2)]
        gathered = [sem(f"gathered{b}") for b in range(BODY)]
        ea_in = [sem(f"ea_in{k}") for k in range(2)]
        bw_in = [sem(f"bw_in{k}") for k in range(2)]
        sg_in = [sem(f"sg_in{k}") for k in range(2)]
        mm = [sem(f"mm{l}") for l in range(4)]
        onehot = [sem(f"onehot{l}") for l in range(4)]
        added = [sem(f"added{l}") for l in range(4)]
        hT_ps, hT_sb, score, scored, ex_ready, sT_ps, sT_sb, pre, summed, relu = (
            sem(n) for n in ("hT_ps", "hT_sb", "score", "scored", "ex_ready", "sT_ps", "sT_sb", "pre", "summed", "relu"))
        g3_in = sem("g3_in")
        s_id = sem("ident_zero")
        sxa, sxb = sem("softmax_pe"), sem("softmax_dve")
        mm2, onehot2 = mm[0], onehot[0]

        block = ctx.enter_context(nc.Block())

        def after(r):
            return r + BODY

        def when(sem_, value, eng, name):
            eng.wait_ge(sem_, value)
            eng.sem_inc(s_junk[name], 1)

        def matrices(buf, W):
            return buf[:, 0:2 * TB * W].rearrange("p (k j w) -> p k j w", k=2, j=TB)

        def window_bases(eng, n, G):
            eng.sem_inc(s_junk["loads"], 1)
            return [eng.value_load(base_i[0:1, bass.ds(n * TB + g, 1)], min_val=0, max_val=N - 1) for g in range(0, TB, G)]

        def by_mode(eng, run):
            eng.wait_ge(flag_ready, 1)
            few = eng.value_load(flag[0:1, 0:1], min_val=0, max_val=1)
            with eng.If(few):
                run(*FEW)
            with eng.Else():
                run(*ANY)

        def steps(eng, one):
            one(0, 0, True, False)
            with eng.Fori(0, IT - 1) as i:
                for c in range(1, BODY + 1):
                    one(i, c, True, True)
            for c in range(1, BODY):
                one(IT - 1, c, True, True)
            one(IT - 1, BODY, False, True)

        def supersteps(eng, one):
            one(0, 0, True, False)
            with eng.Fori(0, IT - 1) as i:
                one(i, 1, True, True)
                one(i, 2, True, True)
            one(IT - 1, 1, True, True)
            one(IT - 1, 2, False, True)

        @block.vector
        def _(eng):
            v = nc.vector
            t = Tally()
            for x in onehot + added + [scored, summed]:
                eng.sem_inc(x, BODY)
            eng.wait_ge(loaded, LOADS * 16)
            eng.wait_ge(consts, 3)
            v.tensor_scalar(base_f, dst_i[0:1, :], float(N - 1), None, ALU.min)
            v.tensor_scalar(reach, last_i[0:1, TB - 1:NT:TB], float(N - 1), None, ALU.min).then_inc(ch, 1)
            eng.wait_ge(ch, t.up())
            v.tensor_copy(base_i[:, :], base_f).then_inc(bases_done, 1)
            v.tensor_tensor(reach, reach, base_f[0:1, 0:NT:TB], ALU.subtract).then_inc(ch, 1)
            eng.wait_ge(ch, t.up())
            v.tensor_reduce(tail[:, :], reach, AX.X, ALU.max).then_inc(ch, 1)
            eng.wait_ge(ch, t.up())
            v.tensor_scalar(flag[:, :], tail[:, :], float(FEW[1]), None, ALU.is_lt).then_inc(flag_ready, 1)
            v.memset(dloc[:, NT:NT + TB], -1.0)
            v.memset(bv_weT[:, P:P + 1], 0.0).then_inc(ch, 1)
            eng.wait_ge(ch, t.up())
            v.memset(bv_weT[0:1, P:P + 1], 1.0)
            eng.wait_ge(wT_ps, 1)
            for k, w in enumerate((WqT, WvT, WskT, W2T)):
                v.tensor_copy(w[:, :], bank[0][:, k * P:(k + 1) * P])
            v.tensor_copy(WuT[:, :], bank[1][:, 0:P])
            v.tensor_copy(W1abT[:, :], bank[1][:, P:3 * P])
            v.tensor_copy(bv_weT[:, 0:P], bank[2][0:E0 + 1, 0:P])
            v.tensor_copy(W1cT[:, :], bank[2][0:E3, P:2 * P]).then_inc(wT_sb, 1)

            links = t.n

            def run(G, W):
                NW = TB // G
                S, S2 = matrices(S_, W), matrices(S2_, W)
                t.n = links
                for k in range(NW):
                    eng.wait_ge(base_ps, k + 1)
                    tiles = slice(k * NB * G, (k + 1) * NB * G)
                    v.tensor_tensor(dloc[:, tiles].rearrange("p (w g) -> p w g", g=G),
                                    dst_i[:, tiles].rearrange("p (w g) -> p w g", g=G),
                                    bank[4 + k][:, 0:NB].unsqueeze(2).to_broadcast([P, NB, G]), ALU.subtract).then_inc(ch, 1)
                    eng.wait_ge(ch, t.up())

                def layernorm(x, h, sq, l):
                    v.tensor_reduce(stat[0:NPT, 0, :], x, AX.X, ALU.add).then_inc(ch, 1)
                    eng.wait_ge(ch, t.up())
                    v.tensor_scalar(stat[0:NPT, 1, :], stat[0:NPT, 0, :], 1.0 / F, None, ALU.mult).then_inc(ch, 1)
                    eng.wait_ge(ch, t.up())
                    v.tensor_tensor(h, x, stat[0:NPT, 1, :].unsqueeze(2).to_broadcast([NPT, NTL, F]), ALU.subtract).then_inc(ch, 1)
                    eng.wait_ge(ch, t.up())
                    v.tensor_tensor(sq, h, h, ALU.mult).then_inc(ch, 1)
                    eng.wait_ge(ch, t.up())
                    v.tensor_reduce(stat[0:NPT, 0, :], sq, AX.X, ALU.add).then_inc(ch, 1)
                    eng.wait_ge(ch, t.up())
                    v.tensor_scalar(stat[0:NPT, 1, :], stat[0:NPT, 0, :], 1.0 / F, EPS, ALU.mult, ALU.add).then_inc(var_ready, 1)
                    eng.wait_ge(sd_ready, l + 1)
                    v.reciprocal(stat[0:NPT, 3, :], stat[0:NPT, 2, :]).then_inc(ch, 1)
                    eng.wait_ge(ch, t.up())
                    return stat[0:NPT, 3, :].unsqueeze(2).to_broadcast([NPT, NTL, F])

                def head(l, k):
                    hb = rows(U if l == 3 else A)
                    rstd = layernorm(rows(R), hb, rows(C), k)
                    v.scalar_tensor_tensor(out=hb, in0=hb, scalar=0.0, in1=rstd, op0=ALU.max, op1=ALU.mult).then_inc(h_ready, 1)
                    eng.wait_ge(h_ready, l + 1)

                def prep(l):
                    m = node[l, 0]
                    hb = U if l == 3 else A
                    def one(i):
                        v.tensor_scalar(st1[0:NPT, :, :].rearrange("p k f -> p (k f)"),
                                        hb[0:NPT, bass.ds(i * 2 * F, 2 * F)], 1.0, None, ALU.mult).then_inc(m["st"], 1)
                        eng.wait_ge(m["T"], i + 1)
                        if l in (1, 2):
                            v.tensor_scalar(U[:, bass.ds(i * 2 * NPT, 2 * NPT)], bank[0][:, 0:2 * NPT], 1.0, None, ALU.mult).then_inc(m["hT"], 1)
                            return
                        v.tensor_copy(st4[:, :], bank[0][:, 0:2 * NPT]).then_inc(m["hT"], 1)
                        eng.wait_ge(m["q"], i + 1)
                        if l == 3:
                            for k in range(2):
                                v.tensor_scalar(A[0:NPT, bass.ds(i * 2 * F + k * F, F)], bank[1 + k][0:NPT, 0:F], 1.0, None, ALU.mult)
                                last = v.tensor_scalar(C[0:NPT, bass.ds(i * 2 * F + k * F, F)], bank[1 + k][0:NPT, F:2 * F], 1.0, None, ALU.mult)
                            last.then_inc(m["qs"], 1)
                            return
                        v.tensor_scalar(st2[:, :, :].rearrange("p k f -> p (k f)")[:, 0:2 * NPT], bank[1][:, 0:2 * NPT],
                                        bq_c[:, 0:1], None, ALU.add).then_inc(m["qs"], 1)
                        v.tensor_scalar(R[0:NPT, bass.ds(i * 2 * F, 2 * F)], bank[2][0:NPT, 0:2 * F], 1.0, None, ALU.mult)
                        eng.wait_ge(m["y"], i + 1)
                        v.tensor_scalar(U[:, bass.ds(i * 2 * NPT, 2 * NPT)], bank[3][:, 0:2 * NPT], SCALE, None, ALU.mult)
                        v.tensor_scalar(D[:, bass.ds(i * 2 * NPT, 2 * NPT)], bank[3][0:E0 + 1, 256:256 + 2 * NPT], SCALE, None, ALU.mult).then_inc(m["yout"], 1)
                    with eng.Fori(0, PAIRS) as i:
                        one(i)

                def one_hot(to, n):
                    return v.tensor_tensor(to, iota[:, 0:W].unsqueeze(1).to_broadcast([P, TB, W]),
                                           dloc[:, bass.ds(n * TB, TB)].unsqueeze(2).to_broadcast([P, TB, W]), ALU.is_equal)

                def clear(l):
                    eng.wait_ge(h_stored, STORED[l] * 16)
                    v.memset(A[:, :], 0.0).then_inc(ch, 1)
                    eng.wait_ge(ch, t.up())
                    if l == 0:
                        v.memset(C[0:E0 + 1, :], 0.0)
                        v.memset(U[:, N:NCOL], 0.0)
                        v.memset(D[:, N:NCOL], 0.0).then_inc(prepared, 1)
                    elif l == 1:
                        v.memset(D[0:1, :], 0.0).then_inc(prepared, 1)
                    else:
                        v.memset(tail[:, :], 0.0).then_inc(prepared, 1)
                    eng.wait_ge(prepared, l + 1)

                eng.wait_ge(x_loaded, 16)
                head(0, 0)
                prep(0)
                clear(0)
                v.memset(tail[:, :], -BIG)
                v.memset(row[:, :, :], 0.0)
                v.memset(step[:, :], 0.0).then_inc(ch, 1)
                eng.wait_ge(ch, t.up())
                v.memset(row[0:1, 5, ST:ST + 1], -BIG).then_inc(ch, 1)
                eng.wait_ge(ch, t.up())

                def scores(i, c):
                    n = i * BODY + c
                    one_hot(S2[:, 0], n).then_inc(ch, 1)
                    eng.wait_ge(ch, t.up())
                    eng.wait_ge(score, after(n + 1))
                    v.tensor_tensor(S2[:, 1], S2[:, 0], bank[2 + c % 2][:, 0:TB * W].rearrange("p (j w) -> p j w", w=W), ALU.mult).then_inc(ch, 1)
                    eng.wait_ge(ch, t.up())
                    b = c % PIECE
                    v.tensor_reduce(alpha[:, b * TB:(b + 1) * TB], S2[:, 1], AX.X, ALU.add).then_inc(scored, 1)
                    eng.wait_ge(scored, after(n + 1))

                def weigh(i, c, p):
                    n = i * BODY + c
                    eng.wait_ge(mm2, after(n - 1))
                    one_hot(S[:, c % 2], n).then_inc(ch, 1)
                    eng.wait_ge(ch, t.up())
                    b = c % PIECE
                    v.tensor_tensor(S[:, c % 2], S[:, c % 2], ex[:, p, b * TB:(b + 1) * TB].unsqueeze(2).to_broadcast([P, TB, W]),
                                    ALU.mult).then_inc(onehot2, 1)

                def accumulate(l, i, c, done, acc2, part2):
                    n = i * BODY + c
                    regs = window_bases(eng, n, G)
                    eng.wait_ge(done, after(n + 1))
                    for w in range(NW):
                        at = bass.ds(regs[w], W)
                        if acc2 is not None:
                            v.tensor_tensor(acc2[0:part2, at], acc2[0:part2, at], bank[6 + c % 2][0:part2, w * W:(w + 1) * W], ALU.add)
                        v.tensor_tensor(A[:, at], A[:, at], bank[4 + c % 2][:, w * W:(w + 1) * W], ALU.add).then_inc(added[l], 1)
                        eng.wait_ge(added[l], after(NW * n + w + 1))

                def softmax(i, q):
                    p = q % 2
                    eng.wait_ge(sg_in[p], 64 * (i + q // 2 + 1))
                    v.tensor_scalar(sd[:, :], dst_r[:, p, :], BIG, None, ALU.mult)
                    v.tensor_scalar(row[0:1, 0, :], edge_r[0:1, p, 0:ST + 1], BIG, None, ALU.mult)
                    v.tensor_scalar(row[0:1, 1, 0:ST], edge_r[0:1, p, ST + 1:2 * ST + 1], BIG, None, ALU.mult).then_inc(ch, 1)
                    eng.wait_ge(ch, t.up())
                    v.tensor_tensor(step[:, 1:P], sd[:, 0:P - 1], sd[:, 1:P], ALU.subtract)
                    v.tensor_scalar(at_first[:, :], sd[:, :], sd[:, 0:1], -1.0, ALU.subtract, ALU.mult)
                    v.tensor_scalar(at_last[:, :], sd[:, :], sd[:, P - 1:P], None, ALU.subtract)
                    v.tensor_tensor(row[0:1, 2, 0:ST], row[0:1, 0, 0:ST], row[0:1, 1, 0:ST], ALU.subtract)
                    v.tensor_tensor(row[0:1, 3, 0:ST], row[0:1, 1, 0:ST], row[0:1, 0, 1:ST + 1], ALU.subtract).then_inc(ch, 1)
                    eng.wait_ge(ch, t.up())
                    v.tensor_tensor(row[0:1, 0, 0:ST], row[0:1, 2, 0:ST], row[0:1, 3, 0:ST], ALU.add)
                    v.tensor_tensor(row[0:1, 1, 0:ST], row[0:1, 2, 1:ST + 1], row[0:1, 3, 0:ST], ALU.add)
                    v.tensor_copy(row[0:1, 4, 0:1], tail[:, :])
                    eng.wait_ge(sxa, 4 * (2 * i + q) + 1)
                    v.tensor_copy(al_t[:, :], bank[2][0:ST, 0:P]).then_inc(ch, 1)
                    eng.wait_ge(ch, t.up())
                    v.tensor_tensor_scan(out=run_f[:, :], data0=step[:, 0:P], data1=al_t[:, :], initial=-BIG, op0=ALU.add, op1=ALU.max)
                    v.tensor_tensor_scan(out=run_b[:, ::-1], data0=step[:, 1:P + 1][:, ::-1], data1=al_t[:, ::-1], initial=-BIG,
                                         op0=ALU.add, op1=ALU.max).then_inc(sxb, 1)
                    eng.wait_ge(sxa, 4 * (2 * i + q) + 2)
                    v.tensor_tensor_scan(out=row[0:1, 4, 1:ST + 1], data0=row[0:1, 0, 0:ST], data1=bank[2][0:1, 128:128 + ST],
                                         initial=tail[:, :], op0=ALU.add, op1=ALU.max)
                    v.tensor_tensor_scan(out=row[0:1, 5, 0:ST][:, ::-1], data0=row[0:1, 1, 0:ST][:, ::-1],
                                         data1=bank[2][0:1, 192:192 + ST][:, ::-1], initial=-BIG, op0=ALU.add, op1=ALU.max).then_inc(ch, 1)
                    eng.wait_ge(ch, t.up())
                    v.tensor_tensor(row[0:1, 6, 0:ST], row[0:1, 4, 0:ST], row[0:1, 2, 0:ST], ALU.add)
                    v.tensor_tensor(row[0:1, 7, 0:ST], row[0:1, 5, 1:ST + 1], row[0:1, 2, 1:ST + 1], ALU.add)
                    v.tensor_copy(tail[:, :], row[0:1, 4, ST:ST + 1]).then_inc(sxb, 1)
                    eng.wait_ge(sxa, 4 * (2 * i + q) + 3)
                    v.tensor_copy(cin[:, :], bank[3][0:ST, 0:2]).then_inc(ch, 1)
                    eng.wait_ge(ch, t.up())
                    v.scalar_tensor_tensor(out=run_f[:, :], in0=at_first[:, :], scalar=cin[:, 0:1], in1=run_f[:, :], op0=ALU.add, op1=ALU.max)
                    v.scalar_tensor_tensor(out=run_b[:, :], in0=at_last[:, :], scalar=cin[:, 1:2], in1=run_b[:, :], op0=ALU.add, op1=ALU.max).then_inc(ch, 1)
                    eng.wait_ge(ch, t.up())
                    v.tensor_tensor(run_f[:, :], run_f[:, :], run_b[:, :], ALU.max).then_inc(ch, 1)
                    eng.wait_ge(ch, t.up())
                    v.tensor_tensor(al_t[:, :], al_t[:, :], run_f[:, :], ALU.subtract)
                    v.tensor_tensor(facr[:, :], row[0:1, 6, 0:1], run_f[0:1, 0:1], ALU.subtract).then_inc(sxb, 1)

                def rescale(i, c, q):
                    reg = window_bases(eng, i * BODY + c, TB)[0]
                    eng.wait_ge(ex_ready, after(2 * i + q))
                    v.tensor_scalar(C[0:E0 + 1, bass.ds(reg, 1)], C[0:E0 + 1, bass.ds(reg, 1)], fac[0:E0 + 1, 0:1], None, ALU.mult)
                    v.tensor_scalar(A[:, bass.ds(reg, 1)], A[:, bass.ds(reg, 1)], fac[:, 0:1], None, ALU.mult).then_inc(ch, 1)
                    eng.wait_ge(ch, t.up())

                def layer0(i, q, a, b):
                    if b:
                        rescale(i, q * PIECE - PIECE, q)
                    for k in range(PIECE):
                        if b:
                            weigh(i, (q - 1) * PIECE + k, (q - 1) % 2)
                        if a:
                            scores(i, q * PIECE + k)
                        if b:
                            accumulate(0, i, (q - 1) * PIECE + k, mm2, C, E0 + 1)
                    if a:
                        softmax(i, q)

                layer0(0, 0, True, False)
                with eng.Fori(0, IT - 1) as i:
                    with t.loop(i, IT - 1, 2 * (1 + PIECE * 3 + 7)):
                        layer0(i, 1, True, True)
                        layer0(i, 2, True, True)
                layer0(IT - 1, 1, True, True)
                layer0(IT - 1, 2, False, True)

                m = node[0, 1]
                with eng.Fori(0, PAIRS) as i:
                    v.tensor_scalar(st4[:, :], A[:, bass.ds(i * 2 * NPT, 2 * NPT)], 1.0, None, ALU.mult)
                    v.tensor_scalar(st3[:, :], C[0:E0 + 1, bass.ds(i * 2 * NPT, 2 * NPT)], 1.0, None, ALU.mult).then_inc(m["st"], 1)
                    eng.wait_ge(m["y"], i + 1)
                    for k in range(2):
                        last = v.reciprocal(rc[0:NPT, k:k + 1], bank[k][0:NPT, F:F + 1])
                    last.then_inc(m["qs"], 1)
                    eng.wait_ge(m["qs"], i + 1)
                    for k in range(2):
                        at = bass.ds(i * 2 * F + k * F, F)
                        last = v.scalar_tensor_tensor(out=R[0:NPT, at], in0=bank[k][0:NPT, 0:F], scalar=rc[0:NPT, k:k + 1], in1=R[0:NPT, at],
                                                      op0=ALU.mult, op1=ALU.add)
                    last.then_inc(m["yout"], 1)
                eng.wait_ge(m["yout"], PAIRS)

                v.tensor_scalar(rows(R), rows(R), 0.0, None, ALU.max).then_inc(bn_x, 1)
                eng.wait_ge(bn_sum, 1)
                v.tensor_reduce(tmp_bc[:, :], bank[2][:, :].rearrange("p (j f) -> p f j", f=F), AX.X, ALU.add).then_inc(ch, 1)
                eng.wait_ge(ch, t.up())
                v.tensor_scalar(mean_bc[:, :], tmp_bc[:, :], 1.0 / N, None, ALU.mult).then_inc(ch, 1)
                eng.wait_ge(ch, t.up())
                v.tensor_tensor(rows(A), rows(R), mean_bc[0:NPT, :].unsqueeze(1).to_broadcast([NPT, NTL, F]), ALU.subtract).then_inc(ch, 1)
                eng.wait_ge(ch, t.up())
                v.tensor_tensor(rows(C), rows(A), rows(A), ALU.mult).then_inc(bn_x, 1)
                eng.wait_ge(bn_sum, 2)
                v.tensor_reduce(tmp_bc[:, :], bank[2][:, :].rearrange("p (j f) -> p f j", f=F), AX.X, ALU.add).then_inc(ch, 1)
                eng.wait_ge(ch, t.up())
                v.tensor_scalar(mean_bc[:, :], tmp_bc[:, :], 1.0 / N, EPS, ALU.mult, ALU.add).then_inc(var_ready, 1)
                eng.wait_ge(sd_ready, 2)
                v.reciprocal(scale_bc[:, :], tmp_bc[:, :]).then_inc(ch, 1)
                eng.wait_ge(ch, t.up())
                v.tensor_tensor(scale_bc[:, :], scale_bc[:, :], g0[:, :], ALU.mult).then_inc(ch, 1)
                eng.wait_ge(ch, t.up())
                v.tensor_tensor(rows(A), rows(A), scale_bc[0:NPT, :].unsqueeze(1).to_broadcast([NPT, NTL, F]), ALU.mult).then_inc(ch, 1)
                eng.wait_ge(ch, t.up())
                v.tensor_tensor(rows(A), rows(A), be0[0:NPT, :].unsqueeze(1).to_broadcast([NPT, NTL, F]), ALU.add).then_inc(ch, 1)
                eng.wait_ge(ch, t.up())
                eng.wait_ge(x_loaded, 32)
                v.tensor_tensor(rows(R), rows(A), rows(U), ALU.add).then_inc(ch, 1)
                eng.wait_ge(ch, t.up())

                def messages(l):
                    def matrix(i, c):
                        n = i * BODY + c
                        eng.wait_ge(mm[l], after(n - 1))
                        if l == 1:
                            one_hot(S[:, c % 2], n).then_inc(onehot[l], 1)
                            return
                        one_hot(S2[:, c % 2], n).then_inc(ch, 1)
                        eng.wait_ge(ch, t.up())
                        v.tensor_tensor(S[:, c % 2], S2[:, c % 2], C[:, bass.ds(n * TB, TB)].unsqueeze(2).to_broadcast([P, TB, W]),
                                        ALU.mult).then_inc(onehot[l], 1)

                    def one(i, c, a, b):
                        if a:
                            matrix(i, c)
                        if b:
                            accumulate(l, i, c - 1, mm[l], D if l == 1 else None, 1)

                    if l == 2:
                        eng.wait_ge(wt_in, 16)
                    links = 1 if l == 2 else 0
                    one(0, 0, True, False)
                    with eng.Fori(0, IT - 1) as i:
                        with t.loop(i, IT - 1, links * BODY):
                            for c in range(1, BODY + 1):
                                one(i, c, True, True)
                    for c in range(1, BODY):
                        one(IT - 1, c, True, True)
                    one(IT - 1, BODY, False, True)

                if LAYERS > 1:
                    head(1, 2)
                    prep(1)
                    clear(1)
                    messages(1)
                    m = node[1, 1]
                    with eng.Fori(0, PAIRS) as i:
                        v.tensor_scalar(st4[:, :], A[:, bass.ds(i * 2 * NPT, 2 * NPT)], 1.0, None, ALU.mult)
                        v.tensor_scalar(st3[0:1, :], D[0:1, bass.ds(i * 2 * NPT, 2 * NPT)], 1.0, None, ALU.mult)
                        v.tensor_scalar(st2[:, :, :].rearrange("p k f -> p (k f)")[:, 0:2 * NPT], U[:, bass.ds(i * 2 * NPT, 2 * NPT)],
                                        1.0, None, ALU.mult).then_inc(m["st"], 1)
                        eng.wait_ge(m["y"], i + 1)
                        for k in range(2):
                            last = v.tensor_scalar(rc[0:NPT, k:k + 1], bank[k][0:NPT, F:F + 1], 1.0, None, ALU.max)
                        last.then_inc(m["q"], 1)
                        at2 = bass.ds(i * 2 * F, 2 * F)
                        v.tensor_tensor(R[0:NPT, at2], R[0:NPT, at2], bank[2][0:NPT, 0:2 * F], ALU.add)
                        eng.wait_ge(m["q"], i + 1)
                        v.reciprocal(rc[0:NPT, :], rc[0:NPT, :]).then_inc(m["qs"], 1)
                        eng.wait_ge(m["qs"], i + 1)
                        for k in range(2):
                            at = bass.ds(i * 2 * F + k * F, F)
                            last = v.scalar_tensor_tensor(out=R[0:NPT, at], in0=bank[k][0:NPT, 0:F], scalar=rc[0:NPT, k:k + 1], in1=R[0:NPT, at],
                                                          op0=ALU.mult, op1=ALU.add)
                        last.then_inc(m["yout"], 1)
                    eng.wait_ge(m["yout"], PAIRS)

                if LAYERS > 2:
                    head(2, 3)
                    prep(2)
                    clear(2)
                    messages(2)
                    m = node[2, 1]
                    with eng.Fori(0, PAIRS) as i:
                        v.tensor_scalar(st1[:, :, :].rearrange("p k f -> p (k f)")[:, 0:2 * NPT], A[:, bass.ds(i * 2 * NPT, 2 * NPT)],
                                        1.0 - ALPHA, None, ALU.mult).then_inc(m["q"], 1)
                        eng.wait_ge(m["q"], i + 1)
                        v.scalar_tensor_tensor(out=st4[:, :], in0=U[:, bass.ds(i * 2 * NPT, 2 * NPT)], scalar=0.5 + ALPHA,
                                               in1=st1[:, :, :].rearrange("p k f -> p (k f)")[:, 0:2 * NPT], op0=ALU.mult, op1=ALU.add).then_inc(m["st"], 1)
                        eng.wait_ge(m["y"], i + 1)
                        at2 = bass.ds(i * 2 * F, 2 * F)
                        v.tensor_tensor(R[0:NPT, at2], R[0:NPT, at2], bank[2][0:NPT, 0:2 * F], ALU.add).then_inc(m["yout"], 1)
                    eng.wait_ge(m["yout"], PAIRS)

                if LAYERS > 3:
                    head(3, 4)
                    prep(3)
                    eng.wait_ge(node[3, 0]["qs"], PAIRS)
                    clear(3)

                    def layer3(i, c, a, b):
                        n = i * BODY + c
                        if b:
                            accumulate(3, i, c - 1, mm[3], None, 0)
                        if a and not b:
                            one_hot(S[:, c % 2], n).then_inc(onehot[3], 1)
                        if a:
                            eng.wait_ge(mm[3], after(n))
                            one_hot(S[:, (c + 1) % 2], n + 1).then_inc(onehot[3], 1)
                            eng.wait_ge(gathered[c % BODY], 16 * TB * (3 * IT + i + c // BODY + 1))
                            eng.wait_ge(pre, after(n + 1))
                            v.tensor_tensor(ring[:, c % BODY].rearrange("p j f -> p (j f)"), ring[:, c % BODY].rearrange("p j f -> p (j f)"),
                                            bank[2 + c % 2][:, :], ALU.add).then_inc(summed, 1)
                    steps(eng, layer3)
                    m = node[3, 1]
                    with eng.Fori(0, PAIRS) as i:
                        v.tensor_scalar(st3[0:1, :], D[0:1, bass.ds(i * 2 * NPT, 2 * NPT)], 1.0, None, ALU.mult)
                        v.tensor_scalar(st4[:, :], A[:, bass.ds(i * 2 * NPT, 2 * NPT)], 1.0, None, ALU.mult).then_inc(m["st"], 1)
                        eng.wait_ge(m["q"], i + 1)
                        v.tensor_copy(st2[:, :, :].rearrange("p k f -> p (k f)")[:, 0:2 * NPT], bank[0][:, 0:2 * NPT]).then_inc(m["qs"], 1)
                        eng.wait_ge(m["y"], i + 1)
                        at2 = bass.ds(i * 2 * F, 2 * F)
                        v.scalar_tensor_tensor(out=U[0:NPT, at2], in0=bank[2][0:NPT, 0:2 * F], scalar=0.0, in1=U[0:NPT, at2],
                                               op0=ALU.max, op1=ALU.add).then_inc(m["yout"], 1)
                    eng.wait_ge(m["yout"], PAIRS)
                    rstd = layernorm(rows(U), rows(A), rows(C), 5)
                    eng.wait_ge(g3_in, 32)
                    v.tensor_tensor(rows(A), rows(A), rstd, ALU.mult).then_inc(ch, 1)
                    eng.wait_ge(ch, t.up())
                    v.tensor_tensor(rows(A), rows(A), g3[0:NPT, :].unsqueeze(1).to_broadcast([NPT, NTL, F]), ALU.mult).then_inc(ch, 1)
                    eng.wait_ge(ch, t.up())
                    v.tensor_tensor(rows(A), rows(A), be3[0:NPT, :].unsqueeze(1).to_broadcast([NPT, NTL, F]), ALU.add).then_inc(ch, 1)
                    eng.wait_ge(ch, t.up())
                    v.tensor_tensor(rows(R), rows(R), rows(A), ALU.add).then_inc(ch, 1)
                    eng.wait_ge(ch, t.up())

            by_mode(eng, run)
            v.memset(tmp_bc[0:1, 0:1], 0.0).then_inc(y_done, 1)

        @block.gpsimd
        def _(eng):
            g = nc.gpsimd
            g.iota(iota[:, :], [[1, P]], base=0, channel_multiplier=0, allow_small_or_imprecise_dtypes=True).then_inc(consts, 1)
            g.memset(ones[:, :], 1.0).then_inc(consts, 1)
            g.memset(ident[:, :], 0.0).then_inc(s_id, 1)
            eng.wait_ge(s_id, 1)
            g.affine_select(out=ident[:, :], in_=ident[:, :], compare_op=ALU.not_equal, fill=1.0, base=0, pattern=[[-1, P]],
                            channel_multiplier=1).then_inc(consts, 1)
            for l in range(LAYERS):
                eng.wait_ge(h_stored, 16 * STORED[l])
                with eng.Fori(0, IT) as i:
                    for c in range(BODY):
                        p = c // PIECE
                        if c % PIECE == 0:
                            when(idx_ready[p], 16 * (l * IT + i + 1), eng, "pool")
                        when(mm[l], after(i * BODY + c - BODY + 1), eng, "pool")
                        for j in range(TB):
                            k = (c % PIECE) * TB + j
                            g.indirect_dma_start(
                                out=ring[:, c, j, :], out_offset=None, in_=h_table[:, :],
                                in_offset=bass.IndirectOffsetOnAxis(ap=idx[:, p, k:k + 1], axis=0)).then_inc(gathered[c], 16)

        @block.sync
        def _(eng):
            def load(to, of, sem_=loaded):
                eng.dma_start(to, of).then_inc(sem_, 16)

            one = lambda a: a.rearrange("(a n) -> a n", a=1)
            by_tile = lambda a: a.rearrange("(t p) f -> p t f", p=NPT)
            load(rows(R), by_tile(d["x"]), x_loaded)
            load(dst_i, d["dst_cols"][:, 1:NT + 1])
            load(last_i, d["dst_cols"][P - 1:P, 1:NT + 1])
            for n in raw:
                load(raw[n], d[{"q": "L0_gnn_Wq", "v": "L0_gnn_Wv", "skip": "L0_gnn_Wskip", "w2": "L3_gnn_W2", "wu": "L3_gnn_Wu"}[n]])
            load(raw_w1, d["L3_gnn_W1"])
            for to, n in ((WK, "L0_gnn_Wk"), (WN, "L1_gnn_W_neigh"), (WS, "L1_gnn_W_self"), (W2L, "L2_gnn_W")):
                load(to[:, :], d[n])
            with nc.allow_non_contiguous_dma(reason="small weights beside a bias column"):
                load(bk_we[:, 1:], d["L0_gnn_We"])
                load(bv_we[:, 1:], d["L0_gnn_We"])
                load(bk_we[:, 0:1], d["L0_gnn_bk"].rearrange("(n a) -> n a", a=1))
                load(bv_we[:, 0:1], d["L0_gnn_bv"].rearrange("(n a) -> n a", a=1))
                load(bq_c[:, :], d["L0_gnn_bq"].rearrange("(n a) -> n a", a=1))
            for to, n in ((g0, "L0_gnn_gamma"), (be0, "L0_gnn_beta")):
                load(to[:, :], d[n].partition_broadcast(P))
            for to, n in ((bskip, "L0_gnn_bskip"), (bself, "L1_gnn_b_self"), (btwo, "L2_gnn_b"), (b1, "L3_gnn_b1"), (b2, "L3_gnn_b2"),
                          (bu, "L3_gnn_bu")):
                load(to[:, :], one(d[n]))

            def load_idx(l, i, p):
                if not (l == 0 and isinstance(i, int) and i == 0):
                    for c in range(p * PIECE, (p + 1) * PIECE):
                        eng.wait_ge(gathered[c], 16 * TB * (l * IT + i))
                load(idx[:, p, :], d["src_cols"][:, bass.ds((2 * i + p) * ST, ST)], idx_ready[p])

            def load_ea(name, done, to, i, c):
                n = i * BODY + c
                eng.wait_ge(done, after(n - 1))
                load(to[:, c % 2, :], d[name][:, bass.ds(n * TB * P, TB * P)], ea_in[c % 2])

            def store(l, buf):
                eng.wait_ge(h_ready, l + 1)
                load(by_tile(h_table), rows(buf), h_stored)

            def run(G, W):
                NW, BOTH = TB // G, W + E3 <= 64
                bwin = S2_[:, 0:2 * NW * F].rearrange("p (k w f) -> p k w f", k=2, f=F)
                store(0, A)
                for p in range(2):
                    load_idx(0, 0, p)

                def layer0(i, more):
                    for p in range(2):
                        s_ = 2 * i + p
                        eng.wait_ge(mm[0], after(s_ * PIECE - PIECE))
                        load(dst_r[:, p, :], d["dst_rows"][bass.ds(s_ * ST, ST), :], sg_in[p])
                        load(ea_rows[:, p, :, :].rearrange("p t e -> p (t e)"), d["ea10_cols"][:, bass.ds(s_ * ST * (E0 + 1), ST * (E0 + 1))], sg_in[p])
                        load(edge_r[0:1, p, 0:ST + 1], d["dst_cols"][P - 1:P, bass.ds(s_ * ST, ST + 1)], sg_in[p])
                        load(edge_r[0:1, p, ST + 1:], d["dst_cols"][0:1, bass.ds(s_ * ST + 1, ST)], sg_in[p])
                        for k in range(PIECE):
                            load_ea("ea10_rows", score, eaT[0:E0 + 1], i, p * PIECE + k)
                        if more:
                            load_idx(0, i + 1, p)
                with eng.Fori(0, IT - 1) as i:
                    layer0(i, True)
                layer0(IT - 1, False)
                eng.wait_ge(node[0, 1]["yout"], PAIRS)
                load(rows(U), by_tile(d["x"]), x_loaded)

                for l in (1, 2)[:max(0, LAYERS - 1)]:
                    store(l, A)
                    if l == 2:
                        eng.wait_ge(node[2, 0]["hT"], PAIRS)
                        load(C[:, 0:NT + TB], d["weight_cols"], wt_in)
                    with eng.Fori(0, IT) as i:
                        for p in range(2):
                            load_idx(l, i, p)

                if LAYERS > 3:
                    eng.wait_ge(node[3, 0]["qs"], PAIRS)
                    load(by_tile(h_table), rows(A), h_stored)
                    load(by_tile(b_table[0:N, :]), rows(C), h_stored)
                    load(b_table[N:N + P, :], ident[:, :], h_stored)
                    for p in range(2):
                        load_idx(3, 0, p)
                    if BOTH:
                        for k in range(2):
                            load(bwin[W:W + E3, k, 0, :], W1cT[:, :], w1c_in)
                    eng.wait_ge(h_stored, 16 * STORED[3])

                    def layer3(i, more):
                        for c in range(BODY):
                            n = i * BODY + c
                            load_ea("ea32_rows", pre, hT[W:W + E3] if BOTH else eaT[:, :, :], i, c)
                            regs = window_bases(eng, n, G)
                            for w in range(NW):
                                load(bwin[0:W, c % 2, w, :], b_table[bass.ds(regs[w], W), :], bw_in[c % 2])
                            if more and c % PIECE == PIECE - 1:
                                load_idx(3, i + 1, c // PIECE)
                    with eng.Fori(0, IT - 1) as i:
                        layer3(i, True)
                    layer3(IT - 1, False)
                    eng.wait_ge(node[3, 1]["st"], 1)
                    for to, n in ((g3, "L3_gnn_gamma"), (be3, "L3_gnn_beta")):
                        load(to, d[n].partition_broadcast(P), g3_in)


            by_mode(eng, run)
            eng.wait_ge(y_done, 1)
            eng.dma_start(by_tile(out), rows(R)).then_inc(stored, 16)
            eng.wait_ge(stored, 16)

        @block.scalar
        def _(eng):
            a = nc.scalar
            for x in (hT_sb, ex_ready, sT_sb, relu):
                eng.sem_inc(x, BODY)

            def root(k, to, of):
                eng.wait_ge(var_ready, k + 1)
                a.activation(to, of, ACT.Sqrt).then_inc(sd_ready, 1)

            def run(G, W):
                stats = stat[0:NPT, 2, :], stat[0:NPT, 1, :]
                root(0, *stats)

                def transposed(i, c):
                    n = i * BODY + c
                    when(hT_ps, after(n + 1), eng, "act")
                    when(score, after(n - 1), eng, "act")
                    a.copy(hT[:, c % 2, :], bank[c % 2][:, :]).then_inc(hT_sb, 1)

                def softmax(i, q):
                    p = q % 2
                    when(sxa, 4 * (2 * i + q) + 4, eng, "act")
                    a.activation(fac[:, :], bank[3][:, 256:257], ACT.Exp)
                    a.activation(ex[:, p, :], bank[3][:, P:P + ST], ACT.Exp).then_inc(ex_ready, 1)

                def layer0(i, q, x, y):
                    if x:
                        for k in range(PIECE):
                            transposed(i, q * PIECE + k)
                        softmax(i, q)
                supersteps(eng, layer0)
                root(1, tmp_bc[:, :], mean_bc[:, :])
                for l in range(1, LAYERS):
                    root(l + 1, *stats)
                if LAYERS > 3:
                    def layer3(i, c, x, y):
                        if x:
                            n = i * BODY + c
                            when(sT_ps, after(n + 1), eng, "act")
                            when(pre, after(n - 1), eng, "act")
                            a.copy(hT[0:W, c % 2, :], bank[c % 2][0:W, :]).then_inc(sT_sb, 1)
                            when(summed, after(n + 1), eng, "act")
                            rows_ = ring[:, c % BODY].rearrange("p j f -> p (j f)")
                            a.activation(rows_, rows_, ACT.Relu).then_inc(relu, 1)
                    steps(eng, layer3)
                    root(5, *stats)

            by_mode(eng, run)

        @block.tensor
        def _(eng):
            def mul(to, l_, r_, start=True, stop=True):
                return nc.tensor.matmul(to, l_, r_, start=start, stop=stop)

            def flip(to, of, n):
                return nc.tensor.transpose(to, of, ident[0:n, 0:n])

            for x in mm + [hT_ps, score, sT_ps, pre]:
                eng.sem_inc(x, BODY)
            eng.wait_ge(loaded, 16 * LOADS)
            eng.wait_ge(consts, 3)
            for k, n in enumerate(("q", "v", "skip", "w2")):
                flip(bank[0][:, k * P:(k + 1) * P], raw[n], P)
            flip(bank[1][:, 0:P], raw["wu"], P)
            for k in range(2):
                flip(bank[1][:, (k + 1) * P:(k + 2) * P], raw_w1[:, k * P:(k + 1) * P], P)
            flip(bank[2][0:E0 + 1, 0:P], bv_we[:, :], P)
            flip(bank[2][0:E3, P:2 * P], raw_w1[:, 2 * P:2 * P + E3], P).then_inc(wT_ps, 1)
            eng.wait_ge(bases_done, 1)
            def run(G, W):
                NW, BOTH = TB // G, W + E3 <= 64
                S = matrices(S_, W)
                bwin = S2_[:, 0:2 * NW * F].rearrange("p (k w f) -> p k w f", k=2, f=F)
                for k in range(NW):
                    mul(bank[4 + k][:, 0:NB], ones[0:1, :], base_f[0:1, k * NB * G:(k + 1) * NB * G:G]).then_inc(base_ps, 1)
                eng.wait_ge(wT_sb, 1)

                def prep(l):
                    m = node[l, 0]
                    def one(i):
                        when(m["st"], i + 1, eng, "pe")
                        for k in range(2):
                            last = flip(bank[0][:, k * NPT:(k + 1) * NPT], st1[0:NPT, k, :], NPT)
                        last.then_inc(m["T"], 1)
                        if l in (1, 2):
                            return
                        when(m["hT"], i + 1, eng, "pe")
                        if l == 3:
                            for k in range(2):
                                to, h = bank[1 + k], st4[:, k * NPT:(k + 1) * NPT]
                                mul(to[0:NPT, 0:F], h, W1abT[:, 0:F])
                                mul(to[0:NPT, F:2 * F], h, W1abT[:, F:2 * F], stop=False)
                                last = mul(to[0:NPT, F:2 * F], ones[0:1, 0:NPT], b1[:, :], start=False)
                            last.then_inc(m["q"], 1)
                            return
                        mul(bank[1][:, 0:2 * NPT], WqT[:, :], st4[:, :])
                        for k in range(2):
                            to = bank[2][0:NPT, k * F:(k + 1) * F]
                            mul(to, st4[:, k * NPT:(k + 1) * NPT], WskT[:, :], stop=False)
                            last = mul(to, ones[0:1, 0:NPT], bskip[:, :], start=False)
                        last.then_inc(m["q"], 1)
                        when(m["qs"], i + 1, eng, "pe")
                        q = st2[:, :, :].rearrange("p k f -> p (k f)")[:, 0:2 * NPT]
                        mul(bank[3][:, 0:2 * NPT], WK[:, :], q)
                        mul(bank[3][0:E0 + 1, 256:256 + 2 * NPT], bk_we[:, :], q).then_inc(m["y"], 1)
                    with eng.Fori(0, PAIRS) as i:
                        one(i)

                prep(0)
                eng.wait_ge(prepared, 1)

                def scores(i, c):
                    n = i * BODY + c
                    regs = window_bases(eng, n, G)
                    when(hT_sb, after(n + 1), eng, "pe")
                    when(ea_in[c % 2], 16 * (PIECE * i + c // 2 + 1), eng, "pe")
                    when(scored, after(n - 1), eng, "pe")
                    for j in range(TB):
                        at = bass.ds(regs[j // G], W)
                        to = bank[2 + c % 2][:, j * W:(j + 1) * W]
                        mul(to, hT[:, c % 2, j * P:(j + 1) * P], U[:, at], stop=False)
                        last = mul(to, eaT[0:E0 + 1, c % 2, j * P:(j + 1) * P], D[0:E0 + 1, at], start=False)
                    last.then_inc(score, 1)

                def sums(l, i, c, ready, of, mat, second):
                    n = i * BODY + c
                    when(ready, after(n + 1), eng, "pe")
                    when(added[l], after(NW * (n - 1)), eng, "pe")
                    for j in range(TB):
                        to = slice((j // G) * W, (j // G + 1) * W)
                        first, end = j % G == 0, j % G == G - 1
                        if second is not None:
                            x = second(j)
                            mul(bank[6 + c % 2][0:x.shape[1], to], x, mat[:, c % 2, j, :], start=first, stop=end)
                        last = mul(bank[4 + c % 2][:, to], of[:, c % BODY, j, :], mat[:, c % 2, j, :], start=first, stop=end)
                    last.then_inc(mm[l], 1)

                def softmax(i, q):
                    s_ = 2 * i + q
                    when(scored, after(s_ * PIECE + PIECE), eng, "pe")
                    flip(bank[2][0:ST, 0:P], alpha[:, :], P).then_inc(sxa, 1)
                    when(sxb, 3 * s_ + 1, eng, "pe")
                    mul(bank[2][0:1, 128:128 + ST], run_f[:, P - 1:P], ident[0:ST, 0:ST])
                    mul(bank[2][0:1, 192:192 + ST], run_b[:, 0:1], ident[0:ST, 0:ST]).then_inc(sxa, 1)
                    when(sxb, 3 * s_ + 2, eng, "pe")
                    for k in range(2):
                        last = mul(bank[3][0:ST, k:k + 1], row[0:1, 6 + k, 0:ST], ones[0:1, 0:1])
                    last.then_inc(sxa, 1)
                    when(sxb, 3 * s_ + 3, eng, "pe")
                    mul(bank[3][:, 256:257], ones[0:1, :], facr[:, :])
                    flip(bank[3][:, P:P + ST], al_t[:, :], ST).then_inc(sxa, 1)

                def layer0(i, q, a, b):
                    if b:
                        when(sg_in[(q - 1) % 2], 64 * (i + (q - 1) // 2 + 1), eng, "pe")
                    for k in range(PIECE):
                        c = q * PIECE + k
                        if a:
                            n = i * BODY + c
                            when(gathered[c % BODY], 16 * TB * (i + c // BODY + 1), eng, "pe")
                            when(hT_sb, after(n - 1), eng, "pe")
                            for j in range(TB):
                                last = flip(bank[c % 2][:, j * P:(j + 1) * P], ring[:, c % BODY, j, :], P)
                            last.then_inc(hT_ps, 1)
                        if b:
                            e = ea_rows[:, (q - 1) % 2]
                            sums(0, i, c - PIECE, onehot2, ring, S, lambda j: e[:, k * TB + j, :])
                        if a:
                            if k == 0:
                                when(ex_ready, after(2 * i + q), eng, "pe")
                            scores(i, c)
                    if a:
                        softmax(i, q)
                supersteps(eng, layer0)

                m = node[0, 1]
                with eng.Fori(0, PAIRS) as i:
                    when(m["st"], i + 1, eng, "pe")
                    for k in range(2):
                        at = slice(k * NPT, (k + 1) * NPT)
                        mul(bank[k][0:NPT, 0:F], st4[:, at], WvT[:, :], stop=False)
                        mul(bank[k][0:NPT, 0:F], st3[:, at], bv_weT[:, 0:F], start=False)
                        last = mul(bank[k][0:NPT, F:F + 1], st3[:, at], bv_weT[:, F:F + 1])
                    last.then_inc(m["y"], 1)
                for k, buf in enumerate((R, C)):
                    eng.wait_ge(bn_x, k + 1)
                    for o in range(0, NCOL, 512):
                        wd = min(512, NCOL - o)
                        last = nc.tensor.matmul(bank[2][:, 0:wd], ones[0:NPT, :], buf[0:NPT, o:o + wd], start=o == 0,
                                                stop=o + 512 >= NCOL, skip_group_check=True)
                    last.then_inc(bn_sum, 1)

                def messages(l):
                    def one(i, c):
                        when(gathered[c], 16 * TB * (l * IT + i + 1), eng, "pe")
                        sums(l, i, c, onehot[l], ring, S, (lambda j: ones[:, 0:1]) if l == 1 else None)
                    with eng.Fori(0, IT) as i:
                        for c in range(BODY):
                            one(i, c)

                if LAYERS > 1:
                    prep(1)
                    eng.wait_ge(prepared, 2)
                    messages(1)
                    m = node[1, 1]
                    with eng.Fori(0, PAIRS) as i:
                        when(m["st"], i + 1, eng, "pe")
                        for k in range(2):
                            at = slice(k * NPT, (k + 1) * NPT)
                            mul(bank[k][0:NPT, 0:F], st4[:, at], WN[:, :])
                            mul(bank[k][0:NPT, F:F + 1], st3[0:1, at], ones[0:1, 0:1])
                            to = bank[2][0:NPT, k * F:(k + 1) * F]
                            mul(to, st2[:, :, :].rearrange("p k f -> p (k f)")[:, at], WS[:, :], stop=False)
                            last = mul(to, ones[0:1, 0:NPT], bself[:, :], start=False)
                        last.then_inc(m["y"], 1)
                if LAYERS > 2:
                    prep(2)
                    eng.wait_ge(prepared, 3)
                    messages(2)
                    m = node[2, 1]
                    with eng.Fori(0, PAIRS) as i:
                        when(m["st"], i + 1, eng, "pe")
                        for k in range(2):
                            to = bank[2][0:NPT, k * F:(k + 1) * F]
                            mul(to, st4[:, k * NPT:(k + 1) * NPT], W2L[:, :], stop=False)
                            last = mul(to, ones[0:1, 0:NPT], btwo[:, :], start=False)
                        last.then_inc(m["y"], 1)
                if LAYERS > 3:
                    prep(3)
                    eng.wait_ge(prepared, 4)
                    if BOTH:
                        eng.wait_ge(w1c_in, 32)

                    def layer3(i, c, a, b):
                        n = i * BODY + c
                        if a:
                            when(onehot[3], after(n + 1), eng, "pe")
                            when(sT_sb, after(n - 1), eng, "pe")
                            for j in range(TB):
                                last = flip(bank[c % 2][0:W, j * P:(j + 1) * P], S[:, c % 2, j, :], P)
                            last.then_inc(sT_ps, 1)
                        if b:
                            sums(3, i, c - 1, relu, ring, S, None)
                        if a:
                            when(sT_sb, after(n + 1), eng, "pe")
                            when(bw_in[c % 2], 16 * NW * (PIECE * i + c // 2 + 1), eng, "pe")
                            when(ea_in[c % 2], 16 * (NB // 2 + PIECE * i + c // 2 + 1), eng, "pe")
                            when(summed, after(n - 1), eng, "pe")
                            for j in range(TB):
                                to, e = bank[2 + c % 2][:, j * P:(j + 1) * P], slice(j * P, (j + 1) * P)
                                if BOTH:
                                    last = mul(to, hT[0:W + E3, c % 2, e], bwin[0:W + E3, c % 2, 0, :])
                                else:
                                    mul(to, hT[:, c % 2, e], bwin[:, c % 2, j // G, :], stop=False)
                                    last = mul(to, eaT[:, c % 2, e], W1cT[:, :], start=False)
                            last.then_inc(pre, 1)
                    steps(eng, layer3)
                    m = node[3, 1]
                    with eng.Fori(0, PAIRS) as i:
                        when(m["st"], i + 1, eng, "pe")
                        mul(bank[0][:, 0:2 * NPT], W2T[:, :], st4[:, :], stop=False)
                        mul(bank[0][:, 0:2 * NPT], b2[:, :], st3[0:1, :], start=False).then_inc(m["q"], 1)
                        when(m["qs"], i + 1, eng, "pe")
                        for k in range(2):
                            to = bank[2][0:NPT, k * F:(k + 1) * F]
                            mul(to, st2[:, :, :].rearrange("p k f -> p (k f)")[:, k * NPT:(k + 1) * NPT], WuT[:, :], stop=False)
                            last = mul(to, ones[0:1, 0:NPT], bu[:, :], start=False)
                        last.then_inc(m["y"], 1)

            by_mode(eng, run)


def kernel(**inputs):
    import numpy as _np
    import concourse.bacc as _bacc
    from concourse import mybir as _mybir
    from concourse.bass_utils import run_bass_kernel_spmd as _run

    nc = _bacc.Bacc("TRN2", target_bir_lowering=False, num_devices=1)
    pad = NT * P - E
    a = {k: _np.asarray(v) for k, v in inputs.items()}
    src, dst, weight = a.pop("src"), a.pop("dst"), a.pop("edge_weight")
    ea10, ea32 = a.pop("edge_attr_10"), a.pop("edge_attr_32")
    dst = _np.pad(dst, (0, pad), constant_values=PAD_DST)
    ea10 = _np.pad(_np.pad(ea10, ((0, pad), (0, 0))), ((0, 0), (1, 0)), constant_values=1)
    a["src_cols"] = _np.pad(src, (0, pad)).reshape(NT, P).T
    a["dst_cols"] = _np.pad(dst.reshape(NT, P).T, ((0, 0), (1, 0)), constant_values=-1)
    a["dst_rows"] = dst.reshape(NT, P)
    a["weight_cols"] = _np.pad(_np.pad(weight, (0, pad)).reshape(NT, P).T, ((0, 0), (0, TB)))
    a["ea10_cols"] = ea10.reshape(NT, P, E0 + 1).transpose(1, 0, 2).reshape(P, NT * (E0 + 1))
    a["ea10_rows"] = ea10.T
    a["ea32_rows"] = _np.pad(ea32, ((0, pad), (0, 0))).T
    arrays, d = {}, {}
    for name, v in a.items():
        v = _np.ascontiguousarray(v)
        arrays["in_" + name] = v
        d[name] = nc.dram_tensor("in_" + name, v.shape, _mybir.dt.from_np(v.dtype), kind="ExternalInput").ap()
    out = nc.dram_tensor("x_out", (N, F), fp32, kind="ExternalOutput").ap()
    program(nc, d, out)
    r = _run(nc, [arrays], core_ids=[0])
    return r.results[0]["x_out"]
```

```python
import concourse.bass as bass
from concourse import mybir
from contextlib import ExitStack, contextmanager

fp32 = mybir.dt.float32
bf16 = mybir.dt.bfloat16
i32 = mybir.dt.int32
ALU = mybir.AluOpType
ACT = mybir.ActivationFunctionType
AX = mybir.AxisListType

N, F, E = 6250, 128, 206250
UC = F + 11
EP = 33
E0, E3 = 10, 32
P = 128
TB = 4
PIECE = 7
BODY = 2 * PIECE
IT = 29
NB = IT * BODY
NT = NB * TB
ST = PIECE * TB
assert NT * P >= E
NPT, NTL = 125, 50
assert NPT * NTL == N
PAIRS = NTL // 2
NCOL = 6400
EPS = 1e-5
BIG = 1e30
ALPHA = 0.05
LAYERS = 4
FEW = (4, 32)
ANY = (1, 128)
STORED = (4, 5, 6, 9)
LOADS = 29
PAD_DST = 2 * N



class Tally:

    def __init__(self):
        self.n, self.i, self.per = 0, 0, 0

    def up(self):
        self.n += 1
        return self.i * self.per + self.n

    @contextmanager
    def loop(self, i, runs, per):
        start = self.n
        self.i, self.per = i, per
        yield
        assert self.n - start == per, (self.n - start, per)
        self.i, self.per, self.n = 0, 0, start + runs * per


def program(nc, d, out):
    SCALE = float(F) ** -0.5
    ctx = ExitStack()
    with ctx:
        def sb(name, shape, dt=fp32):
            return ctx.enter_context(nc.sbuf_tensor(name, shape, dt))

        def sem(name):
            return ctx.enter_context(nc.semaphore(name))

        h_table = nc.dram_tensor("h_table", (N, F), fp32).ap()
        u_table = nc.dram_tensor("u_table", (N + P, 3 * UC), bf16).ap()
        b_table = nc.dram_tensor("b_table", (N + P, F), fp32).ap()

        R = sb("R", [P, NCOL])
        U = sb("U", [P, NCOL])
        A = sb("A", [P, NCOL])
        CD = sb("CD", [P, 2 * NCOL])
        C = CD[:, 0:NCOL]
        D = CD[0:E0 + 1, NCOL:]
        u_rows = CD[0:NPT, 0:NTL * 3 * UC // 2].bitcast(bf16)

        def rows(buf):
            return buf[0:NPT, :].rearrange("p (t f) -> p t f", f=F)

        ring = sb("ring", [P, BODY, TB, F])
        idx = sb("idx", [P, 2, ST], i32)
        dloc = sb("dloc", [P, NT + 2 * TB])
        base_i = sb("base_i", [1, NT], i32)
        flag = sb("flag", [1, 1], i32)
        S_ = sb("S", [P, 2 * TB * P])
        S2_ = sb("S2", [P, 2 * TB * P])
        eaT = C[0:E3, 2 * TB * P:4 * TB * P].rearrange("p (k e) -> p k e", k=2)
        hT = C[:, 0:2 * TB * P].rearrange("p (k e) -> p k e", k=2)
        ea_rows = sb("ea_rows", [P, 2, ST, E0 + 1])
        oh3_ = C[:, 4 * TB * P:5 * TB * P].bitcast(bf16)
        dst_r = sb("dst_r", [ST, 2, P], i32)
        sd = sb("sd", [ST, P])
        step = sb("step", [ST, P + 1])
        run_f = sb("run_f", [ST, P])
        run_b = sb("run_b", [ST, P])
        at_first = sb("at_first", [ST, P])
        at_last = sb("at_last", [ST, P])
        al_t = sb("al_t", [ST, P])
        alpha = sb("alpha", [P, ST])
        ex = sb("ex", [P, 2, ST])
        edge_r = sb("edge_r", [1, 2, 2 * ST + 1], i32)
        row = sb("row", [1, 8, ST + 1])
        tail = sb("tail", [1, 1])
        cin = sb("cin", [ST, 2])
        fac = sb("fac", [P, 1])
        facr = sb("facr", [1, 1])
        iota = sb("iota", [P, P])
        iota3 = sb("iota3", [P, 3 * FEW[1]])
        ident = sb("ident", [P, P])
        ones = sb("ones", [P, P])
        ident_b = sb("ident_b", [P, P], bf16)
        WN, WS, W2L = (sb(n, [P, P]) for n in ("w_neigh", "w_self", "w_two"))
        WKb = sb("wk_bk_we", [P, UC])
        WqT, WvT, WskT, W2T, WuT = (sb(n, [P, P]) for n in ("wqT", "wvT", "wskT", "w2T", "wuT"))
        W1abT = sb("w1abT", [P, 2 * P])
        W1cT = sb("w1cT", [E3, P])
        bv_we = sb("bv_we", [P, 3, E0 + 1])
        bv_weT = sb("bv_weT", [EP, P + 1])
        bq_c = sb("bq_c", [P, 1])
        g0, be0 = (sb(n, [P, P]) for n in ("g0", "be0"))
        g3, be3 = (ring[:, k, 0, :] for k in range(2))
        bskip, bself, btwo, b1, b2, bu = (sb(n, [1, P]) for n in ("bskip", "bself", "btwo", "b1", "b2", "bu"))
        stat = sb("stat", [P, 4, NTL])
        st1 = sb("st1", [P, 2, P])
        st2 = sb("st2", [P, 2, P])
        st3 = sb("st3", [EP, 2 * NPT])
        st4 = sb("st4", [P, 2 * NPT])
        rc = sb("rc", [P, 2])
        mean_bc, scale_bc, tmp_bc = (ring[:, k, 0, :] for k in range(3))

        off = [NT + 8]

        def in_U(width):
            off[0] += width
            assert off[0] <= NCOL
            return U[:, off[0] - width:off[0]]

        win_ = in_U(2 * TB * 3 * UC // 2)
        prod = in_U(TB * UC).rearrange("p (j f) -> p j f", f=UC)
        sT = in_U(TB * P).bitcast(bf16).rearrange("p (k e) -> p k e", k=2)
        oh_ = in_U(TB * P).bitcast(bf16)
        ea_s = in_U(2 * ST * (E0 + 1)).rearrange("p (k t e) -> p k t e", k=2, t=ST)
        dp = in_U(ST * EP // 2).bitcast(bf16).rearrange("p (t a e) -> p t a e", t=ST, a=3)
        dx = in_U(ST * (E0 + 1)).rearrange("p (t e) -> p t e", t=ST)
        off[0] = NT + 8
        ut = in_U(2 * UC)[0:NPT, :]
        up = in_U(3 * UC)[0:NPT, :].bitcast(bf16).rearrange("p (k a f) -> p k a f", k=2, a=3)

        bank = [ctx.enter_context(nc.psum_tensor(f"bank{k}", [P, 512], fp32)) for k in range(8)]

        raw = {n: ring[:, k, 0, :] for k, n in enumerate(("q", "v", "skip", "w2", "wu"))}
        raw_w1 = ring[:, 6, 0:3, :].rearrange("p a f -> p (a f)")[:, 0:2 * F + E3]
        dst_i = C[:, 0:NT].bitcast(i32)
        base_f = U[0:1, 0:NT]
        last_i = A[0:1, 0:NT].bitcast(i32)
        reach = A[0:1, NT:NT + NB]

        s_junk = {e: sem("passed_" + e) for e in ("pool", "act", "pe", "dve", "loads")}
        loaded, consts, x_loaded, wT_ps, wT_sb, bases_done, base_ps = (
            sem(n) for n in ("loaded", "consts", "x_loaded", "wT_ps", "wT_sb", "bases_done", "base_ps"))
        ch = sem("dve_chain")
        flag_ready = sem("flag_ready")
        h_ready, h_stored, var_ready, sd_ready, prepared = (
            sem(n) for n in ("h_ready", "h_stored", "var_ready", "sd_ready", "prepared"))
        node = {(l, w): {n: sem(f"{('prep', 'finish')[w]}{l}_{n}") for n in names} for (l, w), names in {
            (0, 0): ("st", "T", "hT", "q", "qs", "y", "parts", "yout"), (0, 1): ("st", "y", "qs", "yout"),
            (1, 0): ("st", "T", "hT"), (1, 1): ("st", "y", "q", "qs", "yout"),
            (2, 0): ("st", "T", "hT"), (2, 1): ("q", "st", "y", "yout"),
            (3, 0): ("st", "T", "hT", "q", "qs"), (3, 1): ("st", "q", "qs", "y", "yout")}.items()}
        bn_sum, bn_x, y_done, stored, wt_in, w1c_in = (sem(n) for n in ("bn_sum", "bn_x", "y_done", "stored", "wt_in", "w1c_in"))
        idx_ready = [sem(f"idx_ready{p}") for p in range(2)]
        gathered = [sem(f"gathered{b}") for b in range(BODY)]
        ea_in = [sem(f"ea_in{k}") for k in range(2)]
        bw_in = [sem(f"bw_in{k}") for k in range(2)]
        uw_in = [sem(f"uw_in{k}") for k in range(2)]
        es_in = [sem(f"es_in{k}") for k in range(2)]
        sg_in = [sem(f"sg_in{k}") for k in range(2)]
        mm = [sem(f"mm{l}") for l in range(4)]
        onehot = [sem(f"onehot{l}") for l in range(4)]
        added = [sem(f"added{l}") for l in range(4)]
        oh3, oh, ohT_ps, ohT_sb, expanded, multiplied, scored, ex_ready, sT_ps, sT_sb, pre, summed, relu = (
            sem(n) for n in ("oh3", "oh", "ohT_ps", "ohT_sb", "expanded", "multiplied", "scored", "ex_ready", "sT_ps", "sT_sb", "pre", "summed", "relu"))
        g3_in = sem("g3_in")
        s_id = sem("ident_zero")
        sxa, sxb = sem("softmax_pe"), sem("softmax_dve")
        mm2, onehot2 = mm[0], onehot[0]

        block = ctx.enter_context(nc.Block())

        def after(r):
            return r + BODY

        def when(sem_, value, eng, name):
            eng.wait_ge(sem_, value)
            eng.sem_inc(s_junk[name], 1)

        def matrices(buf, W):
            return buf[:, 0:2 * TB * W].rearrange("p (k j w) -> p k j w", k=2, j=TB)

        def windows(W):
            NW = TB * W // P if W < P else TB
            STACK = 3 if 3 * W <= P else 1
            return (oh_[:, 0:2 * TB * STACK * W].rearrange("p (k j w) -> p k j w", k=2, j=TB),
                    win_.bitcast(bf16)[:, 0:2 * NW * 3 * UC // STACK].rearrange("p (k w f) -> p k w f", k=2, w=NW), STACK)

        def window_bases(eng, n, G):
            eng.sem_inc(s_junk["loads"], 1)
            return [eng.value_load(base_i[0:1, bass.ds(n * TB + g, 1)], min_val=0, max_val=N - 1) for g in range(0, TB, G)]

        def by_mode(eng, run):
            eng.wait_ge(flag_ready, 1)
            few = eng.value_load(flag[0:1, 0:1], min_val=0, max_val=1)
            with eng.If(few):
                run(*FEW)
            with eng.Else():
                run(*ANY)

        def steps(eng, one):
            one(0, 0, True, False)
            with eng.Fori(0, IT - 1) as i:
                for c in range(1, BODY + 1):
                    one(i, c, True, True)
            for c in range(1, BODY):
                one(IT - 1, c, True, True)
            one(IT - 1, BODY, False, True)

        def supersteps(eng, one):
            one(0, 0, True, False)
            with eng.Fori(0, IT - 1) as i:
                one(i, 1, True, True)
                one(i, 2, True, True)
            one(IT - 1, 1, True, True)
            one(IT - 1, 2, False, True)

        @block.vector
        def _(eng):
            v = nc.vector
            t = Tally()
            for x in onehot + added + [oh3, oh, multiplied, scored, summed]:
                eng.sem_inc(x, BODY)
            eng.wait_ge(loaded, LOADS * 16)
            eng.wait_ge(consts, 4)
            v.tensor_scalar(base_f, dst_i[0:1, :], float(N - 1), None, ALU.min)
            v.tensor_scalar(reach, last_i[0:1, TB - 1:NT:TB], float(N - 1), None, ALU.min).then_inc(ch, 1)
            eng.wait_ge(ch, t.up())
            v.tensor_copy(base_i[:, :], base_f).then_inc(bases_done, 1)
            v.tensor_tensor(reach, reach, base_f[0:1, 0:NT:TB], ALU.subtract).then_inc(ch, 1)
            eng.wait_ge(ch, t.up())
            v.tensor_reduce(tail[:, :], reach, AX.X, ALU.max).then_inc(ch, 1)
            eng.wait_ge(ch, t.up())
            v.tensor_scalar(flag[:, :], tail[:, :], float(FEW[1]), None, ALU.is_lt).then_inc(flag_ready, 1)
            v.memset(dloc[:, NT:NT + 2 * TB], -1.0)
            v.tensor_copy(ident_b[:, :], ident[:, :])
            v.tensor_reduce(bv_weT[:, P:P + 1], ident[0:EP, 0:EP:E0 + 1], AX.X, ALU.add)
            eng.wait_ge(wT_ps, 1)
            for k, w in enumerate((WqT, WvT, WskT, W2T)):
                v.tensor_copy(w[:, :], bank[0][:, k * P:(k + 1) * P])
            v.tensor_copy(WuT[:, :], bank[1][:, 0:P])
            v.tensor_copy(W1abT[:, :], bank[1][:, P:3 * P])
            v.tensor_copy(bv_weT[:, 0:P], bank[2][0:EP, 0:P])
            v.tensor_copy(W1cT[:, :], bank[2][0:E3, P:2 * P]).then_inc(wT_sb, 1)

            links = t.n

            def run(G, W):
                NW = TB // G
                S, S2 = matrices(S_, W), matrices(S2_, W)
                t.n = links
                for k in range(NW):
                    eng.wait_ge(base_ps, k + 1)
                    tiles = slice(k * NB * G, (k + 1) * NB * G)
                    v.tensor_tensor(dloc[:, tiles].rearrange("p (w g) -> p w g", g=G),
                                    dst_i[:, tiles].rearrange("p (w g) -> p w g", g=G),
                                    bank[4 + k][:, 0:NB].unsqueeze(2).to_broadcast([P, NB, G]), ALU.subtract).then_inc(ch, 1)
                    eng.wait_ge(ch, t.up())

                def layernorm(x, h, sq, l):
                    v.tensor_reduce(stat[0:NPT, 0, :], x, AX.X, ALU.add).then_inc(ch, 1)
                    eng.wait_ge(ch, t.up())
                    v.tensor_scalar(stat[0:NPT, 1, :], stat[0:NPT, 0, :], 1.0 / F, None, ALU.mult).then_inc(ch, 1)
                    eng.wait_ge(ch, t.up())
                    v.tensor_tensor(h, x, stat[0:NPT, 1, :].unsqueeze(2).to_broadcast([NPT, NTL, F]), ALU.subtract).then_inc(ch, 1)
                    eng.wait_ge(ch, t.up())
                    v.tensor_tensor(sq, h, h, ALU.mult).then_inc(ch, 1)
                    eng.wait_ge(ch, t.up())
                    v.tensor_reduce(stat[0:NPT, 0, :], sq, AX.X, ALU.add).then_inc(ch, 1)
                    eng.wait_ge(ch, t.up())
                    v.tensor_scalar(stat[0:NPT, 1, :], stat[0:NPT, 0, :], 1.0 / F, EPS, ALU.mult, ALU.add).then_inc(var_ready, 1)
                    eng.wait_ge(sd_ready, l + 1)
                    v.reciprocal(stat[0:NPT, 3, :], stat[0:NPT, 2, :]).then_inc(ch, 1)
                    eng.wait_ge(ch, t.up())
                    return stat[0:NPT, 3, :].unsqueeze(2).to_broadcast([NPT, NTL, F])

                def head(l, k):
                    hb = rows(U if l == 3 else A)
                    rstd = layernorm(rows(R), hb, rows(C), k)
                    v.scalar_tensor_tensor(out=hb, in0=hb, scalar=0.0, in1=rstd, op0=ALU.max, op1=ALU.mult).then_inc(h_ready, 1)
                    eng.wait_ge(h_ready, l + 1)

                def prep(l):
                    m = node[l, 0]
                    hb = U if l == 3 else A
                    def one(i):
                        v.tensor_scalar(st1[0:NPT, :, :].rearrange("p k f -> p (k f)"),
                                        hb[0:NPT, bass.ds(i * 2 * F, 2 * F)], 1.0, None, ALU.mult).then_inc(m["st"], 1)
                        eng.wait_ge(m["T"], i + 1)
                        if l in (1, 2):
                            v.tensor_scalar(U[:, bass.ds(i * 2 * NPT, 2 * NPT)], bank[0][:, 0:2 * NPT], 1.0, None, ALU.mult).then_inc(m["hT"], 1)
                            return
                        v.tensor_copy(st4[:, :], bank[0][:, 0:2 * NPT]).then_inc(m["hT"], 1)
                        eng.wait_ge(m["q"], i + 1)
                        if l == 3:
                            for k in range(2):
                                v.tensor_scalar(A[0:NPT, bass.ds(i * 2 * F + k * F, F)], bank[1 + k][0:NPT, 0:F], 1.0, None, ALU.mult)
                                last = v.tensor_scalar(C[0:NPT, bass.ds(i * 2 * F + k * F, F)], bank[1 + k][0:NPT, F:2 * F], 1.0, None, ALU.mult)
                            last.then_inc(m["qs"], 1)
                            return
                        v.tensor_scalar(st2[:, :, :].rearrange("p k f -> p (k f)")[:, 0:2 * NPT], bank[1][:, 0:2 * NPT],
                                        bq_c[:, 0:1], None, ALU.add).then_inc(m["qs"], 1)
                        v.tensor_scalar(R[0:NPT, bass.ds(i * 2 * F, 2 * F)], bank[2][0:NPT, 0:2 * F], 1.0, None, ALU.mult)
                        eng.wait_ge(m["y"], i + 1)
                        u = ut.rearrange("p (k f) -> p k f", k=2)
                        v.tensor_scalar(ut, bank[3][0:NPT, 0:2 * UC], SCALE, None, ALU.mult).then_inc(m["parts"], 1)
                        eng.wait_ge(m["parts"], i * 5 + 1)
                        for a in range(2):
                            v.tensor_copy(up[:, :, a, :], u).then_inc(m["parts"], 1)
                            eng.wait_ge(m["parts"], i * 5 + 2 + 2 * a)
                            to = (u, up[:, :, 2, :])[a]
                            v.tensor_tensor(to, u, up[:, :, a, :], ALU.subtract).then_inc(m["parts"], 1)
                            eng.wait_ge(m["parts"], i * 5 + 3 + 2 * a)
                        v.tensor_scalar(u_rows[:, bass.ds(i * 6 * UC, 6 * UC)], up.rearrange("p k a f -> p (k a f)"),
                                        1.0, None, ALU.mult).then_inc(m["yout"], 1)
                    with eng.Fori(0, PAIRS) as i:
                        one(i)

                def one_hot(to, n, nodes=iota[:, 0:W]):
                    shape = [P, TB, nodes.shape[1]]
                    return v.tensor_tensor(to, nodes.unsqueeze(1).to_broadcast(shape),
                                           dloc[:, bass.ds(n * TB, TB)].unsqueeze(2).to_broadcast(shape), ALU.is_equal)

                def clear(l):
                    eng.wait_ge(h_stored, STORED[l] * 16)
                    v.memset(A[:, :], 0.0).then_inc(ch, 1)
                    eng.wait_ge(ch, t.up())
                    if l == 0:
                        v.memset(C[0:EP, :], 0.0).then_inc(prepared, 1)
                    elif l == 1:
                        v.memset(D[0:1, :], 0.0).then_inc(prepared, 1)
                    else:
                        v.memset(tail[:, :], 0.0).then_inc(prepared, 1)
                    eng.wait_ge(prepared, l + 1)

                eng.wait_ge(x_loaded, 16)
                head(0, 0)
                prep(0)
                clear(0)
                v.memset(tail[:, :], -BIG)
                v.memset(row[:, :, :], 0.0)
                v.memset(step[:, :], 0.0).then_inc(ch, 1)
                eng.wait_ge(ch, t.up())
                v.memset(row[0:1, 5, ST:ST + 1], -BIG).then_inc(ch, 1)
                eng.wait_ge(ch, t.up())

                OH, _, STACK = windows(W)
                OH2 = matrices(S2_[:, :].bitcast(bf16), W)

                def locate(n, c):
                    eng.wait_ge(ohT_ps, after(n - 1))
                    one_hot(OH[:, c % 2], n, iota3[:, :] if STACK > 1 else iota[:, :]).then_inc(oh, 1)

                def multiply(i, c):
                    n = i * BODY + c
                    if c % PIECE == 0:
                        eng.wait_ge(es_in[c // PIECE % 2], 16 * (i + c // BODY + 1))
                    eng.wait_ge(gathered[c % BODY], 16 * TB * (i + c // BODY + 1))
                    eng.wait_ge(scored, after(n))
                    eng.wait_ge(expanded, after(n + 1))
                    b = c % PIECE
                    for k in range(2):
                        y = bank[2 + k][:, 0:2 * UC].rearrange("p (j f) -> p j f", f=UC)
                        e = slice(b * TB + 2 * k, b * TB + 2 * k + 2)
                        v.tensor_tensor(prod[:, 2 * k:2 * k + 2, F:], ea_s[:, c // PIECE % 2, e, :], y[:, :, F:], ALU.mult)
                        last = v.tensor_tensor(prod[:, 2 * k:2 * k + 2, 0:F], ring[:, c % BODY, 2 * k:2 * k + 2, :], y[:, :, 0:F], ALU.mult)
                    last.then_inc(multiplied, 1)

                def score(i, c):
                    n, b = i * BODY + c, c % PIECE
                    eng.wait_ge(multiplied, after(n + 1))
                    v.tensor_reduce(alpha[:, b * TB:(b + 1) * TB], prod, AX.X, ALU.add).then_inc(scored, 1)

                def mark(i, c):
                    eng.wait_ge(mm2, after(i * BODY + c - 1))
                    one_hot(OH2[:, c % 2], i * BODY + c).then_inc(ch, 1)
                    return t.up()

                def weigh(c, p, marked):
                    eng.wait_ge(ch, marked)
                    b = c % PIECE
                    v.tensor_tensor(S[:, c % 2], OH2[:, c % 2], ex[:, p, b * TB:(b + 1) * TB].unsqueeze(2).to_broadcast([P, TB, W]),
                                    ALU.mult).then_inc(onehot2, 1)

                def split(p, b0, b1):
                    e = slice(b0 * TB, b1 * TB)
                    shape = [P, (b1 - b0) * TB, E0 + 1]
                    v.tensor_tensor(dx[:, e, :], ea_rows[:, p, e, :], ex[:, p, e].unsqueeze(2).to_broadcast(shape), ALU.mult).then_inc(ch, 1)
                    eng.wait_ge(ch, t.up())
                    for a in range(2):
                        v.tensor_copy(dp[:, e, a, :], dx[:, e, :]).then_inc(ch, 1)
                        eng.wait_ge(ch, t.up())
                        v.tensor_tensor((dx[:, e, :], dp[:, e, 2, :])[a], dx[:, e, :], dp[:, e, a, :], ALU.subtract).then_inc(ch, 1)
                        eng.wait_ge(ch, t.up())

                def accumulate(l, i, c, done, acc2, part2, regs=None):
                    n = i * BODY + c
                    regs = regs or window_bases(eng, n, G)
                    eng.wait_ge(done, after(n + 1))
                    for w in range(NW):
                        at = bass.ds(regs[w], W)
                        eng.wait_ge(added[l], after(NW * n + w))
                        if acc2 is not None:
                            v.tensor_tensor(acc2[0:part2, at], acc2[0:part2, at], bank[6 + c % 2][0:part2, w * W:(w + 1) * W], ALU.add)
                        v.tensor_tensor(A[:, at], A[:, at], bank[4 + c % 2][:, w * W:(w + 1) * W], ALU.add).then_inc(added[l], 1)

                def softmax(i, q):
                    p = q % 2
                    eng.wait_ge(sg_in[p], 64 * (i + q // 2 + 1))
                    v.tensor_scalar(sd[:, :], dst_r[:, p, :], BIG, None, ALU.mult)
                    v.tensor_scalar(row[0:1, 0, :], edge_r[0:1, p, 0:ST + 1], BIG, None, ALU.mult)
                    v.tensor_scalar(row[0:1, 1, 0:ST], edge_r[0:1, p, ST + 1:2 * ST + 1], BIG, None, ALU.mult).then_inc(ch, 1)
                    eng.wait_ge(ch, t.up())
                    v.tensor_tensor(step[:, 1:P], sd[:, 0:P - 1], sd[:, 1:P], ALU.subtract)
                    v.tensor_scalar(at_first[:, :], sd[:, :], sd[:, 0:1], -1.0, ALU.subtract, ALU.mult)
                    v.tensor_scalar(at_last[:, :], sd[:, :], sd[:, P - 1:P], None, ALU.subtract)
                    v.tensor_tensor(row[0:1, 2, 0:ST], row[0:1, 0, 0:ST], row[0:1, 1, 0:ST], ALU.subtract)
                    v.tensor_tensor(row[0:1, 3, 0:ST], row[0:1, 1, 0:ST], row[0:1, 0, 1:ST + 1], ALU.subtract).then_inc(ch, 1)
                    eng.wait_ge(ch, t.up())
                    v.tensor_tensor(row[0:1, 0, 0:ST], row[0:1, 2, 0:ST], row[0:1, 3, 0:ST], ALU.add)
                    v.tensor_tensor(row[0:1, 1, 0:ST], row[0:1, 2, 1:ST + 1], row[0:1, 3, 0:ST], ALU.add)
                    v.tensor_copy(row[0:1, 4, 0:1], tail[:, :])
                    eng.wait_ge(sxa, 4 * (2 * i + q) + 1)
                    v.tensor_copy(al_t[:, :], bank[2][0:ST, 0:P]).then_inc(ch, 1)
                    eng.wait_ge(ch, t.up())
                    v.tensor_tensor_scan(out=run_f[:, :], data0=step[:, 0:P], data1=al_t[:, :], initial=-BIG, op0=ALU.add, op1=ALU.max)
                    v.tensor_tensor_scan(out=run_b[:, ::-1], data0=step[:, 1:P + 1][:, ::-1], data1=al_t[:, ::-1], initial=-BIG,
                                         op0=ALU.add, op1=ALU.max).then_inc(sxb, 1)
                    eng.wait_ge(sxa, 4 * (2 * i + q) + 2)
                    v.tensor_tensor_scan(out=row[0:1, 4, 1:ST + 1], data0=row[0:1, 0, 0:ST], data1=bank[2][0:1, 128:128 + ST],
                                         initial=tail[:, :], op0=ALU.add, op1=ALU.max)
                    v.tensor_tensor_scan(out=row[0:1, 5, 0:ST][:, ::-1], data0=row[0:1, 1, 0:ST][:, ::-1],
                                         data1=bank[2][0:1, 192:192 + ST][:, ::-1], initial=-BIG, op0=ALU.add, op1=ALU.max).then_inc(ch, 1)
                    eng.wait_ge(ch, t.up())
                    v.tensor_tensor(row[0:1, 6, 0:ST], row[0:1, 4, 0:ST], row[0:1, 2, 0:ST], ALU.add)
                    v.tensor_tensor(row[0:1, 7, 0:ST], row[0:1, 5, 1:ST + 1], row[0:1, 2, 1:ST + 1], ALU.add)
                    v.tensor_copy(tail[:, :], row[0:1, 4, ST:ST + 1]).then_inc(sxb, 1)
                    eng.wait_ge(sxa, 4 * (2 * i + q) + 3)
                    v.tensor_copy(cin[:, :], bank[3][0:ST, 0:2]).then_inc(ch, 1)
                    eng.wait_ge(ch, t.up())
                    v.scalar_tensor_tensor(out=run_f[:, :], in0=at_first[:, :], scalar=cin[:, 0:1], in1=run_f[:, :], op0=ALU.add, op1=ALU.max)
                    v.scalar_tensor_tensor(out=run_b[:, :], in0=at_last[:, :], scalar=cin[:, 1:2], in1=run_b[:, :], op0=ALU.add, op1=ALU.max).then_inc(ch, 1)
                    eng.wait_ge(ch, t.up())
                    v.tensor_tensor(run_f[:, :], run_f[:, :], run_b[:, :], ALU.max).then_inc(ch, 1)
                    eng.wait_ge(ch, t.up())
                    v.tensor_tensor(al_t[:, :], al_t[:, :], run_f[:, :], ALU.subtract)
                    v.tensor_tensor(facr[:, :], row[0:1, 6, 0:1], run_f[0:1, 0:1], ALU.subtract).then_inc(sxb, 1)

                def rescale(i, c, q):
                    reg = window_bases(eng, i * BODY + c, TB)[0]
                    eng.wait_ge(ex_ready, after(2 * i + q))
                    if not (isinstance(i, int) and 2 * i + q == 1):
                        eng.wait_ge(added[0], after(NW * PIECE * (2 * i + q - 1)))
                    v.tensor_scalar(C[0:EP, bass.ds(reg, 1)], C[0:EP, bass.ds(reg, 1)], fac[0:EP, 0:1], None, ALU.mult)
                    v.tensor_scalar(A[:, bass.ds(reg, 1)], A[:, bass.ds(reg, 1)], fac[:, 0:1], None, ALU.mult).then_inc(ch, 1)
                    eng.wait_ge(ch, t.up())

                def layer0(i, q, a, b):
                    c, before, p = q * PIECE, (q - 1) * PIECE, (q - 1) % 2
                    if b:
                        rescale(i, before, q)
                        split(p, 0, 1)
                        weigh(before, p, mark(i, before))
                    for k in range(PIECE):
                        early = b and 0 < k < PIECE - 1
                        marked = mark(i, before + k + 1) if early else None
                        if a:
                            locate(i * BODY + c + k + 2, c + k)
                        if early:
                            weigh(before + k + 1, p, marked)
                        add = b and 0 < k < PIECE - 1
                        regs = window_bases(eng, i * BODY + before + k - 1, G) if add else None
                        if a:
                            multiply(i, c + k)
                        if add:
                            accumulate(0, i, before + k - 1, mm2, C, EP, regs)
                        if a:
                            score(i, c + k)
                        if b and k == 0:
                            split(p, 1, PIECE)
                            weigh(before + 1, p, mark(i, before + 1))
                    if a:
                        softmax(i, q)
                    if b:
                        for k in (PIECE - 2, PIECE - 1):
                            accumulate(0, i, before + k, mm2, C, EP)

                locate(0, 0)
                locate(1, 1)
                layer0(0, 0, True, False)
                with eng.Fori(0, IT - 1) as i:
                    with t.loop(i, IT - 1, 2 * (1 + 10 + PIECE + 7)):
                        layer0(i, 1, True, True)
                        layer0(i, 2, True, True)
                layer0(IT - 1, 1, True, True)
                layer0(IT - 1, 2, False, True)

                eng.wait_ge(added[0], after(NW * NB))
                m = node[0, 1]
                with eng.Fori(0, PAIRS) as i:
                    v.tensor_scalar(st4[:, :], A[:, bass.ds(i * 2 * NPT, 2 * NPT)], 1.0, None, ALU.mult)
                    v.tensor_scalar(st3[:, :], C[0:EP, bass.ds(i * 2 * NPT, 2 * NPT)], 1.0, None, ALU.mult).then_inc(m["st"], 1)
                    eng.wait_ge(m["y"], i + 1)
                    for k in range(2):
                        last = v.reciprocal(rc[0:NPT, k:k + 1], bank[k][0:NPT, F:F + 1])
                    last.then_inc(m["qs"], 1)
                    eng.wait_ge(m["qs"], i + 1)
                    for k in range(2):
                        at = bass.ds(i * 2 * F + k * F, F)
                        last = v.scalar_tensor_tensor(out=R[0:NPT, at], in0=bank[k][0:NPT, 0:F], scalar=rc[0:NPT, k:k + 1], in1=R[0:NPT, at],
                                                      op0=ALU.mult, op1=ALU.add)
                    last.then_inc(m["yout"], 1)
                eng.wait_ge(m["yout"], PAIRS)

                v.tensor_scalar(rows(R), rows(R), 0.0, None, ALU.max).then_inc(bn_x, 1)
                eng.wait_ge(bn_sum, 1)
                v.tensor_reduce(tmp_bc[:, :], bank[2][:, :].rearrange("p (j f) -> p f j", f=F), AX.X, ALU.add).then_inc(ch, 1)
                eng.wait_ge(ch, t.up())
                v.tensor_scalar(mean_bc[:, :], tmp_bc[:, :], 1.0 / N, None, ALU.mult).then_inc(ch, 1)
                eng.wait_ge(ch, t.up())
                v.tensor_tensor(rows(A), rows(R), mean_bc[0:NPT, :].unsqueeze(1).to_broadcast([NPT, NTL, F]), ALU.subtract).then_inc(ch, 1)
                eng.wait_ge(ch, t.up())
                v.tensor_tensor(rows(C), rows(A), rows(A), ALU.mult).then_inc(bn_x, 1)
                eng.wait_ge(bn_sum, 2)
                v.tensor_reduce(tmp_bc[:, :], bank[2][:, :].rearrange("p (j f) -> p f j", f=F), AX.X, ALU.add).then_inc(ch, 1)
                eng.wait_ge(ch, t.up())
                v.tensor_scalar(mean_bc[:, :], tmp_bc[:, :], 1.0 / N, EPS, ALU.mult, ALU.add).then_inc(var_ready, 1)
                eng.wait_ge(sd_ready, 2)
                v.reciprocal(scale_bc[:, :], tmp_bc[:, :]).then_inc(ch, 1)
                eng.wait_ge(ch, t.up())
                v.tensor_tensor(scale_bc[:, :], scale_bc[:, :], g0[:, :], ALU.mult).then_inc(ch, 1)
                eng.wait_ge(ch, t.up())
                v.tensor_tensor(rows(A), rows(A), scale_bc[0:NPT, :].unsqueeze(1).to_broadcast([NPT, NTL, F]), ALU.mult).then_inc(ch, 1)
                eng.wait_ge(ch, t.up())
                v.tensor_tensor(rows(A), rows(A), be0[0:NPT, :].unsqueeze(1).to_broadcast([NPT, NTL, F]), ALU.add).then_inc(ch, 1)
                eng.wait_ge(ch, t.up())
                eng.wait_ge(x_loaded, 32)
                v.tensor_tensor(rows(R), rows(A), rows(U), ALU.add).then_inc(ch, 1)
                eng.wait_ge(ch, t.up())

                def messages(l):
                    def matrix(i, c):
                        n = i * BODY + c
                        eng.wait_ge(mm[l], after(n - 1))
                        if l == 1:
                            one_hot(S[:, c % 2], n).then_inc(onehot[l], 1)
                            return
                        one_hot(S2[:, c % 2], n).then_inc(ch, 1)
                        eng.wait_ge(ch, t.up())
                        v.tensor_tensor(S[:, c % 2], S2[:, c % 2], C[:, bass.ds(n * TB, TB)].unsqueeze(2).to_broadcast([P, TB, W]),
                                        ALU.mult).then_inc(onehot[l], 1)

                    def one(i, c, a, b):
                        if a:
                            matrix(i, c)
                        if b:
                            accumulate(l, i, c - 1, mm[l], D if l == 1 else None, 1)

                    if l == 2:
                        eng.wait_ge(wt_in, 16)
                    links = 1 if l == 2 else 0
                    one(0, 0, True, False)
                    with eng.Fori(0, IT - 1) as i:
                        with t.loop(i, IT - 1, links * BODY):
                            for c in range(1, BODY + 1):
                                one(i, c, True, True)
                    for c in range(1, BODY):
                        one(IT - 1, c, True, True)
                    one(IT - 1, BODY, False, True)

                if LAYERS > 1:
                    head(1, 2)
                    prep(1)
                    clear(1)
                    messages(1)
                    eng.wait_ge(added[1], after(NW * NB))
                    m = node[1, 1]
                    with eng.Fori(0, PAIRS) as i:
                        v.tensor_scalar(st4[:, :], A[:, bass.ds(i * 2 * NPT, 2 * NPT)], 1.0, None, ALU.mult)
                        v.tensor_scalar(st3[0:1, :], D[0:1, bass.ds(i * 2 * NPT, 2 * NPT)], 1.0, None, ALU.mult)
                        v.tensor_scalar(st2[:, :, :].rearrange("p k f -> p (k f)")[:, 0:2 * NPT], U[:, bass.ds(i * 2 * NPT, 2 * NPT)],
                                        1.0, None, ALU.mult).then_inc(m["st"], 1)
                        eng.wait_ge(m["y"], i + 1)
                        for k in range(2):
                            last = v.tensor_scalar(rc[0:NPT, k:k + 1], bank[k][0:NPT, F:F + 1], 1.0, None, ALU.max)
                        last.then_inc(m["q"], 1)
                        at2 = bass.ds(i * 2 * F, 2 * F)
                        v.tensor_tensor(R[0:NPT, at2], R[0:NPT, at2], bank[2][0:NPT, 0:2 * F], ALU.add)
                        eng.wait_ge(m["q"], i + 1)
                        v.reciprocal(rc[0:NPT, :], rc[0:NPT, :]).then_inc(m["qs"], 1)
                        eng.wait_ge(m["qs"], i + 1)
                        for k in range(2):
                            at = bass.ds(i * 2 * F + k * F, F)
                            last = v.scalar_tensor_tensor(out=R[0:NPT, at], in0=bank[k][0:NPT, 0:F], scalar=rc[0:NPT, k:k + 1], in1=R[0:NPT, at],
                                                          op0=ALU.mult, op1=ALU.add)
                        last.then_inc(m["yout"], 1)
                    eng.wait_ge(m["yout"], PAIRS)

                if LAYERS > 2:
                    head(2, 3)
                    prep(2)
                    clear(2)
                    messages(2)
                    eng.wait_ge(added[2], after(NW * NB))
                    m = node[2, 1]
                    with eng.Fori(0, PAIRS) as i:
                        v.tensor_scalar(st1[:, :, :].rearrange("p k f -> p (k f)")[:, 0:2 * NPT], A[:, bass.ds(i * 2 * NPT, 2 * NPT)],
                                        1.0 - ALPHA, None, ALU.mult).then_inc(m["q"], 1)
                        eng.wait_ge(m["q"], i + 1)
                        v.scalar_tensor_tensor(out=st4[:, :], in0=U[:, bass.ds(i * 2 * NPT, 2 * NPT)], scalar=0.5 + ALPHA,
                                               in1=st1[:, :, :].rearrange("p k f -> p (k f)")[:, 0:2 * NPT], op0=ALU.mult, op1=ALU.add).then_inc(m["st"], 1)
                        eng.wait_ge(m["y"], i + 1)
                        at2 = bass.ds(i * 2 * F, 2 * F)
                        v.tensor_tensor(R[0:NPT, at2], R[0:NPT, at2], bank[2][0:NPT, 0:2 * F], ALU.add).then_inc(m["yout"], 1)
                    eng.wait_ge(m["yout"], PAIRS)

                if LAYERS > 3:
                    head(3, 4)
                    prep(3)
                    eng.wait_ge(node[3, 0]["qs"], PAIRS)
                    clear(3)

                    OH3 = matrices(oh3_, W)

                    def locate3(n, c):
                        eng.wait_ge(sT_ps, after(n - 1))
                        one_hot(OH3[:, c % 2], n).then_inc(oh3, 1)

                    def layer3(i, c, a, b):
                        n = i * BODY + c
                        if a:
                            eng.wait_ge(mm[3], after(n - 1))
                            one_hot(S[:, c % 2], n).then_inc(onehot[3], 1)
                            locate3(n + 2, c)
                        regs = window_bases(eng, n - 1, G) if b else None
                        if a:
                            eng.wait_ge(gathered[c % BODY], 16 * TB * (3 * IT + i + c // BODY + 1))
                            eng.wait_ge(pre, after(n + 1))
                            v.tensor_tensor(ring[:, c % BODY].rearrange("p j f -> p (j f)"), ring[:, c % BODY].rearrange("p j f -> p (j f)"),
                                            bank[2 + c % 2][:, :], ALU.add).then_inc(summed, 1)
                        if b:
                            accumulate(3, i, c - 1, mm[3], None, 0, regs)
                    locate3(0, 0)
                    locate3(1, 1)
                    steps(eng, layer3)
                    eng.wait_ge(added[3], after(NW * NB))
                    m = node[3, 1]
                    with eng.Fori(0, PAIRS) as i:
                        v.tensor_scalar(st3[0:1, :], D[0:1, bass.ds(i * 2 * NPT, 2 * NPT)], 1.0, None, ALU.mult)
                        v.tensor_scalar(st4[:, :], A[:, bass.ds(i * 2 * NPT, 2 * NPT)], 1.0, None, ALU.mult).then_inc(m["st"], 1)
                        eng.wait_ge(m["q"], i + 1)
                        v.tensor_copy(st2[:, :, :].rearrange("p k f -> p (k f)")[:, 0:2 * NPT], bank[0][:, 0:2 * NPT]).then_inc(m["qs"], 1)
                        eng.wait_ge(m["y"], i + 1)
                        at2 = bass.ds(i * 2 * F, 2 * F)
                        v.scalar_tensor_tensor(out=U[0:NPT, at2], in0=bank[2][0:NPT, 0:2 * F], scalar=0.0, in1=U[0:NPT, at2],
                                               op0=ALU.max, op1=ALU.add).then_inc(m["yout"], 1)
                    eng.wait_ge(m["yout"], PAIRS)
                    rstd = layernorm(rows(U), rows(A), rows(C), 5)
                    eng.wait_ge(g3_in, 32)
                    v.tensor_tensor(rows(A), rows(A), rstd, ALU.mult).then_inc(ch, 1)
                    eng.wait_ge(ch, t.up())
                    v.tensor_tensor(rows(A), rows(A), g3[0:NPT, :].unsqueeze(1).to_broadcast([NPT, NTL, F]), ALU.mult).then_inc(ch, 1)
                    eng.wait_ge(ch, t.up())
                    v.tensor_tensor(rows(A), rows(A), be3[0:NPT, :].unsqueeze(1).to_broadcast([NPT, NTL, F]), ALU.add).then_inc(ch, 1)
                    eng.wait_ge(ch, t.up())
                    v.tensor_tensor(rows(R), rows(R), rows(A), ALU.add).then_inc(ch, 1)
                    eng.wait_ge(ch, t.up())

            by_mode(eng, run)
            v.memset(tmp_bc[0:1, 0:1], 0.0).then_inc(y_done, 1)

        @block.gpsimd
        def _(eng):
            g = nc.gpsimd
            g.iota(iota[:, :], [[1, P]], base=0, channel_multiplier=0, allow_small_or_imprecise_dtypes=True).then_inc(consts, 1)
            g.iota(iota3[:, :].rearrange("p (a w) -> p a w", a=3), [[0, 3], [1, FEW[1]]], base=0, channel_multiplier=0,
                   allow_small_or_imprecise_dtypes=True).then_inc(consts, 1)
            g.memset(ones[:, :], 1.0).then_inc(consts, 1)
            g.memset(ident[:, :], 0.0).then_inc(s_id, 1)
            eng.wait_ge(s_id, 1)
            g.affine_select(out=ident[:, :], in_=ident[:, :], compare_op=ALU.not_equal, fill=1.0, base=0, pattern=[[-1, P]],
                            channel_multiplier=1).then_inc(consts, 1)
            for l in range(LAYERS):
                eng.wait_ge(h_stored, 16 * STORED[l])
                with eng.Fori(0, IT) as i:
                    for c in range(BODY):
                        p = c // PIECE
                        if c % PIECE == 0:
                            when(idx_ready[p], 16 * (l * IT + i + 1), eng, "pool")
                        when(mm[l], after(i * BODY + c - BODY + 1), eng, "pool")
                        for j in range(TB):
                            k = (c % PIECE) * TB + j
                            g.indirect_dma_start(
                                out=ring[:, c, j, :], out_offset=None, in_=h_table[:, :],
                                in_offset=bass.IndirectOffsetOnAxis(ap=idx[:, p, k:k + 1], axis=0)).then_inc(gathered[c], 16)

        @block.sync
        def _(eng):
            def load(to, of, sem_=loaded):
                eng.dma_start(to, of).then_inc(sem_, 16)

            one = lambda a: a.rearrange("(a n) -> a n", a=1)
            by_tile = lambda a: a.rearrange("(t p) f -> p t f", p=NPT)
            load(rows(R), by_tile(d["x"]), x_loaded)
            load(dst_i, d["dst_cols"][:, 1:NT + 1])
            load(last_i, d["dst_cols"][P - 1:P, 1:NT + 1])
            for n in raw:
                load(raw[n], d[{"q": "L0_gnn_Wq", "v": "L0_gnn_Wv", "skip": "L0_gnn_Wskip", "w2": "L3_gnn_W2", "wu": "L3_gnn_Wu"}[n]])
            load(raw_w1, d["L3_gnn_W1"])
            for to, n in ((WKb[:, 0:F], "L0_gnn_Wk"), (WN[:, :], "L1_gnn_W_neigh"), (WS[:, :], "L1_gnn_W_self"), (W2L[:, :], "L2_gnn_W")):
                load(to, d[n])
            with nc.allow_non_contiguous_dma(reason="small weights beside a bias column"):
                load(WKb[:, F + 1:], d["L0_gnn_We"])
                for k in range(3):
                    load(bv_we[:, k, 1:], d["L0_gnn_We"])
                    load(bv_we[:, k, 0:1], d["L0_gnn_bv"].rearrange("(n a) -> n a", a=1))
                load(WKb[:, F:F + 1], d["L0_gnn_bk"].rearrange("(n a) -> n a", a=1))
                load(bq_c[:, :], d["L0_gnn_bq"].rearrange("(n a) -> n a", a=1))
            for to, n in ((g0, "L0_gnn_gamma"), (be0, "L0_gnn_beta")):
                load(to[:, :], d[n].partition_broadcast(P))
            for to, n in ((bskip, "L0_gnn_bskip"), (bself, "L1_gnn_b_self"), (btwo, "L2_gnn_b"), (b1, "L3_gnn_b1"), (b2, "L3_gnn_b2"),
                          (bu, "L3_gnn_bu")):
                load(to[:, :], one(d[n]))

            def load_idx(l, i, p):
                if not (l == 0 and isinstance(i, int) and i == 0):
                    for c in range(p * PIECE, (p + 1) * PIECE):
                        eng.wait_ge(gathered[c], 16 * TB * (l * IT + i))
                load(idx[:, p, :], d["src_cols"][:, bass.ds((2 * i + p) * ST, ST)], idx_ready[p])

            def load_ea(name, done, to, i, c):
                n = i * BODY + c
                eng.wait_ge(done, after(n - 1))
                load(to[:, c % 2, :], d[name][:, bass.ds(n * TB * P, TB * P)], ea_in[c % 2])

            def store(l, buf):
                eng.wait_ge(h_ready, l + 1)
                load(by_tile(h_table), rows(buf), h_stored)

            def run(G, W):
                NW, BOTH = TB // G, W + E3 <= 64
                bwin = S2_[:, 0:2 * NW * F].rearrange("p (k w f) -> p k w f", k=2, f=F)
                store(0, A)
                for p in range(2):
                    load_idx(0, 0, p)
                eng.wait_ge(node[0, 0]["yout"], PAIRS)
                load(by_tile(u_table[0:N, :]), u_rows.rearrange("p (t f) -> p t f", f=3 * UC), h_stored)
                filler = ones[:, :].bitcast(bf16)
                load(u_table[N:N + P, 0:2 * P], filler, h_stored)
                load(u_table[N:N + P, 2 * P:3 * UC], filler[:, 0:3 * UC - 2 * P], h_stored)
                eng.wait_ge(h_stored, 16 * STORED[0])
                _, win, STACK = windows(W)

                def load_es(s_, p):
                    load(ea_s[:, p, :, :].rearrange("p t e -> p (t e)"), d["ea10_cols"][:, bass.ds(s_ * ST * (E0 + 1), ST * (E0 + 1))], es_in[p])

                def layer0(i, more):
                    for p in range(2):
                        s_ = 2 * i + p
                        for k in range(PIECE):
                            n, c = s_ * PIECE + k, p * PIECE + k
                            eng.wait_ge(expanded, after(n - 1))
                            regs = window_bases(eng, n, G)
                            for w in range(NW):
                                for a in range(STACK):
                                    load(win[a * W:(a + 1) * W, c % 2, w, :], u_table[bass.ds(regs[w], W), a * UC:(a + 3 // STACK) * UC], uw_in[c % 2])
                            if k == 1:
                                eng.wait_ge(mm[0], after(s_ * PIECE - PIECE))
                                load(dst_r[:, p, :], d["dst_rows"][bass.ds(s_ * ST, ST), :], sg_in[p])
                                load(ea_rows[:, p, :, :].rearrange("p t e -> p (t e)"), d["ea10_cols"][:, bass.ds(s_ * ST * (E0 + 1), ST * (E0 + 1))], sg_in[p])
                                load(edge_r[0:1, p, 0:ST + 1], d["dst_cols"][P - 1:P, bass.ds(s_ * ST, ST + 1)], sg_in[p])
                                load(edge_r[0:1, p, ST + 1:], d["dst_cols"][0:1, bass.ds(s_ * ST + 1, ST)], sg_in[p])
                            if k == 3 and (more or p == 0):
                                eng.wait_ge(scored, after(s_ * PIECE))
                                load_es(s_ + 1, 1 - p)
                        if more:
                            load_idx(0, i + 1, p)
                load_es(0, 0)
                with eng.Fori(0, IT - 1) as i:
                    layer0(i, True)
                layer0(IT - 1, False)
                eng.wait_ge(node[0, 1]["yout"], PAIRS)
                load(rows(U), by_tile(d["x"]), x_loaded)

                for l in (1, 2)[:max(0, LAYERS - 1)]:
                    store(l, A)
                    if l == 2:
                        eng.wait_ge(node[2, 0]["hT"], PAIRS)
                        load(C[:, 0:NT + TB], d["weight_cols"], wt_in)
                    with eng.Fori(0, IT) as i:
                        for p in range(2):
                            load_idx(l, i, p)

                if LAYERS > 3:
                    eng.wait_ge(node[3, 0]["qs"], PAIRS)
                    load(by_tile(h_table), rows(A), h_stored)
                    load(by_tile(b_table[0:N, :]), rows(C), h_stored)
                    load(b_table[N:N + P, :], ident[:, :], h_stored)
                    for p in range(2):
                        load_idx(3, 0, p)
                    if BOTH:
                        for k in range(2):
                            load(bwin[W:W + E3, k, 0, :], W1cT[:, :], w1c_in)
                    eng.wait_ge(h_stored, 16 * STORED[3])

                    def layer3(i, more):
                        for c in range(BODY):
                            n = i * BODY + c
                            load_ea("ea32_rows", pre, hT[W:W + E3] if BOTH else eaT[:, :, :], i, c)
                            regs = window_bases(eng, n, G)
                            for w in range(NW):
                                load(bwin[0:W, c % 2, w, :], b_table[bass.ds(regs[w], W), :], bw_in[c % 2])
                            if more and c % PIECE == PIECE - 1:
                                load_idx(3, i + 1, c // PIECE)
                    with eng.Fori(0, IT - 1) as i:
                        layer3(i, True)
                    layer3(IT - 1, False)
                    eng.wait_ge(node[3, 1]["st"], 1)
                    for to, n in ((g3, "L3_gnn_gamma"), (be3, "L3_gnn_beta")):
                        load(to, d[n].partition_broadcast(P), g3_in)


            by_mode(eng, run)
            eng.wait_ge(y_done, 1)
            eng.dma_start(by_tile(out), rows(R)).then_inc(stored, 16)
            eng.wait_ge(stored, 16)

        @block.scalar
        def _(eng):
            a = nc.scalar
            for x in (ohT_sb, ex_ready, sT_sb, relu):
                eng.sem_inc(x, BODY)

            def root(k, to, of):
                eng.wait_ge(var_ready, k + 1)
                a.activation(to, of, ACT.Sqrt).then_inc(sd_ready, 1)

            def run(G, W):
                stats = stat[0:NPT, 2, :], stat[0:NPT, 1, :]
                root(0, *stats)

                K = W * windows(W)[2]

                def transposed(n, c):
                    when(ohT_ps, after(n + 1), eng, "act")
                    when(expanded, after(n - 1), eng, "act")
                    a.copy(sT[0:K, c % 2, :], bank[c % 2][0:K, :]).then_inc(ohT_sb, 1)

                def softmax(i, q):
                    p = q % 2
                    when(sxa, 4 * (2 * i + q) + 4, eng, "act")
                    a.activation(fac[:, :], bank[3][:, 256:257], ACT.Exp)
                    a.activation(ex[:, p, :], bank[3][:, P:P + ST], ACT.Exp).then_inc(ex_ready, 1)

                def layer0(i, q, x, y):
                    if x:
                        for k in range(PIECE):
                            n = i * BODY + q * PIECE + k + 1
                            if not (isinstance(n, int) and n == NB):
                                transposed(n, q * PIECE + k + 1)
                        softmax(i, q)
                transposed(0, 0)
                supersteps(eng, layer0)
                root(1, tmp_bc[:, :], mean_bc[:, :])
                for l in range(1, LAYERS):
                    root(l + 1, *stats)
                if LAYERS > 3:
                    def transposed3(n, c):
                        when(sT_ps, after(n + 1), eng, "act")
                        when(pre, after(n - 1), eng, "act")
                        a.copy(hT[0:W, c % 2, :], bank[c % 2][0:W, :]).then_inc(sT_sb, 1)

                    def layer3(i, c, x, y):
                        if x:
                            n = i * BODY + c
                            if not (isinstance(n, int) and n + 1 == NB):
                                transposed3(n + 1, c + 1)
                            when(summed, after(n + 1), eng, "act")
                            rows_ = ring[:, c % BODY].rearrange("p j f -> p (j f)")
                            a.activation(rows_, rows_, ACT.Relu).then_inc(relu, 1)
                    transposed3(0, 0)
                    steps(eng, layer3)
                    root(5, *stats)

            by_mode(eng, run)

        @block.tensor
        def _(eng):
            def mul(to, l_, r_, start=True, stop=True):
                return nc.tensor.matmul(to, l_, r_, start=start, stop=stop)

            def flip(to, of, n):
                return nc.tensor.transpose(to, of, ident[0:n, 0:n])

            for x in mm + [ohT_ps, expanded, sT_ps, pre]:
                eng.sem_inc(x, BODY)
            eng.wait_ge(loaded, 16 * LOADS)
            eng.wait_ge(consts, 4)
            for k, n in enumerate(("q", "v", "skip", "w2")):
                flip(bank[0][:, k * P:(k + 1) * P], raw[n], P)
            flip(bank[1][:, 0:P], raw["wu"], P)
            for k in range(2):
                flip(bank[1][:, (k + 1) * P:(k + 2) * P], raw_w1[:, k * P:(k + 1) * P], P)
            flip(bank[2][0:EP, 0:P], bv_we[:, :, :].rearrange("p a e -> p (a e)"), P)
            flip(bank[2][0:E3, P:2 * P], raw_w1[:, 2 * P:2 * P + E3], P).then_inc(wT_ps, 1)
            eng.wait_ge(bases_done, 1)
            def run(G, W):
                NW, BOTH = TB // G, W + E3 <= 64
                S = matrices(S_, W)
                OH2 = matrices(S2_[:, :].bitcast(bf16), W)
                bwin = S2_[:, 0:2 * NW * F].rearrange("p (k w f) -> p k w f", k=2, f=F)
                for k in range(NW):
                    mul(bank[4 + k][:, 0:NB], ones[0:1, :], base_f[0:1, k * NB * G:(k + 1) * NB * G:G]).then_inc(base_ps, 1)
                eng.wait_ge(wT_sb, 1)

                def prep(l):
                    m = node[l, 0]
                    def one(i):
                        when(m["st"], i + 1, eng, "pe")
                        for k in range(2):
                            last = flip(bank[0][:, k * NPT:(k + 1) * NPT], st1[0:NPT, k, :], NPT)
                        last.then_inc(m["T"], 1)
                        if l in (1, 2):
                            return
                        when(m["hT"], i + 1, eng, "pe")
                        if l == 3:
                            for k in range(2):
                                to, h = bank[1 + k], st4[:, k * NPT:(k + 1) * NPT]
                                mul(to[0:NPT, 0:F], h, W1abT[:, 0:F])
                                mul(to[0:NPT, F:2 * F], h, W1abT[:, F:2 * F], stop=False)
                                last = mul(to[0:NPT, F:2 * F], ones[0:1, 0:NPT], b1[:, :], start=False)
                            last.then_inc(m["q"], 1)
                            return
                        mul(bank[1][:, 0:2 * NPT], WqT[:, :], st4[:, :])
                        for k in range(2):
                            to = bank[2][0:NPT, k * F:(k + 1) * F]
                            mul(to, st4[:, k * NPT:(k + 1) * NPT], WskT[:, :], stop=False)
                            last = mul(to, ones[0:1, 0:NPT], bskip[:, :], start=False)
                        last.then_inc(m["q"], 1)
                        when(m["qs"], i + 1, eng, "pe")
                        q = st2[:, :, :].rearrange("p k f -> p (k f)")[:, 0:2 * NPT]
                        for k in range(2):
                            last = mul(bank[3][0:NPT, k * UC:(k + 1) * UC], q[:, k * NPT:(k + 1) * NPT], WKb[:, :])
                        last.then_inc(m["y"], 1)
                    with eng.Fori(0, PAIRS) as i:
                        one(i)

                prep(0)
                eng.wait_ge(prepared, 1)

                OH, win, STACK = windows(W)
                U_LOADS = NW * STACK

                def transpose(n, c):
                    when(oh, after(n + 1), eng, "pe")
                    when(ohT_sb, after(n - 1), eng, "pe")
                    for j in range(TB):
                        last = mul(bank[c % 2][0:STACK * W, j * P:(j + 1) * P], OH[:, c % 2, j, :], ident_b[:, :])
                    last.then_inc(ohT_ps, 1)

                def expand(i, c):
                    n = i * BODY + c
                    when(ohT_sb, after(n + 1), eng, "pe")
                    when(uw_in[c % 2], 16 * U_LOADS * (PIECE * i + c // 2 + 1), eng, "pe")
                    when(multiplied, after(n), eng, "pe")
                    for j in range(TB):
                        to = bank[2 + j // 2][:, (j % 2) * UC:(j % 2 + 1) * UC]
                        products = 3 // STACK
                        for a in range(products):
                            last = mul(to, sT[0:STACK * W, c % 2, j * P:(j + 1) * P], win[0:STACK * W, c % 2, j // G, a * UC:(a + 1) * UC],
                                       start=a == 0, stop=a == products - 1)
                    last.then_inc(expanded, 1)

                def sums(l, i, c, ready, of, mat, second):
                    n = i * BODY + c
                    when(ready, after(n + 1), eng, "pe")
                    when(added[l], after(NW * (n - 1)), eng, "pe")
                    for j in range(TB):
                        to = slice((j // G) * W, (j // G + 1) * W)
                        first, end = j % G == 0, j % G == G - 1
                        if second is not None:
                            x, mat2 = second(j)
                            mul(bank[6 + c % 2][0:x.shape[1], to], x, mat2[:, c % 2, j, :], start=first, stop=end)
                        last = mul(bank[4 + c % 2][:, to], of[:, c % BODY, j, :], mat[:, c % 2, j, :], start=first, stop=end)
                    last.then_inc(mm[l], 1)

                def softmax(i, q, meanwhile):
                    s_ = 2 * i + q
                    when(scored, after(s_ * PIECE + PIECE), eng, "pe")
                    flip(bank[2][0:ST, 0:P], alpha[:, :], P).then_inc(sxa, 1)
                    meanwhile(PIECE - 2)
                    when(sxb, 3 * s_ + 1, eng, "pe")
                    mul(bank[2][0:1, 128:128 + ST], run_f[:, P - 1:P], ident[0:ST, 0:ST])
                    mul(bank[2][0:1, 192:192 + ST], run_b[:, 0:1], ident[0:ST, 0:ST]).then_inc(sxa, 1)
                    meanwhile(PIECE - 1)
                    when(sxb, 3 * s_ + 2, eng, "pe")
                    for k in range(2):
                        last = mul(bank[3][0:ST, k:k + 1], row[0:1, 6 + k, 0:ST], ones[0:1, 0:1])
                    last.then_inc(sxa, 1)
                    when(sxb, 3 * s_ + 3, eng, "pe")
                    mul(bank[3][:, 256:257], ones[0:1, :], facr[:, :])
                    flip(bank[3][:, P:P + ST], al_t[:, :], ST).then_inc(sxa, 1)

                def layer0(i, q, a, b):
                    def sum_up(k):
                        if b:
                            sums(0, i, (q - 1) * PIECE + k, onehot2, ring, S,
                                 lambda j: (dp[:, k * TB + j].rearrange("p a e -> p (a e)"), OH2))

                    for k in range(PIECE):
                        if a:
                            if k == 0:
                                when(ex_ready, after(2 * i + q), eng, "pe")
                            expand(i, q * PIECE + k)
                            n = i * BODY + q * PIECE + k + 1
                            if not (isinstance(n, int) and n == NB):
                                transpose(n, q * PIECE + k + 1)
                        if k < PIECE - 2 or not a:
                            sum_up(k)
                    if a:
                        softmax(i, q, sum_up)
                transpose(0, 0)
                supersteps(eng, layer0)

                m = node[0, 1]
                with eng.Fori(0, PAIRS) as i:
                    when(m["st"], i + 1, eng, "pe")
                    for k in range(2):
                        at = slice(k * NPT, (k + 1) * NPT)
                        mul(bank[k][0:NPT, 0:F], st4[:, at], WvT[:, :], stop=False)
                        mul(bank[k][0:NPT, 0:F], st3[:, at], bv_weT[:, 0:F], start=False)
                        last = mul(bank[k][0:NPT, F:F + 1], st3[:, at], bv_weT[:, F:F + 1])
                    last.then_inc(m["y"], 1)
                for k, buf in enumerate((R, C)):
                    eng.wait_ge(bn_x, k + 1)
                    for o in range(0, NCOL, 512):
                        wd = min(512, NCOL - o)
                        last = nc.tensor.matmul(bank[2][:, 0:wd], ones[0:NPT, :], buf[0:NPT, o:o + wd], start=o == 0,
                                                stop=o + 512 >= NCOL, skip_group_check=True)
                    last.then_inc(bn_sum, 1)

                def messages(l):
                    def one(i, c):
                        when(gathered[c], 16 * TB * (l * IT + i + 1), eng, "pe")
                        sums(l, i, c, onehot[l], ring, S, (lambda j: (ones[:, 0:1], S)) if l == 1 else None)
                    with eng.Fori(0, IT) as i:
                        for c in range(BODY):
                            one(i, c)

                if LAYERS > 1:
                    prep(1)
                    eng.wait_ge(prepared, 2)
                    messages(1)
                    m = node[1, 1]
                    with eng.Fori(0, PAIRS) as i:
                        when(m["st"], i + 1, eng, "pe")
                        for k in range(2):
                            at = slice(k * NPT, (k + 1) * NPT)
                            mul(bank[k][0:NPT, 0:F], st4[:, at], WN[:, :])
                            mul(bank[k][0:NPT, F:F + 1], st3[0:1, at], ones[0:1, 0:1])
                            to = bank[2][0:NPT, k * F:(k + 1) * F]
                            mul(to, st2[:, :, :].rearrange("p k f -> p (k f)")[:, at], WS[:, :], stop=False)
                            last = mul(to, ones[0:1, 0:NPT], bself[:, :], start=False)
                        last.then_inc(m["y"], 1)
                if LAYERS > 2:
                    prep(2)
                    eng.wait_ge(prepared, 3)
                    messages(2)
                    m = node[2, 1]
                    with eng.Fori(0, PAIRS) as i:
                        when(m["st"], i + 1, eng, "pe")
                        for k in range(2):
                            to = bank[2][0:NPT, k * F:(k + 1) * F]
                            mul(to, st4[:, k * NPT:(k + 1) * NPT], W2L[:, :], stop=False)
                            last = mul(to, ones[0:1, 0:NPT], btwo[:, :], start=False)
                        last.then_inc(m["y"], 1)
                if LAYERS > 3:
                    prep(3)
                    eng.wait_ge(prepared, 4)
                    if BOTH:
                        eng.wait_ge(w1c_in, 32)

                    OH3 = matrices(oh3_, W)

                    def transpose3(n, c):
                        when(oh3, after(n + 1), eng, "pe")
                        when(sT_sb, after(n - 1), eng, "pe")
                        for j in range(TB):
                            last = mul(bank[c % 2][0:W, j * P:(j + 1) * P], OH3[:, c % 2, j, :], ident_b[:, :])
                        last.then_inc(sT_ps, 1)

                    def layer3(i, c, a, b):
                        n = i * BODY + c
                        if a:
                            when(sT_sb, after(n + 1), eng, "pe")
                            when(bw_in[c % 2], 16 * NW * (PIECE * i + c // 2 + 1), eng, "pe")
                            when(ea_in[c % 2], 16 * (PIECE * i + c // 2 + 1), eng, "pe")
                            when(summed, after(n - 1), eng, "pe")
                            for j in range(TB):
                                to, e = bank[2 + c % 2][:, j * P:(j + 1) * P], slice(j * P, (j + 1) * P)
                                if BOTH:
                                    last = mul(to, hT[0:W + E3, c % 2, e], bwin[0:W + E3, c % 2, 0, :])
                                else:
                                    mul(to, hT[:, c % 2, e], bwin[:, c % 2, j // G, :], stop=False)
                                    last = mul(to, eaT[:, c % 2, e], W1cT[:, :], start=False)
                            last.then_inc(pre, 1)
                            if not (isinstance(n, int) and n + 1 == NB):
                                transpose3(n + 1, c + 1)
                        if b:
                            sums(3, i, c - 1, relu, ring, S, None)
                    transpose3(0, 0)
                    steps(eng, layer3)
                    m = node[3, 1]
                    with eng.Fori(0, PAIRS) as i:
                        when(m["st"], i + 1, eng, "pe")
                        mul(bank[0][:, 0:2 * NPT], W2T[:, :], st4[:, :], stop=False)
                        mul(bank[0][:, 0:2 * NPT], b2[:, :], st3[0:1, :], start=False).then_inc(m["q"], 1)
                        when(m["qs"], i + 1, eng, "pe")
                        for k in range(2):
                            to = bank[2][0:NPT, k * F:(k + 1) * F]
                            mul(to, st2[:, :, :].rearrange("p k f -> p (k f)")[:, k * NPT:(k + 1) * NPT], WuT[:, :], stop=False)
                            last = mul(to, ones[0:1, 0:NPT], bu[:, :], start=False)
                        last.then_inc(m["y"], 1)

            by_mode(eng, run)


def kernel(**inputs):
    import numpy as _np
    import concourse.bacc as _bacc
    from concourse import mybir as _mybir
    from concourse.bass_utils import run_bass_kernel_spmd as _run

    nc = _bacc.Bacc("TRN2", target_bir_lowering=False, num_devices=1)
    pad = NT * P - E
    a = {k: _np.asarray(v) for k, v in inputs.items()}
    src, dst, weight = a.pop("src"), a.pop("dst"), a.pop("edge_weight")
    ea10, ea32 = a.pop("edge_attr_10"), a.pop("edge_attr_32")
    dst = _np.pad(dst, (0, pad), constant_values=PAD_DST)
    ea10 = _np.pad(_np.pad(ea10, ((0, pad), (0, 0))), ((0, 0), (1, 0)), constant_values=1)
    a["src_cols"] = _np.pad(src, (0, pad)).reshape(NT, P).T
    a["dst_cols"] = _np.pad(dst.reshape(NT, P).T, ((0, 0), (1, 0)), constant_values=-1)
    a["dst_rows"] = dst.reshape(NT, P)
    a["weight_cols"] = _np.pad(_np.pad(weight, (0, pad)).reshape(NT, P).T, ((0, 0), (0, TB)))
    a["ea10_cols"] = ea10.reshape(NT, P, E0 + 1).transpose(1, 0, 2).reshape(P, NT * (E0 + 1))
    a["ea10_rows"] = ea10.T
    a["ea32_rows"] = _np.pad(ea32, ((0, pad), (0, 0))).T
    arrays, d = {}, {}
    for name, v in a.items():
        v = _np.ascontiguousarray(v)
        arrays["in_" + name] = v
        d[name] = nc.dram_tensor("in_" + name, v.shape, _mybir.dt.from_np(v.dtype), kind="ExternalInput").ap()
    out = nc.dram_tensor("x_out", (N, F), fp32, kind="ExternalOutput").ap()
    program(nc, d, out)
    r = _run(nc, [arrays], core_ids=[0])
    return r.results[0]["x_out"]
```

```python
import concourse.bass as bass
from concourse import mybir
from contextlib import ExitStack, contextmanager

fp32 = mybir.dt.float32
bf16 = mybir.dt.bfloat16
i32 = mybir.dt.int32
ALU = mybir.AluOpType
ACT = mybir.ActivationFunctionType
AX = mybir.AxisListType

N, F, E = 6250, 128, 206250
UC = F + 11
EP = 33
E0, E3 = 10, 32
P = 128
TB = 4
PIECE = 7
BODY = 2 * PIECE
IT = 29
NB = IT * BODY
NT = NB * TB
ST = PIECE * TB
assert NT * P >= E
NPT, NTL = 125, 50
assert NPT * NTL == N
PAIRS = NTL // 2
NCOL = 6400
EPS = 1e-5
BIG = 1e30
ALPHA = 0.05
LAYERS = 4
FEW = (4, 32)
ANY = (1, 128)
GATHERABLE = (1, 2, 3, 5)
OTHERS = (4, 4, 4, 7)
HALF = 12
HALVES = (slice(0, 2 * HALF), slice(2 * HALF, NTL))
LOADS = 29
PAD_DST = 2 * N



class Tally:

    def __init__(self):
        self.n, self.i, self.per = 0, 0, 0

    def up(self):
        self.n += 1
        return self.i * self.per + self.n

    @contextmanager
    def loop(self, i, runs, per):
        start = self.n
        self.i, self.per = i, per
        yield
        assert self.n - start == per, (self.n - start, per)
        self.i, self.per, self.n = 0, 0, start + runs * per


def program(nc, d, out):
    SCALE = float(F) ** -0.5
    ctx = ExitStack()
    with ctx:
        def sb(name, shape, dt=fp32):
            return ctx.enter_context(nc.sbuf_tensor(name, shape, dt))

        def sem(name):
            return ctx.enter_context(nc.semaphore(name))

        h_table = nc.dram_tensor("h_table", (N, F), fp32).ap()
        u_table = nc.dram_tensor("u_table", (N + P, 3 * UC), bf16).ap()
        b_table = nc.dram_tensor("b_table", (N + P, F), fp32).ap()

        R = sb("R", [P, NCOL])
        U = sb("U", [P, NCOL])
        A = sb("A", [P, NCOL])
        CD = sb("CD", [P, 2 * NCOL])
        C = CD[:, 0:NCOL]
        D = CD[0:E0 + 1, NCOL:]
        u_rows = CD[0:NPT, 0:NTL * 3 * UC // 2].bitcast(bf16)

        def rows(buf):
            return buf[0:NPT, :].rearrange("p (t f) -> p t f", f=F)

        ring = sb("ring", [P, BODY, TB, F])
        idx = sb("idx", [P, 2, ST], i32)
        dloc = sb("dloc", [P, NT + 2 * TB])
        base_i = sb("base_i", [1, NT], i32)
        flag = sb("flag", [1, 1], i32)
        S_ = sb("S", [P, 2 * TB * P])
        S2_ = sb("S2", [P, 2 * TB * P])
        eaT = C[0:E3, 2 * TB * P:4 * TB * P].rearrange("p (k e) -> p k e", k=2)
        hT = C[:, 0:2 * TB * P].rearrange("p (k e) -> p k e", k=2)
        ea_rows = sb("ea_rows", [P, 2, ST, E0 + 1])
        oh3_ = C[:, 4 * TB * P:5 * TB * P].bitcast(bf16)
        dst_r = sb("dst_r", [ST, 2, P], i32)
        sd = sb("sd", [ST, P])
        step = sb("step", [ST, P + 1])
        run_f = sb("run_f", [ST, P])
        run_b = sb("run_b", [ST, P])
        at_first = sb("at_first", [ST, P])
        at_last = sb("at_last", [ST, P])
        al_t = sb("al_t", [ST, P])
        alpha = sb("alpha", [P, ST])
        ex = sb("ex", [P, 2, ST])
        edge_r = sb("edge_r", [1, 2, 2 * ST + 1], i32)
        row = sb("row", [1, 8, ST + 1])
        tail = sb("tail", [1, 1])
        cin = sb("cin", [ST, 2])
        fac = sb("fac", [P, 1])
        facr = sb("facr", [1, 1])
        iota = sb("iota", [P, P])
        iota3 = sb("iota3", [P, 3 * FEW[1]])
        ident = sb("ident", [P, P])
        ones = sb("ones", [P, P])
        ident_b = sb("ident_b", [P, P], bf16)
        WN, WS, W2L = (sb(n, [P, P]) for n in ("w_neigh", "w_self", "w_two"))
        WKb = sb("wk_bk_we", [P, UC])
        WqT, WskT, W2T, WuT = (sb(n, [P, P]) for n in ("wqT", "wskT", "w2T", "wuT"))
        WvT = sb("wvT", [P, P + 1])
        W1abT = sb("w1abT", [P, 2 * P])
        W1cT = sb("w1cT", [E3, P])
        bv_we = sb("bv_we", [P, 3, E0 + 1])
        bv_weT = sb("bv_weT", [EP, P + 1])
        bq_c = sb("bq_c", [P, 1])
        g0, be0 = (sb(n, [P, P]) for n in ("g0", "be0"))
        g3, be3 = (ring[:, k, 0, :] for k in range(2))
        bskip, btwo, b2 = (sb(n, [1, P]) for n in ("bskip", "btwo", "b2"))
        bself, b1, bu = (sb(n, [P, P]) for n in ("bself", "b1", "bu"))
        stat = sb("stat", [P, 4, NTL])
        st1 = sb("st1", [P, 2, 2 * P])
        st2 = sb("st2", [P, 2, 2 * NPT])
        st3 = sb("st3", [EP, 2, 2 * NPT])
        st4 = sb("st4", [P, 2, 2 * NPT])
        rc = sb("rc", [P, 2, 2])
        mean_bc, scale_bc, tmp_bc = (ring[:, k, 0, :] for k in range(3))

        off = [NT + 8]

        def in_U(width):
            off[0] += width
            assert off[0] <= NCOL
            return U[:, off[0] - width:off[0]]

        win_ = in_U(2 * TB * 3 * UC // 2)
        prod = in_U(TB * UC).rearrange("p (j f) -> p j f", f=UC)
        sT = in_U(TB * P).bitcast(bf16).rearrange("p (k e) -> p k e", k=2)
        oh_ = in_U(TB * P).bitcast(bf16)
        ea_s = in_U(2 * ST * (E0 + 1)).rearrange("p (k t e) -> p k t e", k=2, t=ST)
        dp = in_U(ST * EP // 2).bitcast(bf16).rearrange("p (t a e) -> p t a e", t=ST, a=3)
        dx = in_U(ST * (E0 + 1)).rearrange("p (t e) -> p t e", t=ST)
        off[0] = NT + 8
        ut = in_U(4 * UC)[0:NPT, :].rearrange("p (s f) -> p s f", s=2)
        up = in_U(6 * UC)[0:NPT, :].bitcast(bf16).rearrange("p (s k a f) -> p s k a f", s=2, k=2, a=3)

        bank = [ctx.enter_context(nc.psum_tensor(f"bank{k}", [P, 512], fp32)) for k in range(8)]

        raw = {n: ring[:, k, 0, :] for k, n in enumerate(("q", "v", "skip", "w2", "wu"))}
        raw_w1 = ring[:, 6, 0:3, :].rearrange("p a f -> p (a f)")[:, 0:2 * F + E3]
        dst_i = C[:, 0:NT].bitcast(i32)
        base_f = U[0:1, 0:NT]
        last_i = A[0:1, 0:NT].bitcast(i32)
        reach = A[0:1, NT:NT + NB]

        s_junk = {e: sem("passed_" + e) for e in ("pool", "act", "pe", "dve", "loads")}
        loaded, consts, x_loaded, wT_ps, wT_sb, bases_done, base_ps = (
            sem(n) for n in ("loaded", "consts", "x_loaded", "wT_ps", "wT_sb", "bases_done", "base_ps"))
        ch = sem("dve_chain")
        flag_ready = sem("flag_ready")
        h_ready, h_stored, u_stored, var_ready, sd_ready, prepared = (
            sem(n) for n in ("h_ready", "h_stored", "u_stored", "var_ready", "sd_ready", "prepared"))
        node = {(l, w): {n: sem(f"{('prep', 'finish')[w]}{l}_{n}") for n in names} for (l, w), names in {
            (0, 0): ("st", "T", "hT", "q", "qs", "y", "skip", "parts", "yout"), (0, 1): ("st", "y", "qs", "yout"),
            (1, 0): ("st", "T", "hT"), (1, 1): ("st", "y", "q", "qs", "yout"),
            (2, 0): ("st", "T", "hT"), (2, 1): ("q", "st", "y", "yout"),
            (3, 0): ("st", "T", "hT", "q", "qs"), (3, 1): ("st", "q", "qs", "y", "biased", "yout")}.items()}
        centered, squared, with_beta = (sem(n) for n in ("centered", "squared", "with_beta"))
        bn_sum, bn_x, y_done, stored, wt_in, w1c_in = (sem(n) for n in ("bn_sum", "bn_x", "y_done", "stored", "wt_in", "w1c_in"))
        idx_ready = [sem(f"idx_ready{p}") for p in range(2)]
        gathered = [sem(f"gathered{b}") for b in range(BODY)]
        ea_in = [sem(f"ea_in{k}") for k in range(2)]
        bw_in = [sem(f"bw_in{k}") for k in range(2)]
        uw_in = [sem(f"uw_in{k}") for k in range(2)]
        es_in = [sem(f"es_in{k}") for k in range(2)]
        sg_in = [sem(f"sg_in{k}") for k in range(2)]
        mm = [sem(f"mm{l}") for l in range(4)]
        onehot = [sem(f"onehot{l}") for l in range(4)]
        added = [sem(f"added{l}") for l in range(4)]
        oh3, oh, ohT_ps, ohT_sb, expanded, multiplied, scored, ex_ready, sT_ps, sT_sb, pre, summed, relu = (
            sem(n) for n in ("oh3", "oh", "ohT_ps", "ohT_sb", "expanded", "multiplied", "scored", "ex_ready", "sT_ps", "sT_sb", "pre", "summed", "relu"))
        g3_in = sem("g3_in")
        s_id = sem("ident_zero")
        sxa, sxb = sem("softmax_pe"), sem("softmax_dve")
        mm2, onehot2 = mm[0], onehot[0]

        block = ctx.enter_context(nc.Block())

        def after(r):
            return r + BODY

        def when(sem_, value, eng, name):
            eng.wait_ge(sem_, value)
            eng.sem_inc(s_junk[name], 1)

        def matrices(buf, W):
            return buf[:, 0:2 * TB * W].rearrange("p (k j w) -> p k j w", k=2, j=TB)

        def windows(W):
            NW = TB * W // P if W < P else TB
            STACK = 3 if 3 * W <= P else 1
            return (oh_[:, 0:2 * TB * STACK * W].rearrange("p (k j w) -> p k j w", k=2, j=TB),
                    win_.bitcast(bf16)[:, 0:2 * NW * 3 * UC // STACK].rearrange("p (k w f) -> p k w f", k=2, w=NW), STACK)

        def window_bases(eng, n, G):
            eng.sem_inc(s_junk["loads"], 1)
            return [eng.value_load(base_i[0:1, bass.ds(n * TB + g, 1)], min_val=0, max_val=N - 1) for g in range(0, TB, G)]

        def by_mode(eng, run):
            eng.wait_ge(flag_ready, 1)
            few = eng.value_load(flag[0:1, 0:1], min_val=0, max_val=1)
            with eng.If(few):
                run(*FEW)
            with eng.Else():
                run(*ANY)

        def node_steps(eng, one):
            with eng.Fori(0, PAIRS // 2) as i:
                one(i * 2, 0, True)
                one(i * 2 + 1, 1, True)
            one(PAIRS - 1, 0, False)

        def steps(eng, one):
            one(0, 0, True, False)
            with eng.Fori(0, IT - 1) as i:
                for c in range(1, BODY + 1):
                    one(i, c, True, True)
            for c in range(1, BODY):
                one(IT - 1, c, True, True)
            one(IT - 1, BODY, False, True)

        def supersteps(eng, one):
            one(0, 0, True, False)
            with eng.Fori(0, IT - 1) as i:
                one(i, 1, True, True)
                one(i, 2, True, True)
            one(IT - 1, 1, True, True)
            one(IT - 1, 2, False, True)

        @block.vector
        def _(eng):
            v = nc.vector
            t = Tally()
            for x in onehot + added + [oh3, oh, multiplied, scored, summed]:
                eng.sem_inc(x, BODY)
            eng.wait_ge(loaded, LOADS * 16)
            eng.wait_ge(consts, 4)
            v.tensor_scalar(base_f, dst_i[0:1, :], float(N - 1), None, ALU.min)
            v.tensor_scalar(reach, last_i[0:1, TB - 1:NT:TB], float(N - 1), None, ALU.min).then_inc(ch, 1)
            eng.wait_ge(ch, t.up())
            v.tensor_copy(base_i[:, :], base_f).then_inc(bases_done, 1)
            v.tensor_tensor(reach, reach, base_f[0:1, 0:NT:TB], ALU.subtract).then_inc(ch, 1)
            eng.wait_ge(ch, t.up())
            v.tensor_reduce(tail[:, :], reach, AX.X, ALU.max).then_inc(ch, 1)
            eng.wait_ge(ch, t.up())
            v.tensor_scalar(flag[:, :], tail[:, :], float(FEW[1]), None, ALU.is_lt).then_inc(flag_ready, 1)
            v.memset(dloc[:, NT:NT + 2 * TB], -1.0)
            v.tensor_copy(ident_b[:, :], ident[:, :])
            v.tensor_reduce(bv_weT[:, P:P + 1], ident[0:EP, 0:EP:E0 + 1], AX.X, ALU.add)
            eng.wait_ge(wT_ps, 1)
            v.memset(WvT[:, P:P + 1], 0.0)
            for k, w in enumerate((WqT, WvT, WskT, W2T)):
                v.tensor_copy(w[:, 0:P], bank[0][:, k * P:(k + 1) * P])
            v.tensor_copy(WuT[:, :], bank[1][:, 0:P])
            v.tensor_copy(W1abT[:, :], bank[1][:, P:3 * P])
            v.tensor_copy(bv_weT[:, 0:P], bank[2][0:EP, 0:P])
            v.tensor_copy(W1cT[:, :], bank[2][0:E3, P:2 * P]).then_inc(wT_sb, 1)

            links = t.n

            def run(G, W):
                NW = TB // G
                S, S2 = matrices(S_, W), matrices(S2_, W)
                t.n = links
                for k in range(NW):
                    eng.wait_ge(base_ps, k + 1)
                    tiles = slice(k * NB * G, (k + 1) * NB * G)
                    v.tensor_tensor(dloc[:, tiles].rearrange("p (w g) -> p w g", g=G),
                                    dst_i[:, tiles].rearrange("p (w g) -> p w g", g=G),
                                    bank[4 + k][:, 0:NB].unsqueeze(2).to_broadcast([P, NB, G]), ALU.subtract).then_inc(ch, 1)
                    eng.wait_ge(ch, t.up())

                def layernorm(x, h, sq, l, norm):
                    v.tensor_reduce(stat[0:NPT, 0, :], x, AX.X, ALU.add).then_inc(ch, 1)
                    eng.wait_ge(ch, t.up())
                    v.tensor_scalar(stat[0:NPT, 1, :], stat[0:NPT, 0, :], 1.0 / F, None, ALU.mult).then_inc(ch, 1)
                    eng.wait_ge(ch, t.up())
                    mean = stat[0:NPT, 1, :].unsqueeze(2).to_broadcast([NPT, NTL, F])
                    for tiles in HALVES:
                        v.tensor_tensor(h[:, tiles, :], x[:, tiles, :], mean[:, tiles, :], ALU.subtract).then_inc(centered, 1)
                    for half, tiles in enumerate(HALVES):
                        eng.wait_ge(squared, 2 * norm + half + 1)
                        v.tensor_reduce(stat[0:NPT, 0, tiles], sq[:, tiles, :], AX.X, ALU.add).then_inc(ch, 1)
                        eng.wait_ge(ch, t.up())
                    v.tensor_scalar(stat[0:NPT, 1, :], stat[0:NPT, 0, :], 1.0 / F, EPS, ALU.mult, ALU.add).then_inc(var_ready, 1)
                    eng.wait_ge(sd_ready, l + 1)
                    v.reciprocal(stat[0:NPT, 3, :], stat[0:NPT, 2, :]).then_inc(ch, 1)
                    eng.wait_ge(ch, t.up())
                    return stat[0:NPT, 3, :].unsqueeze(2).to_broadcast([NPT, NTL, F])

                def head(l, k):
                    hb = rows(U if l == 3 else A)
                    rstd = layernorm(rows(R), hb, rows(C), k, l)
                    v.scalar_tensor_tensor(out=hb, in0=hb, scalar=0.0, in1=rstd, op0=ALU.max, op1=ALU.mult).then_inc(h_ready, 1)
                    eng.wait_ge(h_ready, l + 1)

                def prep(l):
                    m = node[l, 0]
                    hb = U if l == 3 else A

                    def stage(n, s_):
                        v.tensor_scalar(st1[0:NPT, s_, :], hb[0:NPT, bass.ds(n * 2 * F, 2 * F)], 1.0, None, ALU.mult).then_inc(m["st"], 1)

                    def one(n, s_, more):
                        bk = bank[4 * s_:4 * s_ + 4]
                        if more:
                            stage(n + 1, 1 - s_)
                            eng.wait_ge(m["st"], n + 2)
                        if l in (1, 2):
                            eng.wait_ge(m["T"], n + 1)
                            v.tensor_scalar(U[:, bass.ds(n * 2 * NPT, 2 * NPT)], bk[0][:, 0:2 * NPT], 1.0, None, ALU.mult).then_inc(m["hT"], 1)
                            return
                        eng.wait_ge(m["q"], n + 1)
                        if l == 3:
                            y = bk[1][0:NPT, :].rearrange("p (k f) -> p k f", k=2)
                            at = bass.ds(n * 2 * F, 2 * F)
                            v.tensor_scalar(A[0:NPT, at].rearrange("p (k f) -> p k f", k=2), y[:, :, 0:F], 1.0, None, ALU.mult)
                            v.tensor_tensor(C[0:NPT, at].rearrange("p (k f) -> p k f", k=2), y[:, :, F:],
                                            b1[0:NPT, :].unsqueeze(1).to_broadcast([NPT, 2, F]), ALU.add).then_inc(m["qs"], 1)
                            return
                        v.tensor_scalar(st2[:, s_, :], bk[1][:, 0:2 * NPT], bq_c[:, 0:1], None, ALU.add).then_inc(m["qs"], 1)
                        eng.wait_ge(m["y"], n + 1)
                        u, parts = ut[:, s_, :].rearrange("p (k f) -> p k f", k=2), up[:, s_]
                        v.tensor_scalar(ut[:, s_, :], bk[3][0:NPT, 0:2 * UC], SCALE, None, ALU.mult).then_inc(m["parts"], 1)
                        eng.wait_ge(m["parts"], n * 5 + 1)
                        for a in range(2):
                            v.tensor_copy(parts[:, :, a, :], u).then_inc(m["parts"], 1)
                            eng.wait_ge(m["parts"], n * 5 + 2 + 2 * a)
                            to = (u, parts[:, :, 2, :])[a]
                            v.tensor_tensor(to, u, parts[:, :, a, :], ALU.subtract).then_inc(m["parts"], 1)
                            eng.wait_ge(m["parts"], n * 5 + 3 + 2 * a)
                        v.tensor_scalar(u_rows[:, bass.ds(n * 6 * UC, 6 * UC)], parts.rearrange("p k a f -> p (k a f)"), 1.0, None, ALU.mult)
                        eng.wait_ge(m["skip"], n + 1)
                        v.tensor_scalar(R[0:NPT, bass.ds(n * 2 * F, 2 * F)], bk[2][0:NPT, 0:2 * F], 1.0, None, ALU.mult).then_inc(m["yout"], 1)
                    stage(0, 0)
                    node_steps(eng, one)

                def one_hot(to, n, nodes=iota[:, 0:W]):
                    shape = [P, TB, nodes.shape[1]]
                    return v.tensor_tensor(to, nodes.unsqueeze(1).to_broadcast(shape),
                                           dloc[:, bass.ds(n * TB, TB)].unsqueeze(2).to_broadcast(shape), ALU.is_equal)

                def clear(l):
                    eng.wait_ge(h_stored, GATHERABLE[l] * 16)
                    v.memset(A[:, :], 0.0).then_inc(ch, 1)
                    eng.wait_ge(ch, t.up())
                    eng.wait_ge(u_stored, OTHERS[l] * 16)
                    if l == 0:
                        v.memset(C[0:EP, :], 0.0).then_inc(prepared, 1)
                    elif l == 1:
                        v.memset(D[0:1, :], 0.0).then_inc(prepared, 1)
                    else:
                        v.memset(tail[:, :], 0.0).then_inc(prepared, 1)
                    eng.wait_ge(prepared, l + 1)

                eng.wait_ge(x_loaded, 16)
                head(0, 0)
                prep(0)
                clear(0)
                v.memset(tail[:, :], -BIG)
                v.memset(row[:, :, :], 0.0)
                v.memset(step[:, :], 0.0).then_inc(ch, 1)
                eng.wait_ge(ch, t.up())
                v.memset(row[0:1, 5, ST:ST + 1], -BIG).then_inc(ch, 1)
                eng.wait_ge(ch, t.up())

                OH, _, STACK = windows(W)
                OH2 = matrices(S2_[:, :].bitcast(bf16), W)

                def locate(n, c):
                    eng.wait_ge(ohT_ps, after(n - 1))
                    one_hot(OH[:, c % 2], n, iota3[:, :] if STACK > 1 else iota[:, :]).then_inc(oh, 1)

                def multiply(i, c):
                    n = i * BODY + c
                    if c % PIECE == 0:
                        eng.wait_ge(es_in[c // PIECE % 2], 16 * (i + c // BODY + 1))
                    eng.wait_ge(gathered[c % BODY], 16 * TB * (i + c // BODY + 1))
                    eng.wait_ge(scored, after(n))
                    eng.wait_ge(expanded, after(n + 1))
                    b = c % PIECE
                    for k in range(2):
                        y = bank[2 + k][:, 0:2 * UC].rearrange("p (j f) -> p j f", f=UC)
                        e = slice(b * TB + 2 * k, b * TB + 2 * k + 2)
                        v.tensor_tensor(prod[:, 2 * k:2 * k + 2, F:], ea_s[:, c // PIECE % 2, e, :], y[:, :, F:], ALU.mult)
                        last = v.tensor_tensor(prod[:, 2 * k:2 * k + 2, 0:F], ring[:, c % BODY, 2 * k:2 * k + 2, :], y[:, :, 0:F], ALU.mult)
                    last.then_inc(multiplied, 1)

                def mark(i, c):
                    eng.wait_ge(mm2, after(i * BODY + c - 1))
                    one_hot(OH2[:, c % 2], i * BODY + c).then_inc(ch, 1)
                    return t.up()

                def weigh(c, p, marked):
                    eng.wait_ge(ch, marked)
                    b = c % PIECE
                    v.tensor_tensor(S[:, c % 2], OH2[:, c % 2], ex[:, p, b * TB:(b + 1) * TB].unsqueeze(2).to_broadcast([P, TB, W]),
                                    ALU.mult).then_inc(onehot2, 1)

                def split(p, b0, b1):
                    e = slice(b0 * TB, b1 * TB)
                    shape = [P, (b1 - b0) * TB, E0 + 1]
                    v.tensor_tensor(dx[:, e, :], ea_rows[:, p, e, :], ex[:, p, e].unsqueeze(2).to_broadcast(shape), ALU.mult).then_inc(ch, 1)
                    eng.wait_ge(ch, t.up())
                    for a in range(2):
                        v.tensor_copy(dp[:, e, a, :], dx[:, e, :]).then_inc(ch, 1)
                        eng.wait_ge(ch, t.up())
                        v.tensor_tensor((dx[:, e, :], dp[:, e, 2, :])[a], dx[:, e, :], dp[:, e, a, :], ALU.subtract).then_inc(ch, 1)
                        eng.wait_ge(ch, t.up())

                def accumulate(l, i, c, done, acc2, part2, regs=None):
                    n = i * BODY + c
                    regs = regs or window_bases(eng, n, G)
                    eng.wait_ge(done, after(n + 1))
                    for w in range(NW):
                        at = bass.ds(regs[w], W)
                        eng.wait_ge(added[l], after(NW * n + w))
                        if acc2 is not None:
                            v.tensor_tensor(acc2[0:part2, at], acc2[0:part2, at], bank[6 + c % 2][0:part2, w * W:(w + 1) * W], ALU.add)
                        v.tensor_tensor(A[:, at], A[:, at], bank[4 + c % 2][:, w * W:(w + 1) * W], ALU.add).then_inc(added[l], 1)

                def softmax(i, q):
                    p = q % 2
                    eng.wait_ge(sg_in[p], 64 * (i + q // 2 + 1))
                    v.tensor_scalar(sd[:, :], dst_r[:, p, :], BIG, None, ALU.mult)
                    v.tensor_scalar(row[0:1, 0, :], edge_r[0:1, p, 0:ST + 1], BIG, None, ALU.mult)
                    v.tensor_scalar(row[0:1, 1, 0:ST], edge_r[0:1, p, ST + 1:2 * ST + 1], BIG, None, ALU.mult).then_inc(ch, 1)
                    eng.wait_ge(ch, t.up())
                    v.tensor_tensor(step[:, 1:P], sd[:, 0:P - 1], sd[:, 1:P], ALU.subtract)
                    v.tensor_scalar(at_first[:, :], sd[:, :], sd[:, 0:1], -1.0, ALU.subtract, ALU.mult)
                    v.tensor_scalar(at_last[:, :], sd[:, :], sd[:, P - 1:P], None, ALU.subtract)
                    v.tensor_tensor(row[0:1, 2, 0:ST], row[0:1, 0, 0:ST], row[0:1, 1, 0:ST], ALU.subtract)
                    v.tensor_tensor(row[0:1, 3, 0:ST], row[0:1, 1, 0:ST], row[0:1, 0, 1:ST + 1], ALU.subtract).then_inc(ch, 1)
                    eng.wait_ge(ch, t.up())
                    v.tensor_tensor(row[0:1, 0, 0:ST], row[0:1, 2, 0:ST], row[0:1, 3, 0:ST], ALU.add)
                    v.tensor_tensor(row[0:1, 1, 0:ST], row[0:1, 2, 1:ST + 1], row[0:1, 3, 0:ST], ALU.add)
                    v.tensor_copy(row[0:1, 4, 0:1], tail[:, :])
                    eng.wait_ge(sxa, 4 * (2 * i + q) + 1)
                    v.tensor_copy(al_t[:, :], bank[2][0:ST, 0:P]).then_inc(ch, 1)
                    eng.wait_ge(ch, t.up())
                    v.tensor_tensor_scan(out=run_f[:, :], data0=step[:, 0:P], data1=al_t[:, :], initial=-BIG, op0=ALU.add, op1=ALU.max)
                    v.tensor_tensor_scan(out=run_b[:, ::-1], data0=step[:, 1:P + 1][:, ::-1], data1=al_t[:, ::-1], initial=-BIG,
                                         op0=ALU.add, op1=ALU.max).then_inc(sxb, 1)
                    eng.wait_ge(sxa, 4 * (2 * i + q) + 2)
                    v.tensor_tensor_scan(out=row[0:1, 4, 1:ST + 1], data0=row[0:1, 0, 0:ST], data1=bank[2][0:1, 128:128 + ST],
                                         initial=tail[:, :], op0=ALU.add, op1=ALU.max)
                    v.tensor_tensor_scan(out=row[0:1, 5, 0:ST][:, ::-1], data0=row[0:1, 1, 0:ST][:, ::-1],
                                         data1=bank[2][0:1, 192:192 + ST][:, ::-1], initial=-BIG, op0=ALU.add, op1=ALU.max).then_inc(ch, 1)
                    eng.wait_ge(ch, t.up())
                    v.tensor_tensor(row[0:1, 6, 0:ST], row[0:1, 4, 0:ST], row[0:1, 2, 0:ST], ALU.add)
                    v.tensor_tensor(row[0:1, 7, 0:ST], row[0:1, 5, 1:ST + 1], row[0:1, 2, 1:ST + 1], ALU.add)
                    v.tensor_copy(tail[:, :], row[0:1, 4, ST:ST + 1]).then_inc(sxb, 1)
                    eng.wait_ge(sxa, 4 * (2 * i + q) + 3)
                    v.tensor_copy(cin[:, :], bank[3][0:ST, 0:2]).then_inc(ch, 1)
                    eng.wait_ge(ch, t.up())
                    v.scalar_tensor_tensor(out=run_f[:, :], in0=at_first[:, :], scalar=cin[:, 0:1], in1=run_f[:, :], op0=ALU.add, op1=ALU.max)
                    v.scalar_tensor_tensor(out=run_b[:, :], in0=at_last[:, :], scalar=cin[:, 1:2], in1=run_b[:, :], op0=ALU.add, op1=ALU.max).then_inc(ch, 1)
                    eng.wait_ge(ch, t.up())
                    v.tensor_tensor(run_f[:, :], run_f[:, :], run_b[:, :], ALU.max).then_inc(ch, 1)
                    eng.wait_ge(ch, t.up())
                    v.tensor_tensor(al_t[:, :], al_t[:, :], run_f[:, :], ALU.subtract)
                    v.tensor_tensor(facr[:, :], row[0:1, 6, 0:1], run_f[0:1, 0:1], ALU.subtract).then_inc(sxb, 1)

                def rescale(i, c, q):
                    reg = window_bases(eng, i * BODY + c, TB)[0]
                    eng.wait_ge(ex_ready, after(2 * i + q))
                    if not (isinstance(i, int) and 2 * i + q == 1):
                        eng.wait_ge(added[0], after(NW * PIECE * (2 * i + q - 1)))
                    v.tensor_scalar(C[0:EP, bass.ds(reg, 1)], C[0:EP, bass.ds(reg, 1)], fac[0:EP, 0:1], None, ALU.mult)
                    v.tensor_scalar(A[:, bass.ds(reg, 1)], A[:, bass.ds(reg, 1)], fac[:, 0:1], None, ALU.mult).then_inc(ch, 1)
                    eng.wait_ge(ch, t.up())

                def layer0(i, q, a, b):
                    c, before, p = q * PIECE, (q - 1) * PIECE, (q - 1) % 2
                    if b:
                        rescale(i, before, q)
                        split(p, 0, 1)
                        weigh(before, p, mark(i, before))
                    for k in range(PIECE):
                        early = b and 0 < k < PIECE - 1
                        marked = mark(i, before + k + 1) if early else None
                        if a:
                            locate(i * BODY + c + k + 2, c + k)
                        if early:
                            weigh(before + k + 1, p, marked)
                        add = b and k > 0
                        regs = window_bases(eng, i * BODY + before + k - 1, G) if add else None
                        if a:
                            multiply(i, c + k)
                        if add:
                            accumulate(0, i, before + k - 1, mm2, C, EP, regs)
                        if b and k == 0:
                            split(p, 1, PIECE)
                            weigh(before + 1, p, mark(i, before + 1))
                    if b:
                        accumulate(0, i, before + PIECE - 1, mm2, C, EP)
                    if a:
                        softmax(i, q)

                locate(0, 0)
                locate(1, 1)
                layer0(0, 0, True, False)
                with eng.Fori(0, IT - 1) as i:
                    with t.loop(i, IT - 1, 2 * (1 + 10 + PIECE + 7)):
                        layer0(i, 1, True, True)
                        layer0(i, 2, True, True)
                layer0(IT - 1, 1, True, True)
                layer0(IT - 1, 2, False, True)

                eng.wait_ge(added[0], after(NW * NB))
                m = node[0, 1]

                def stage0(n, s_):
                    v.tensor_scalar(st4[:, s_, :], A[:, bass.ds(n * 2 * NPT, 2 * NPT)], 1.0, None, ALU.mult)
                    v.tensor_scalar(st3[:, s_, :], C[0:EP, bass.ds(n * 2 * NPT, 2 * NPT)], 1.0, None, ALU.mult).then_inc(m["st"], 1)

                def finish0(n, s_, more):
                    if more:
                        stage0(n + 1, 1 - s_)
                        eng.wait_ge(m["st"], n + 2)
                    eng.wait_ge(m["y"], n + 1)
                    y = bank[4 * s_][0:NPT, 0:2 * (F + 1)].rearrange("p (k f) -> p k f", k=2)
                    v.reciprocal(rc[0:NPT, s_, :].unsqueeze(2), y[:, :, F:]).then_inc(m["qs"], 1)
                    eng.wait_ge(m["qs"], n + 1)
                    for k in range(2):
                        at = bass.ds(n * 2 * F + k * F, F)
                        last = v.scalar_tensor_tensor(out=R[0:NPT, at], in0=y[:, k, 0:F], scalar=rc[0:NPT, s_, k:k + 1], in1=R[0:NPT, at],
                                                      op0=ALU.mult, op1=ALU.add)
                    last.then_inc(m["yout"], 1)
                stage0(0, 0)
                node_steps(eng, finish0)
                eng.wait_ge(m["yout"], PAIRS)

                v.tensor_scalar(rows(R), rows(R), 0.0, None, ALU.max).then_inc(bn_x, 1)
                eng.wait_ge(bn_sum, 1)
                v.tensor_reduce(tmp_bc[:, :], bank[2][:, :].rearrange("p (j f) -> p f j", f=F), AX.X, ALU.add).then_inc(ch, 1)
                eng.wait_ge(ch, t.up())
                v.tensor_scalar(mean_bc[:, :], tmp_bc[:, :], 1.0 / N, None, ALU.mult).then_inc(ch, 1)
                eng.wait_ge(ch, t.up())
                v.tensor_tensor(rows(A), rows(R), mean_bc[0:NPT, :].unsqueeze(1).to_broadcast([NPT, NTL, F]), ALU.subtract).then_inc(ch, 1)
                eng.wait_ge(ch, t.up())
                v.tensor_tensor(rows(C), rows(A), rows(A), ALU.mult).then_inc(bn_x, 1)
                eng.wait_ge(bn_sum, 2)
                v.tensor_reduce(tmp_bc[:, :], bank[2][:, :].rearrange("p (j f) -> p f j", f=F), AX.X, ALU.add).then_inc(ch, 1)
                eng.wait_ge(ch, t.up())
                v.tensor_scalar(mean_bc[:, :], tmp_bc[:, :], 1.0 / N, EPS, ALU.mult, ALU.add).then_inc(var_ready, 1)
                eng.wait_ge(sd_ready, 2)
                v.reciprocal(scale_bc[:, :], tmp_bc[:, :]).then_inc(ch, 1)
                eng.wait_ge(ch, t.up())
                v.tensor_tensor(scale_bc[:, :], scale_bc[:, :], g0[:, :], ALU.mult).then_inc(ch, 1)
                eng.wait_ge(ch, t.up())
                v.tensor_tensor(rows(A), rows(A), scale_bc[0:NPT, :].unsqueeze(1).to_broadcast([NPT, NTL, F]), ALU.mult).then_inc(ch, 1)
                eng.wait_ge(ch, t.up())
                eng.wait_ge(with_beta, 1)
                v.tensor_tensor(rows(R), rows(A), rows(U), ALU.add).then_inc(ch, 1)
                eng.wait_ge(ch, t.up())

                def messages(l):
                    def matrix(i, c):
                        n = i * BODY + c
                        eng.wait_ge(mm[l], after(n - 1))
                        if l == 1:
                            one_hot(S[:, c % 2], n).then_inc(onehot[l], 1)
                            return
                        one_hot(S2[:, c % 2], n).then_inc(ch, 1)
                        eng.wait_ge(ch, t.up())
                        v.tensor_tensor(S[:, c % 2], S2[:, c % 2], C[:, bass.ds(n * TB, TB)].unsqueeze(2).to_broadcast([P, TB, W]),
                                        ALU.mult).then_inc(onehot[l], 1)

                    def one(i, c, a, b):
                        if a:
                            matrix(i, c)
                        if b:
                            accumulate(l, i, c - 1, mm[l], D if l == 1 else None, 1)

                    if l == 2:
                        eng.wait_ge(wt_in, 16)
                    links = 1 if l == 2 else 0
                    one(0, 0, True, False)
                    with eng.Fori(0, IT - 1) as i:
                        with t.loop(i, IT - 1, links * BODY):
                            for c in range(1, BODY + 1):
                                one(i, c, True, True)
                    for c in range(1, BODY):
                        one(IT - 1, c, True, True)
                    one(IT - 1, BODY, False, True)

                head(1, 2)
                prep(1)
                clear(1)
                messages(1)
                eng.wait_ge(added[1], after(NW * NB))
                m = node[1, 1]

                def stage1(n, s_):
                    at = bass.ds(n * 2 * NPT, 2 * NPT)
                    v.tensor_scalar(st4[:, s_, :], A[:, at], 1.0, None, ALU.mult)
                    v.tensor_scalar(st3[0:1, s_, :], D[0:1, at], 1.0, None, ALU.mult)
                    v.tensor_scalar(st2[:, s_, :], U[:, at], 1.0, None, ALU.mult).then_inc(m["st"], 1)

                def finish1(n, s_, more):
                    bk = bank[4 * s_:4 * s_ + 3]
                    if more:
                        stage1(n + 1, 1 - s_)
                        eng.wait_ge(m["st"], n + 2)
                    eng.wait_ge(m["y"], n + 1)
                    v.tensor_scalar(rc[0:NPT, s_, :], bk[2][0:NPT, 0:2], 1.0, None, ALU.max).then_inc(m["q"], 1)
                    v.tensor_tensor(st1[0:NPT, s_, :].rearrange("p (k f) -> p k f", k=2), bk[1][0:NPT, 0:2 * F].rearrange("p (k f) -> p k f", k=2),
                                    bself[0:NPT, :].unsqueeze(1).to_broadcast([NPT, 2, F]), ALU.add).then_inc(m["q"], 1)
                    eng.wait_ge(m["q"], 2 * n + 2)
                    v.reciprocal(rc[0:NPT, s_, :], rc[0:NPT, s_, :])
                    at2 = bass.ds(n * 2 * F, 2 * F)
                    v.tensor_tensor(R[0:NPT, at2], R[0:NPT, at2], st1[0:NPT, s_, :], ALU.add).then_inc(m["qs"], 1)
                    eng.wait_ge(m["qs"], n + 1)
                    for k in range(2):
                        at = bass.ds(n * 2 * F + k * F, F)
                        last = v.scalar_tensor_tensor(out=R[0:NPT, at], in0=bk[0][0:NPT, k * F:(k + 1) * F], scalar=rc[0:NPT, s_, k:k + 1],
                                                      in1=R[0:NPT, at], op0=ALU.mult, op1=ALU.add)
                    last.then_inc(m["yout"], 1)
                stage1(0, 0)
                node_steps(eng, finish1)
                eng.wait_ge(m["yout"], PAIRS)

                head(2, 3)
                prep(2)
                clear(2)
                messages(2)
                eng.wait_ge(added[2], after(NW * NB))
                m = node[2, 1]

                def stage2(n, s_):
                    at = bass.ds(n * 2 * NPT, 2 * NPT)
                    v.tensor_scalar(st1[:, s_, 0:2 * NPT], A[:, at], 1.0 - ALPHA, None, ALU.mult).then_inc(m["q"], 1)
                    eng.wait_ge(m["q"], n + 1)
                    v.scalar_tensor_tensor(out=st4[:, s_, :], in0=U[:, at], scalar=0.5 + ALPHA, in1=st1[:, s_, 0:2 * NPT],
                                           op0=ALU.mult, op1=ALU.add).then_inc(m["st"], 1)

                def finish2(n, s_, more):
                    if more:
                        stage2(n + 1, 1 - s_)
                    eng.wait_ge(m["y"], n + 1)
                    at2 = bass.ds(n * 2 * F, 2 * F)
                    v.tensor_tensor(R[0:NPT, at2], R[0:NPT, at2], bank[4 * s_][0:NPT, 0:2 * F], ALU.add).then_inc(m["yout"], 1)
                stage2(0, 0)
                node_steps(eng, finish2)
                eng.wait_ge(m["yout"], PAIRS)

                head(3, 4)
                prep(3)
                eng.wait_ge(node[3, 0]["qs"], PAIRS)
                clear(3)

                OH3 = matrices(oh3_, W)

                def locate3(n, c):
                    eng.wait_ge(sT_ps, after(n - 1))
                    one_hot(OH3[:, c % 2], n).then_inc(oh3, 1)

                def layer3(i, c, a, b):
                    n = i * BODY + c
                    if a:
                        eng.wait_ge(mm[3], after(n - 1))
                        one_hot(S[:, c % 2], n).then_inc(onehot[3], 1)
                        locate3(n + 2, c)
                    regs = window_bases(eng, n - 1, G) if b else None
                    if a:
                        eng.wait_ge(gathered[c % BODY], 16 * TB * (3 * IT + i + c // BODY + 1))
                        eng.wait_ge(pre, after(n + 1))
                        v.tensor_tensor(ring[:, c % BODY].rearrange("p j f -> p (j f)"), ring[:, c % BODY].rearrange("p j f -> p (j f)"),
                                        bank[2 + c % 2][:, :], ALU.add).then_inc(summed, 1)
                    if b:
                        accumulate(3, i, c - 1, mm[3], None, 0, regs)
                locate3(0, 0)
                locate3(1, 1)
                steps(eng, layer3)
                eng.wait_ge(added[3], after(NW * NB))
                m = node[3, 1]

                def stage3(n, s_):
                    at = bass.ds(n * 2 * NPT, 2 * NPT)
                    v.tensor_scalar(st3[0:1, s_, :], D[0:1, at], 1.0, None, ALU.mult)
                    v.tensor_scalar(st4[:, s_, :], A[:, at], 1.0, None, ALU.mult).then_inc(m["st"], 1)

                def finish3(n, s_, more):
                    if more:
                        stage3(n + 1, 1 - s_)
                        eng.wait_ge(m["st"], n + 2)
                    eng.wait_ge(m["y"], n + 1)
                    v.tensor_tensor(st1[0:NPT, s_, :].rearrange("p (k f) -> p k f", k=2),
                                    bank[4 * s_ + 2][0:NPT, 0:2 * F].rearrange("p (k f) -> p k f", k=2),
                                    bu[0:NPT, :].unsqueeze(1).to_broadcast([NPT, 2, F]), ALU.add).then_inc(m["biased"], 1)
                    eng.wait_ge(m["biased"], n + 1)
                    at2 = bass.ds(n * 2 * F, 2 * F)
                    v.scalar_tensor_tensor(out=U[0:NPT, at2], in0=st1[0:NPT, s_, :], scalar=0.0, in1=U[0:NPT, at2],
                                           op0=ALU.max, op1=ALU.add).then_inc(m["yout"], 1)
                stage3(0, 0)
                node_steps(eng, finish3)
                eng.wait_ge(m["yout"], PAIRS)
                rstd = layernorm(rows(U), rows(A), rows(C), 5, 4)
                eng.wait_ge(g3_in, 32)
                for tiles in HALVES:
                    y, shape = rows(A)[:, tiles, :], [NPT, tiles.stop - tiles.start, F]
                    v.tensor_tensor(y, y, rstd[:, tiles, :], ALU.mult).then_inc(ch, 1)
                    eng.wait_ge(ch, t.up())
                    v.tensor_tensor(y, y, g3[0:NPT, :].unsqueeze(1).to_broadcast(shape), ALU.mult).then_inc(ch, 1)
                    eng.wait_ge(ch, t.up())
                    if tiles.start == 0:
                        eng.wait_ge(with_beta, 2)
                    v.tensor_tensor(rows(R)[:, tiles, :], rows(R)[:, tiles, :], y, ALU.add).then_inc(y_done, 1)

            by_mode(eng, run)

        @block.gpsimd
        def _(eng):
            g = nc.gpsimd
            g.iota(iota[:, :], [[1, P]], base=0, channel_multiplier=0, allow_small_or_imprecise_dtypes=True).then_inc(consts, 1)
            g.iota(iota3[:, :].rearrange("p (a w) -> p a w", a=3), [[0, 3], [1, FEW[1]]], base=0, channel_multiplier=0,
                   allow_small_or_imprecise_dtypes=True).then_inc(consts, 1)
            g.memset(ones[:, :], 1.0).then_inc(consts, 1)
            g.memset(ident[:, :], 0.0).then_inc(s_id, 1)
            eng.wait_ge(s_id, 1)
            g.affine_select(out=ident[:, :], in_=ident[:, :], compare_op=ALU.not_equal, fill=1.0, base=0, pattern=[[-1, P]],
                            channel_multiplier=1).then_inc(consts, 1)
            def add_beta(x, beta, ready):
                eng.wait_ge(ready, 32)
                g.tensor_tensor(rows(x), rows(x), beta[0:NPT, :].unsqueeze(1).to_broadcast([NPT, NTL, F]), ALU.add).then_inc(with_beta, 1)

            for l in range(LAYERS):
                if l == 1:
                    add_beta(U, be0, x_loaded)
                if l == 0:
                    eng.wait_ge(wT_ps, 1)
                eng.wait_ge(h_stored, 16 * GATHERABLE[l])
                with eng.Fori(0, IT) as i:
                    for c in range(BODY):
                        p = c // PIECE
                        if c % PIECE == 0:
                            when(idx_ready[p], 16 * (l * IT + i + 1), eng, "pool")
                        when(mm[l], after(i * BODY + c - BODY + 1), eng, "pool")
                        for j in range(TB):
                            k = (c % PIECE) * TB + j
                            g.indirect_dma_start(
                                out=ring[:, c, j, :], out_offset=None, in_=h_table[:, :],
                                in_offset=bass.IndirectOffsetOnAxis(ap=idx[:, p, k:k + 1], axis=0)).then_inc(gathered[c], 16)
            add_beta(R, be3, g3_in)

        @block.sync
        def _(eng):
            def load(to, of, sem_=loaded):
                eng.dma_start(to, of).then_inc(sem_, 16)

            one = lambda a: a.rearrange("(a n) -> a n", a=1)
            by_tile = lambda a: a.rearrange("(t p) f -> p t f", p=NPT)
            load(rows(R), by_tile(d["x"]), x_loaded)
            load(dst_i, d["dst_cols"][:, 1:NT + 1])
            load(last_i, d["dst_cols"][P - 1:P, 1:NT + 1])
            for n in raw:
                load(raw[n], d[{"q": "L0_gnn_Wq", "v": "L0_gnn_Wv", "skip": "L0_gnn_Wskip", "w2": "L3_gnn_W2", "wu": "L3_gnn_Wu"}[n]])
            load(raw_w1, d["L3_gnn_W1"])
            for to, n in ((WKb[:, 0:F], "L0_gnn_Wk"), (WN[:, :], "L1_gnn_W_neigh"), (WS[:, :], "L1_gnn_W_self"), (W2L[:, :], "L2_gnn_W")):
                load(to, d[n])
            with nc.allow_non_contiguous_dma(reason="small weights beside a bias column"):
                load(WKb[:, F + 1:], d["L0_gnn_We"])
                for k in range(3):
                    load(bv_we[:, k, 1:], d["L0_gnn_We"])
                    load(bv_we[:, k, 0:1], d["L0_gnn_bv"].rearrange("(n a) -> n a", a=1))
                load(WKb[:, F:F + 1], d["L0_gnn_bk"].rearrange("(n a) -> n a", a=1))
                load(bq_c[:, :], d["L0_gnn_bq"].rearrange("(n a) -> n a", a=1))
            for to, n in ((g0, "L0_gnn_gamma"), (be0, "L0_gnn_beta")):
                load(to[:, :], d[n].partition_broadcast(P))
            for to, n in ((bskip, "L0_gnn_bskip"), (btwo, "L2_gnn_b"), (b2, "L3_gnn_b2")):
                load(to[:, :], one(d[n]))
            for to, n in ((bself, "L1_gnn_b_self"), (b1, "L3_gnn_b1"), (bu, "L3_gnn_bu")):
                load(to[:, :], d[n].partition_broadcast(P))

            def load_idx(l, i, p):
                if not (l == 0 and isinstance(i, int) and i == 0):
                    for c in range(p * PIECE, (p + 1) * PIECE):
                        eng.wait_ge(gathered[c], 16 * TB * (l * IT + i))
                load(idx[:, p, :], d["src_cols"][:, bass.ds((2 * i + p) * ST, ST)], idx_ready[p])

            def load_ea(name, done, to, i, c):
                n = i * BODY + c
                eng.wait_ge(done, after(n - 1))
                load(to[:, c % 2, :], d[name][:, bass.ds(n * TB * P, TB * P)], ea_in[c % 2])

            def store(l, buf):
                eng.wait_ge(h_ready, l + 1)
                load(by_tile(h_table), rows(buf), h_stored)

            def run(G, W):
                NW, BOTH = TB // G, W + E3 <= 64
                bwin = S2_[:, 0:2 * NW * F].rearrange("p (k w f) -> p k w f", k=2, f=F)
                store(0, A)
                for p in range(2):
                    load_idx(0, 0, p)
                filler = ones[:, :].bitcast(bf16)
                load(u_table[N:N + P, 0:2 * P], filler, u_stored)
                load(u_table[N:N + P, 2 * P:3 * UC], filler[:, 0:3 * UC - 2 * P], u_stored)
                for done, tiles in zip((HALF, PAIRS), HALVES):
                    eng.wait_ge(node[0, 0]["yout"], done)
                    load(by_tile(u_table[0:N, :])[:, tiles, :], u_rows.rearrange("p (t f) -> p t f", f=3 * UC)[:, tiles, :], u_stored)
                eng.wait_ge(u_stored, 16 * OTHERS[0])
                _, win, STACK = windows(W)

                def load_es(s_, p):
                    load(ea_s[:, p, :, :].rearrange("p t e -> p (t e)"), d["ea10_cols"][:, bass.ds(s_ * ST * (E0 + 1), ST * (E0 + 1))], es_in[p])

                def layer0(i, more):
                    for p in range(2):
                        s_ = 2 * i + p
                        for k in range(PIECE):
                            n, c = s_ * PIECE + k, p * PIECE + k
                            eng.wait_ge(expanded, after(n - 1))
                            regs = window_bases(eng, n, G)
                            for w in range(NW):
                                for a in range(STACK):
                                    load(win[a * W:(a + 1) * W, c % 2, w, :], u_table[bass.ds(regs[w], W), a * UC:(a + 3 // STACK) * UC], uw_in[c % 2])
                            if k == 1:
                                eng.wait_ge(mm[0], after(s_ * PIECE - PIECE))
                                load(dst_r[:, p, :], d["dst_rows"][bass.ds(s_ * ST, ST), :], sg_in[p])
                                load(ea_rows[:, p, :, :].rearrange("p t e -> p (t e)"), d["ea10_cols"][:, bass.ds(s_ * ST * (E0 + 1), ST * (E0 + 1))], sg_in[p])
                                load(edge_r[0:1, p, 0:ST + 1], d["dst_cols"][P - 1:P, bass.ds(s_ * ST, ST + 1)], sg_in[p])
                                load(edge_r[0:1, p, ST + 1:], d["dst_cols"][0:1, bass.ds(s_ * ST + 1, ST)], sg_in[p])
                            if k == 3 and (more or p == 0):
                                eng.wait_ge(scored, after(s_ * PIECE))
                                load_es(s_ + 1, 1 - p)
                        if more:
                            load_idx(0, i + 1, p)
                load_es(0, 0)
                with eng.Fori(0, IT - 1) as i:
                    layer0(i, True)
                layer0(IT - 1, False)
                eng.wait_ge(node[0, 1]["yout"], PAIRS)
                load(rows(U), by_tile(d["x"]), x_loaded)

                for l in (1, 2):
                    store(l, A)
                    if l == 2:
                        eng.wait_ge(node[2, 0]["hT"], PAIRS)
                        load(C[:, 0:NT + TB], d["weight_cols"], wt_in)
                    with eng.Fori(0, IT) as i:
                        for p in range(2):
                            load_idx(l, i, p)

                load(b_table[N:N + P, :], ident[:, :], u_stored)
                for done, tiles in zip((HALF, PAIRS), HALVES):
                    eng.wait_ge(node[3, 0]["qs"], done)
                    load(by_tile(h_table)[:, tiles, :], rows(A)[:, tiles, :], h_stored)
                    load(by_tile(b_table[0:N, :])[:, tiles, :], rows(C)[:, tiles, :], u_stored)
                for p in range(2):
                    load_idx(3, 0, p)
                if BOTH:
                    for k in range(2):
                        load(bwin[W:W + E3, k, 0, :], W1cT[:, :], w1c_in)
                eng.wait_ge(u_stored, 16 * OTHERS[3])

                def layer3(i, more):
                    for c in range(BODY):
                        n = i * BODY + c
                        load_ea("ea32_rows", pre, hT[W:W + E3] if BOTH else eaT[:, :, :], i, c)
                        regs = window_bases(eng, n, G)
                        for w in range(NW):
                            load(bwin[0:W, c % 2, w, :], b_table[bass.ds(regs[w], W), :], bw_in[c % 2])
                        if more and c % PIECE == PIECE - 1:
                            load_idx(3, i + 1, c // PIECE)
                with eng.Fori(0, IT - 1) as i:
                    layer3(i, True)
                layer3(IT - 1, False)
                eng.wait_ge(node[3, 1]["st"], 1)
                for to, n in ((g3, "L3_gnn_gamma"), (be3, "L3_gnn_beta")):
                    load(to, d[n].partition_broadcast(P), g3_in)


            by_mode(eng, run)
            for k, tiles in enumerate(HALVES):
                eng.wait_ge(y_done, k + 1)
                eng.dma_start(by_tile(out)[:, tiles, :], rows(R)[:, tiles, :]).then_inc(stored, 16)
            eng.wait_ge(stored, 32)

        @block.scalar
        def _(eng):
            a = nc.scalar
            for x in (ohT_sb, ex_ready, sT_sb, relu):
                eng.sem_inc(x, BODY)

            def root(k, to, of):
                eng.wait_ge(var_ready, k + 1)
                a.activation(to, of, ACT.Sqrt).then_inc(sd_ready, 1)

            def run(G, W):
                stats = stat[0:NPT, 2, :], stat[0:NPT, 1, :]

                def evacuate(sem_ready, sem_done, to, k):
                    def one(n, s_, more):
                        when(sem_ready, n + 1, eng, "act")
                        a.copy(to[:, s_, :], bank[4 * s_ + k][:, 0:2 * NPT]).then_inc(sem_done, 1)
                    node_steps(eng, one)

                def squares(norm, h):
                    for half, tiles in enumerate(HALVES):
                        eng.wait_ge(centered, 2 * norm + half + 1)
                        a.activation(rows(C)[:, tiles, :], rows(h)[:, tiles, :], ACT.Square).then_inc(squared, 1)

                squares(0, A)
                root(0, *stats)
                evacuate(node[0, 0]["T"], node[0, 0]["hT"], st4, 0)

                K = W * windows(W)[2]

                def transposed(n, c):
                    when(ohT_ps, after(n + 1), eng, "act")
                    when(expanded, after(n - 1), eng, "act")
                    a.copy(sT[0:K, c % 2, :], bank[c % 2][0:K, :]).then_inc(ohT_sb, 1)

                def score(i, c):
                    b = c % PIECE
                    when(multiplied, after(i * BODY + c + 1), eng, "act")
                    for j in range(TB):
                        last = a.activation(prod[:, j, :], prod[:, j, :], ACT.Copy, accum_out=alpha[:, b * TB + j:b * TB + j + 1])
                    last.then_inc(scored, 1)

                def softmax(i, q):
                    p = q % 2
                    when(sxa, 4 * (2 * i + q) + 4, eng, "act")
                    a.activation(fac[:, :], bank[3][:, 256:257], ACT.Exp)
                    a.activation(ex[:, p, :], bank[3][:, P:P + ST], ACT.Exp).then_inc(ex_ready, 1)

                def layer0(i, q, x, y):
                    if x:
                        for k in range(PIECE):
                            n = i * BODY + q * PIECE + k + 1
                            if not (isinstance(n, int) and n == NB):
                                transposed(n, q * PIECE + k + 1)
                            score(i, q * PIECE + k)
                        softmax(i, q)
                transposed(0, 0)
                supersteps(eng, layer0)
                root(1, tmp_bc[:, :], mean_bc[:, :])
                for l in range(1, LAYERS):
                    squares(l, U if l == 3 else A)
                    root(l + 1, *stats)
                evacuate(node[3, 0]["T"], node[3, 0]["hT"], st4, 0)

                def transposed3(n, c):
                    when(sT_ps, after(n + 1), eng, "act")
                    when(pre, after(n - 1), eng, "act")
                    a.copy(hT[0:W, c % 2, :], bank[c % 2][0:W, :]).then_inc(sT_sb, 1)

                def layer3(i, c, x, y):
                    if x:
                        n = i * BODY + c
                        if not (isinstance(n, int) and n + 1 == NB):
                            transposed3(n + 1, c + 1)
                        when(summed, after(n + 1), eng, "act")
                        rows_ = ring[:, c % BODY].rearrange("p j f -> p (j f)")
                        a.activation(rows_, rows_, ACT.Relu).then_inc(relu, 1)
                transposed3(0, 0)
                steps(eng, layer3)
                evacuate(node[3, 1]["q"], node[3, 1]["qs"], st2, 0)
                squares(4, A)
                root(5, *stats)

            by_mode(eng, run)

        @block.tensor
        def _(eng):
            def mul(to, l_, r_, start=True, stop=True):
                return nc.tensor.matmul(to, l_, r_, start=start, stop=stop)

            def flip(to, of, n):
                return nc.tensor.transpose(to, of, ident[0:n, 0:n])

            for x in mm + [ohT_ps, expanded, sT_ps, pre]:
                eng.sem_inc(x, BODY)
            eng.wait_ge(loaded, 16 * LOADS)
            eng.wait_ge(consts, 4)
            for k, n in enumerate(("q", "v", "skip", "w2")):
                flip(bank[0][:, k * P:(k + 1) * P], raw[n], P)
            flip(bank[1][:, 0:P], raw["wu"], P)
            for k in range(2):
                flip(bank[1][:, (k + 1) * P:(k + 2) * P], raw_w1[:, k * P:(k + 1) * P], P)
            flip(bank[2][0:EP, 0:P], bv_we[:, :, :].rearrange("p a e -> p (a e)"), P)
            flip(bank[2][0:E3, P:2 * P], raw_w1[:, 2 * P:2 * P + E3], P).then_inc(wT_ps, 1)
            eng.wait_ge(bases_done, 1)
            def run(G, W):
                NW, BOTH = TB // G, W + E3 <= 64
                S = matrices(S_, W)
                OH2 = matrices(S2_[:, :].bitcast(bf16), W)
                bwin = S2_[:, 0:2 * NW * F].rearrange("p (k w f) -> p k w f", k=2, f=F)
                for k in range(NW):
                    mul(bank[4 + k][:, 0:NB], ones[0:1, :], base_f[0:1, k * NB * G:(k + 1) * NB * G:G]).then_inc(base_ps, 1)
                eng.wait_ge(wT_sb, 1)

                def prep(l):
                    m = node[l, 0]

                    def transposes(n, s_):
                        when(m["st"], n + 1, eng, "pe")
                        for k in range(2):
                            last = flip(bank[4 * s_][:, k * NPT:(k + 1) * NPT], st1[0:NPT, s_, k * F:(k + 1) * F], NPT)
                        last.then_inc(m["T"], 1)

                    def one(n, s_, more):
                        bk = bank[4 * s_:4 * s_ + 4]
                        if l in (0, 3):
                            when(m["hT"], n + 1, eng, "pe")
                        if l == 3:
                            for k in range(2):
                                last = mul(bk[1][0:NPT, k * 2 * F:(k + 1) * 2 * F], st4[:, s_, k * NPT:(k + 1) * NPT], W1abT[:, :])
                            last.then_inc(m["q"], 1)
                        if l == 0:
                            mul(bk[1][:, 0:2 * NPT], WqT[:, :], st4[:, s_, :]).then_inc(m["q"], 1)
                            when(m["qs"], n + 1, eng, "pe")
                            for k in range(2):
                                last = mul(bk[3][0:NPT, k * UC:(k + 1) * UC], st2[:, s_, k * NPT:(k + 1) * NPT], WKb[:, :])
                            last.then_inc(m["y"], 1)
                            for k in range(2):
                                to = bk[2][0:NPT, k * F:(k + 1) * F]
                                mul(to, st4[:, s_, k * NPT:(k + 1) * NPT], WskT[:, :], stop=False)
                                last = mul(to, ones[0:1, 0:NPT], bskip[:, :], start=False)
                            last.then_inc(m["skip"], 1)
                        if more:
                            transposes(n + 1, 1 - s_)
                    transposes(0, 0)
                    node_steps(eng, one)

                prep(0)
                eng.wait_ge(prepared, 1)

                OH, win, STACK = windows(W)
                U_LOADS = NW * STACK

                def transpose(n, c):
                    when(oh, after(n + 1), eng, "pe")
                    when(ohT_sb, after(n - 1), eng, "pe")
                    for j in range(TB):
                        last = mul(bank[c % 2][0:STACK * W, j * P:(j + 1) * P], OH[:, c % 2, j, :], ident_b[:, :])
                    last.then_inc(ohT_ps, 1)

                def expand(i, c):
                    n = i * BODY + c
                    when(ohT_sb, after(n + 1), eng, "pe")
                    when(uw_in[c % 2], 16 * U_LOADS * (PIECE * i + c // 2 + 1), eng, "pe")
                    when(multiplied, after(n), eng, "pe")
                    for j in range(TB):
                        to = bank[2 + j // 2][:, (j % 2) * UC:(j % 2 + 1) * UC]
                        products = 3 // STACK
                        for a in range(products):
                            last = mul(to, sT[0:STACK * W, c % 2, j * P:(j + 1) * P], win[0:STACK * W, c % 2, j // G, a * UC:(a + 1) * UC],
                                       start=a == 0, stop=a == products - 1)
                    last.then_inc(expanded, 1)

                def sums(l, i, c, ready, of, mat, second):
                    n = i * BODY + c
                    when(ready, after(n + 1), eng, "pe")
                    when(added[l], after(NW * (n - 1)), eng, "pe")
                    for j in range(TB):
                        to = slice((j // G) * W, (j // G + 1) * W)
                        first, end = j % G == 0, j % G == G - 1
                        if second is not None:
                            x, mat2 = second(j)
                            mul(bank[6 + c % 2][0:x.shape[1], to], x, mat2[:, c % 2, j, :], start=first, stop=end)
                        last = mul(bank[4 + c % 2][:, to], of[:, c % BODY, j, :], mat[:, c % 2, j, :], start=first, stop=end)
                    last.then_inc(mm[l], 1)

                def softmax(i, q):
                    s_ = 2 * i + q
                    when(scored, after(s_ * PIECE + PIECE), eng, "pe")
                    flip(bank[2][0:ST, 0:P], alpha[:, :], P).then_inc(sxa, 1)
                    when(sxb, 3 * s_ + 1, eng, "pe")
                    mul(bank[2][0:1, 128:128 + ST], run_f[:, P - 1:P], ident[0:ST, 0:ST])
                    mul(bank[2][0:1, 192:192 + ST], run_b[:, 0:1], ident[0:ST, 0:ST]).then_inc(sxa, 1)
                    when(sxb, 3 * s_ + 2, eng, "pe")
                    for k in range(2):
                        last = mul(bank[3][0:ST, k:k + 1], row[0:1, 6 + k, 0:ST], ones[0:1, 0:1])
                    last.then_inc(sxa, 1)
                    when(sxb, 3 * s_ + 3, eng, "pe")
                    mul(bank[3][:, 256:257], ones[0:1, :], facr[:, :])
                    flip(bank[3][:, P:P + ST], al_t[:, :], ST).then_inc(sxa, 1)

                def layer0(i, q, a, b):
                    for k in range(PIECE):
                        if a:
                            if k == 0:
                                when(ex_ready, after(2 * i + q), eng, "pe")
                            expand(i, q * PIECE + k)
                            n = i * BODY + q * PIECE + k + 1
                            if not (isinstance(n, int) and n == NB):
                                transpose(n, q * PIECE + k + 1)
                        if b:
                            sums(0, i, (q - 1) * PIECE + k, onehot2, ring, S,
                                 lambda j: (dp[:, k * TB + j].rearrange("p a e -> p (a e)"), OH2))
                    if a:
                        softmax(i, q)
                transpose(0, 0)
                supersteps(eng, layer0)

                m = node[0, 1]

                def finish0(n, s_, more):
                    when(m["st"], n + 1, eng, "pe")
                    for k in range(2):
                        at, to = slice(k * NPT, (k + 1) * NPT), bank[4 * s_][0:NPT, k * (F + 1):(k + 1) * (F + 1)]
                        mul(to, st4[:, s_, at], WvT[:, :], stop=False)
                        last = mul(to, st3[:, s_, at], bv_weT[:, :], start=False)
                    last.then_inc(m["y"], 1)
                node_steps(eng, finish0)
                for k, buf in enumerate((R, C)):
                    eng.wait_ge(bn_x, k + 1)
                    for o in range(0, NCOL, 512):
                        wd = min(512, NCOL - o)
                        last = nc.tensor.matmul(bank[2][:, 0:wd], ones[0:NPT, :], buf[0:NPT, o:o + wd], start=o == 0,
                                                stop=o + 512 >= NCOL, skip_group_check=True)
                    last.then_inc(bn_sum, 1)

                def messages(l):
                    def one(i, c):
                        when(gathered[c], 16 * TB * (l * IT + i + 1), eng, "pe")
                        sums(l, i, c, onehot[l], ring, S, (lambda j: (ones[:, 0:1], S)) if l == 1 else None)
                    with eng.Fori(0, IT) as i:
                        for c in range(BODY):
                            one(i, c)

                prep(1)
                eng.wait_ge(prepared, 2)
                messages(1)
                m = node[1, 1]

                def finish1(n, s_, more):
                    bk = bank[4 * s_:4 * s_ + 3]
                    when(m["st"], n + 1, eng, "pe")
                    for k in range(2):
                        at = slice(k * NPT, (k + 1) * NPT)
                        mul(bk[0][0:NPT, k * F:(k + 1) * F], st4[:, s_, at], WN[:, :])
                        mul(bk[1][0:NPT, k * F:(k + 1) * F], st2[:, s_, at], WS[:, :])
                        last = mul(bk[2][0:NPT, k:k + 1], st3[0:1, s_, at], ones[0:1, 0:1])
                    last.then_inc(m["y"], 1)
                node_steps(eng, finish1)
                prep(2)
                eng.wait_ge(prepared, 3)
                messages(2)
                m = node[2, 1]

                def finish2(n, s_, more):
                    when(m["st"], n + 1, eng, "pe")
                    for k in range(2):
                        to = bank[4 * s_][0:NPT, k * F:(k + 1) * F]
                        mul(to, st4[:, s_, k * NPT:(k + 1) * NPT], W2L[:, :], stop=False)
                        last = mul(to, ones[0:1, 0:NPT], btwo[:, :], start=False)
                    last.then_inc(m["y"], 1)
                node_steps(eng, finish2)
                prep(3)
                eng.wait_ge(prepared, 4)
                if BOTH:
                    eng.wait_ge(w1c_in, 32)

                OH3 = matrices(oh3_, W)

                def transpose3(n, c):
                    when(oh3, after(n + 1), eng, "pe")
                    when(sT_sb, after(n - 1), eng, "pe")
                    for j in range(TB):
                        last = mul(bank[c % 2][0:W, j * P:(j + 1) * P], OH3[:, c % 2, j, :], ident_b[:, :])
                    last.then_inc(sT_ps, 1)

                def layer3(i, c, a, b):
                    n = i * BODY + c
                    if a:
                        when(sT_sb, after(n + 1), eng, "pe")
                        when(bw_in[c % 2], 16 * NW * (PIECE * i + c // 2 + 1), eng, "pe")
                        when(ea_in[c % 2], 16 * (PIECE * i + c // 2 + 1), eng, "pe")
                        when(summed, after(n - 1), eng, "pe")
                        for j in range(TB):
                            to, e = bank[2 + c % 2][:, j * P:(j + 1) * P], slice(j * P, (j + 1) * P)
                            if BOTH:
                                last = mul(to, hT[0:W + E3, c % 2, e], bwin[0:W + E3, c % 2, 0, :])
                            else:
                                mul(to, hT[:, c % 2, e], bwin[:, c % 2, j // G, :], stop=False)
                                last = mul(to, eaT[:, c % 2, e], W1cT[:, :], start=False)
                        last.then_inc(pre, 1)
                        if not (isinstance(n, int) and n + 1 == NB):
                            transpose3(n + 1, c + 1)
                    if b:
                        sums(3, i, c - 1, relu, ring, S, None)
                transpose3(0, 0)
                steps(eng, layer3)
                m = node[3, 1]

                def sums_times_w2(n, s_):
                    when(m["st"], n + 1, eng, "pe")
                    mul(bank[4 * s_][:, 0:2 * NPT], W2T[:, :], st4[:, s_, :], stop=False)
                    mul(bank[4 * s_][:, 0:2 * NPT], b2[:, :], st3[0:1, s_, :], start=False).then_inc(m["q"], 1)

                def finish3(n, s_, more):
                    if more:
                        sums_times_w2(n + 1, 1 - s_)
                    when(m["qs"], n + 1, eng, "pe")
                    for k in range(2):
                        last = mul(bank[4 * s_ + 2][0:NPT, k * F:(k + 1) * F], st2[:, s_, k * NPT:(k + 1) * NPT], WuT[:, :])
                    last.then_inc(m["y"], 1)
                sums_times_w2(0, 0)
                node_steps(eng, finish3)

            by_mode(eng, run)


def kernel(**inputs):
    import numpy as _np
    import concourse.bacc as _bacc
    from concourse import mybir as _mybir
    from concourse.bass_utils import run_bass_kernel_spmd as _run

    nc = _bacc.Bacc("TRN2", target_bir_lowering=False, num_devices=1)
    pad = NT * P - E
    a = {k: _np.asarray(v) for k, v in inputs.items()}
    src, dst, weight = a.pop("src"), a.pop("dst"), a.pop("edge_weight")
    ea10, ea32 = a.pop("edge_attr_10"), a.pop("edge_attr_32")
    dst = _np.pad(dst, (0, pad), constant_values=PAD_DST)
    ea10 = _np.pad(_np.pad(ea10, ((0, pad), (0, 0))), ((0, 0), (1, 0)), constant_values=1)
    a["src_cols"] = _np.pad(src, (0, pad)).reshape(NT, P).T
    a["dst_cols"] = _np.pad(dst.reshape(NT, P).T, ((0, 0), (1, 0)), constant_values=-1)
    a["dst_rows"] = dst.reshape(NT, P)
    a["weight_cols"] = _np.pad(_np.pad(weight, (0, pad)).reshape(NT, P).T, ((0, 0), (0, TB)))
    a["ea10_cols"] = ea10.reshape(NT, P, E0 + 1).transpose(1, 0, 2).reshape(P, NT * (E0 + 1))
    a["ea32_rows"] = _np.pad(ea32, ((0, pad), (0, 0))).T
    arrays, d = {}, {}
    for name, v in a.items():
        v = _np.ascontiguousarray(v)
        arrays["in_" + name] = v
        d[name] = nc.dram_tensor("in_" + name, v.shape, _mybir.dt.from_np(v.dtype), kind="ExternalInput").ap()
    out = nc.dram_tensor("x_out", (N, F), fp32, kind="ExternalOutput").ap()
    program(nc, d, out)
    r = _run(nc, [arrays], core_ids=[0])
    return r.results[0]["x_out"]
```
